# Optimizing a Trainium2 kernel written in Bass

```python
import numpy as np
import jax
import jax.numpy as jnp

def _softmax(x, axis=-1):
    return jax.nn.softmax(x, axis=axis)

def _gelu(x):
    return jax.nn.gelu(x, approximate=True)

def _silu(x):
    return jax.nn.silu(x)

def _sigmoid(x):
    return jax.nn.sigmoid(x)

def _layernorm(x, axis=-1, eps=1e-05):
    m = jnp.mean(x, axis=axis, keepdims=True)
    v = jnp.var(x, axis=axis, keepdims=True)
    return (x - m) / jnp.sqrt(v + eps)

def _scatter_add(tgt, idx, src, axis=0):
    return tgt.at[idx].add(src)

def _segment_sum(src, seg, n):
    return jax.ops.segment_sum(src, seg, n)
kernel_name = 'mk_flamingo_gated_d1_seqx_r4_2a2c68'

def setup_inputs(seed: int=0):
    np.random.seed(seed)
    _w = jnp.asarray

    def _rec_inputs():
        import jax
        import jax.numpy as jnp
        _rk = jax.random.key(seed)
        x = -0.0002928 + 1 * jax.random.normal(jax.random.fold_in(_rk, 1), (4, 1024, 256), jnp.float32)
        _lenS = 1024 - jax.random.randint(jax.random.fold_in(_rk, 7), (4,), 0, max(1, 1024 // 4) + 1, jnp.int32)
        _lenS2 = 77 - jax.random.randint(jax.random.fold_in(_rk, 8), (4,), 0, max(1, 77 // 4) + 1, jnp.int32)
        _ctx_1024P = jax.random.normal(jax.random.fold_in(_rk, 11), (4, 16, 256), jnp.float32)
        _ctx_1024c = jax.random.dirichlet(jax.random.fold_in(_rk, 511), 0.3 * jnp.ones((16,), jnp.float32), (4, 77))
        _ctx_1024t = jnp.einsum('bsk,bkd->bsd', _ctx_1024c, _ctx_1024P)
        _ctx_1024t = _ctx_1024t * jax.lax.rsqrt(jnp.mean(jnp.square(_ctx_1024t)) + 1e-12) * 0.953939
        ctx_1024 = -1.39393e-06 + 0.999914 * (_ctx_1024t + 0.3 * jax.random.normal(jax.random.fold_in(_rk, 611), (4, 77, 256), jnp.float32))
        _g = jax.random.normal(jax.random.fold_in(_rk, 9001), (2, 1), jnp.float32)
        _g = jnp.sign(_g) * jnp.maximum(jnp.abs(_g), 1.0) + (_g == 0) * 1.0
        g_xattn = _g[0]
        g_ffn = _g[1]
        return (x, ctx_1024, g_xattn, g_ffn)
    x, ctx_1024, g_xattn, g_ffn = _rec_inputs()

    def _L0_xattn_setup():
        import jax, jax.numpy as jnp
        import numpy as np
        D_MODEL = 256
        NUM_HEADS = 16
        D_K = D_MODEL // NUM_HEADS

        def _split_heads(x):
            B, S, _ = x.shape
            return x.reshape(B, S, NUM_HEADS, D_K).transpose(0, 2, 1, 3)
        key = jax.random.key(seed)
        ks = jax.random.split(key, 11)
        B, S = (2, 512)
        scale = 1.0 / np.sqrt(D_MODEL)
        inp = {'q': jax.random.normal(ks[0], (B, S, D_MODEL), dtype=jnp.float32), 'k': jax.random.normal(ks[1], (B, S, D_MODEL), dtype=jnp.float32), 'v': jax.random.normal(ks[2], (B, S, D_MODEL), dtype=jnp.float32), 'W_q': jax.random.normal(ks[3], (D_MODEL, D_MODEL), dtype=jnp.float32) * scale, 'b_q': jnp.zeros((D_MODEL,), dtype=jnp.float32), 'W_k': jax.random.normal(ks[4], (D_MODEL, D_MODEL), dtype=jnp.float32) * scale, 'b_k': jnp.zeros((D_MODEL,), dtype=jnp.float32), 'W_v': jax.random.normal(ks[5], (D_MODEL, D_MODEL), dtype=jnp.float32) * scale, 'b_v': jnp.zeros((D_MODEL,), dtype=jnp.float32), 'W_o': jax.random.normal(ks[6], (D_MODEL, D_MODEL), dtype=jnp.float32) * scale, 'b_o': jnp.zeros((D_MODEL,), dtype=jnp.float32)}
        return inp
    _L0_xattn_all = _L0_xattn_setup()
    _L0_xattn_in = {k: v for k, v in _L0_xattn_all.items() if k in ('W_q', 'b_q', 'W_k', 'b_k', 'W_v', 'b_v', 'W_o', 'b_o')}
    del _L0_xattn_all

    def _L0_ffn_setup():
        import jax, jax.numpy as jnp
        import numpy as np
        import math
        D_MODEL = 256
        D_FF = 1024
        NUM_EXPERTS = 8
        NUM_SHARED = 1
        E_ROUTED = NUM_EXPERTS - NUM_SHARED
        TOP_K = 2
        CAP_FACTOR = 1.25
        B, S = (4, 512)
        T = B * S
        CAPACITY = math.ceil(CAP_FACTOR * T * TOP_K / E_ROUTED)
        SHARED_SCALE = 1.0

        def _layernorm(x, g, b, eps=1e-05):
            mu = jnp.mean(x, axis=-1, keepdims=True)
            var = jnp.mean((x - mu) ** 2, axis=-1, keepdims=True)
            return (x - mu) * jax.lax.rsqrt(var + eps) * g + b
        key = jax.random.key(seed)
        ks = jax.random.split(key, 10)
        s = 0.02
        return {'x': jax.random.normal(ks[0], (B, S, D_MODEL), dtype=jnp.float32), 'ln_g': jnp.ones((D_MODEL,), jnp.float32), 'ln_b': jnp.zeros((D_MODEL,), jnp.float32), 'Wr': jax.random.normal(ks[1], (D_MODEL, E_ROUTED), jnp.float32) * s, 'W1': jax.random.normal(ks[2], (E_ROUTED, D_MODEL, D_FF), jnp.float32) * s, 'W3': jax.random.normal(ks[3], (E_ROUTED, D_MODEL, D_FF), jnp.float32) * s, 'W2': jax.random.normal(ks[4], (E_ROUTED, D_FF, D_MODEL), jnp.float32) * s, 'W1s': jax.random.normal(ks[5], (D_MODEL, D_FF), jnp.float32) * s, 'W3s': jax.random.normal(ks[6], (D_MODEL, D_FF), jnp.float32) * s, 'W2s': jax.random.normal(ks[7], (D_FF, D_MODEL), jnp.float32) * s}
    _L0_ffn_all = _L0_ffn_setup()
    _L0_ffn_in = {k: v for k, v in _L0_ffn_all.items() if k in ('ln_g', 'ln_b', 'Wr', 'W1', 'W3', 'W2', 'W1s', 'W3s', 'W2s')}
    del _L0_ffn_all
    return {'x': x, 'ctx_1024': ctx_1024, 'g_xattn': g_xattn, 'g_ffn': g_ffn, 'L0_xattn_W_q': _L0_xattn_in['W_q'], 'L0_xattn_b_q': _L0_xattn_in['b_q'], 'L0_xattn_W_k': _L0_xattn_in['W_k'], 'L0_xattn_b_k': _L0_xattn_in['b_k'], 'L0_xattn_W_v': _L0_xattn_in['W_v'], 'L0_xattn_b_v': _L0_xattn_in['b_v'], 'L0_xattn_W_o': _L0_xattn_in['W_o'], 'L0_xattn_b_o': _L0_xattn_in['b_o'], 'L0_ffn_ln_g': _L0_ffn_in['ln_g'], 'L0_ffn_ln_b': _L0_ffn_in['ln_b'], 'L0_ffn_Wr': _L0_ffn_in['Wr'], 'L0_ffn_W1': _L0_ffn_in['W1'], 'L0_ffn_W3': _L0_ffn_in['W3'], 'L0_ffn_W2': _L0_ffn_in['W2'], 'L0_ffn_W1s': _L0_ffn_in['W1s'], 'L0_ffn_W3s': _L0_ffn_in['W3s'], 'L0_ffn_W2s': _L0_ffn_in['W2s']}

def reference(x, ctx_1024, g_xattn, g_ffn, L0_xattn_W_q, L0_xattn_b_q, L0_xattn_W_k, L0_xattn_b_k, L0_xattn_W_v, L0_xattn_b_v, L0_xattn_W_o, L0_xattn_b_o, L0_ffn_ln_g, L0_ffn_ln_b, L0_ffn_Wr, L0_ffn_W1, L0_ffn_W3, L0_ffn_W2, L0_ffn_W1s, L0_ffn_W3s, L0_ffn_W2s):
    import jax
    import jax.numpy as jnp

    def _L0_xattn_ref(q, k, v, W_q, b_q, W_k, b_k, W_v, b_v, W_o, b_o):
        import jax, jax.numpy as jnp
        import numpy as np
        D_MODEL = 256
        NUM_HEADS = 16
        D_K = D_MODEL // NUM_HEADS

        def _split_heads(x):
            B, S, _ = x.shape
            return x.reshape(B, S, NUM_HEADS, D_K).transpose(0, 2, 1, 3)
        qh = _split_heads(q @ W_q.T + b_q)
        kh = _split_heads(k @ W_k.T + b_k)
        vh = _split_heads(v @ W_v.T + b_v)
        scores = jnp.einsum('bhsd,bhtd->bhst', qh, kh) / jnp.sqrt(jnp.asarray(D_K, dtype=qh.dtype))
        probs = jax.nn.softmax(scores, axis=-1)
        attn = jnp.einsum('bhst,bhtd->bhsd', probs, vh)
        B, H, S, dk = attn.shape
        combined = attn.transpose(0, 2, 1, 3).reshape(B, S, H * dk)
        return combined @ W_o.T + b_o

    def _L0_ffn_ref(x, ln_g, ln_b, Wr, W1, W3, W2, W1s, W3s, W2s):
        import jax, jax.numpy as jnp
        import numpy as np
        import math
        D_MODEL = 256
        D_FF = 1024
        NUM_EXPERTS = 8
        NUM_SHARED = 1
        E_ROUTED = NUM_EXPERTS - NUM_SHARED
        TOP_K = 2
        CAP_FACTOR = 1.25
        B, S = (4, 512)
        T = B * S
        CAPACITY = math.ceil(CAP_FACTOR * T * TOP_K / E_ROUTED)
        SHARED_SCALE = 1.0

        def _layernorm(x, g, b, eps=1e-05):
            mu = jnp.mean(x, axis=-1, keepdims=True)
            var = jnp.mean((x - mu) ** 2, axis=-1, keepdims=True)
            return (x - mu) * jax.lax.rsqrt(var + eps) * g + b
        Bx, Sx, D = x.shape
        Tn = Bx * Sx
        h = _layernorm(x, ln_g, ln_b).reshape(Tn, D)
        logits = h @ Wr
        top_vals, top_idx = jax.lax.top_k(logits, TOP_K)
        gates = jax.nn.softmax(top_vals, axis=-1)
        idx = top_idx.T.reshape(-1)
        gat = gates.T.reshape(-1)
        tok = jnp.tile(jnp.arange(Tn), TOP_K)
        onehot = jax.nn.one_hot(idx, E_ROUTED, dtype=jnp.int32)
        pos = jnp.sum(jnp.cumsum(onehot, axis=0) * onehot, axis=-1) - 1
        keep = pos < CAPACITY
        pos_c = jnp.where(keep, pos, CAPACITY)
        xe = jnp.zeros((E_ROUTED, CAPACITY, D), h.dtype).at[idx, pos_c].set(h[tok], mode='drop')
        a = jnp.einsum('ecd,edf->ecf', xe, W1)
        b = jnp.einsum('ecd,edf->ecf', xe, W3)
        ye = jnp.einsum('ecf,efd->ecd', jax.nn.silu(a) * b, W2)
        out_slots = ye[jnp.clip(idx, 0, E_ROUTED - 1), jnp.clip(pos_c, 0, CAPACITY - 1)]
        out_slots = out_slots * (gat * keep.astype(gat.dtype))[:, None]
        routed = jnp.zeros((Tn, D), h.dtype).at[tok].add(out_slots)
        shared = jax.nn.silu(h @ W1s) * (h @ W3s) @ W2s
        out = routed + SHARED_SCALE * shared
        return out.reshape(Bx, Sx, D)
    x = x + jnp.tanh(g_xattn[0]) * _L0_xattn_ref(_layernorm(x, axis=-1), ctx_1024, ctx_1024, L0_xattn_W_q, L0_xattn_b_q, L0_xattn_W_k, L0_xattn_b_k, L0_xattn_W_v, L0_xattn_b_v, L0_xattn_W_o, L0_xattn_b_o)
    x = x + jnp.tanh(g_ffn[0]) * _L0_ffn_ref(_layernorm(x, axis=-1), L0_ffn_ln_g, L0_ffn_ln_b, L0_ffn_Wr, L0_ffn_W1, L0_ffn_W3, L0_ffn_W2, L0_ffn_W1s, L0_ffn_W3s, L0_ffn_W2s)
    return x

_drawn_inputs = setup_inputs


def setup_inputs(seed=0):
    import zlib

    import numpy as np

    out = dict(_drawn_inputs(seed))
    spreads = {'L0_xattn_b_q': (0.0, 0.479),
     'L0_xattn_b_k': (0.0, 0.8),
     'L0_xattn_b_v': (0.0, 0.1),
     'L0_xattn_b_o': (0.0, 0.1),
     'L0_ffn_ln_g': (1.0, 0.6),
     'L0_ffn_ln_b': (0.0, 0.8)}
    factors = {'L0_ffn_Wr': 3.212, 'L0_ffn_W1': 2.974, 'L0_ffn_W3': 2.941, 'L0_ffn_W2': 2.946}
    for name, (base, spread) in spreads.items():
        noise = np.random.default_rng([zlib.crc32(name.encode()), seed]).standard_normal(out[name].shape)
        drawn = base * np.exp(spread * noise) if base else spread * noise
        out[name] = jnp.asarray(drawn.astype(out[name].dtype))
    for name, factor in factors.items():
        out[name] = (out[name] * factor).astype(out[name].dtype)
    return out
```

```python
from contextlib import ExitStack

import concourse.bass as bass
import concourse.mybir as mybir

F32 = mybir.dt.float32
F32R = mybir.dt.float32r
I32 = mybir.dt.int32
U32 = mybir.dt.uint32
ALU = mybir.AluOpType
ACT = mybir.ActivationFunctionType
AX = mybir.AxisListType

P = 128
B, S, D = 4, 1024, 256
SK = 77
H, DH = 16, 16
FF = 1024
E = 7
CAP = 732
EPS = 1e-5
T = B * S
N = 512
TT = N // P
NB = T // N
KD = D // P
NF = FF // P
NPAIR = H // 2
NG = H // 4
RT = 122
NR = CAP // RT
HALF = CAP // 2
NTT = T // P
NSL = E * NR
WCOLS = KD * FF
PIECE = 512
NPIECE = 3 * WCOLS // PIECE
RING = 4


NCONST = 11
NQST = 20
XT_AT = (6, 8, 10, 12)
OHB = 4
NSTEP0 = WCOLS // PIECE


class Turn:

    def __init__(self, i, c):
        self.i, self.c = i, c
        self.n = i * 2 + c

    def at(self, n):
        return isinstance(self.n, int) and self.n == n

    def next(self):
        return Turn(self.i, 1) if self.c == 0 else Turn(self.i + 1, 0)


def schedule(eng, s1, s2, ffn, routing):
    s1(Turn(0, 0))
    s2(Turn(0, 0))
    s1(Turn(0, 1))
    ffn(Turn(0, 0))
    with eng.Fori(0, NB // 2 - 1) as i:
        s2(Turn(i, 1))
        s1(Turn(i + 1, 0))
        ffn(Turn(i, 1))
        s2(Turn(i + 1, 0))
        s1(Turn(i + 1, 1))
        ffn(Turn(i + 1, 0))
    s2(Turn(NB // 2 - 1, 1))
    routing()
    ffn(Turn(NB // 2 - 1, 1))


def with_experts(eng, expert):
    with eng.Fori(0, E // 2) as i:
        expert(Turn(i, 0))
        expert(Turn(i, 1))
    expert(Turn(E // 2, 0))


def val_at(par, j):
    return DH * j + 64 * par


def den_at(par, j):
    return DH * j + 64 * (1 - par)


class Steps:

    def __init__(self, eng, sem, base):
        self.eng, self.sem, self.base, self.k = eng, sem, base, 0

    def did(self, ins):
        self.k += 1
        ins.then_inc(self.sem, 1)

    def wait(self):
        self.eng.wait_ge(self.sem, self.base + self.k)


def build(nc, a, out):
    ctx = ExitStack()

    def sem(name):
        return ctx.enter_context(nc.semaphore(name))

    def sb(name, shape, dt=F32):
        return ctx.enter_context(nc.sbuf_tensor(name, shape, dt))

    KB = 256
    AR = sb("split_operands", [P, 142 * KB], F32R)

    def ar(off_kb, *dims):
        n = 1
        for d in dims:
            n *= d
        v = AR[:, off_kb * KB:off_kb * KB + n]
        names = "abcd"[:len(dims)]
        if len(dims) == 1:
            return v
        return v.rearrange(f"p ({' '.join(names)}) -> p {' '.join(names)}", **dict(zip(names, dims)))

    W0 = ar(0, 2, 3, WCOLS)
    W1_ = ar(48, 2, 3, WCOLS)
    wat = ar(48, 2, 4, KD, D)
    xT = ar(64, 2, KD, N)
    qT = ar(72, 2, KD, N)
    aT = qT
    qst = ar(80, NPAIR, N)
    kst = ar(96, NPAIR, 2, SK)
    kbd = ar(101, KD, 8, SK)
    hT = ar(106, 2, KD, N)
    gT = ar(114, 2, RING, N)
    ctx_s = ar(114, 2, KD, B * SK)
    k_s = ar(119, 2, KD, B * SK)
    xe = [ar(130, 2, KD, CAP), ar(96, 2, KD, CAP)]
    wrs = sb("router_split", [P, KD, 2 * E], F32R)
    mtr = sb("row_max_T", [H, N], F32R)

    AF = sb("float_data", [P, 44 * KB], F32)

    def af(off_kb, *dims):
        n = 1
        for d in dims:
            n *= d
        v = AF[:, off_kb * KB:off_kb * KB + n]
        names = "abcd"[:len(dims)]
        if len(dims) == 1:
            return v
        return v.rearrange(f"p ({' '.join(names)}) -> p {' '.join(names)}", **dict(zip(names, dims)))

    xb = [af(0, TT, D), af(4, TT, D)]
    prob = [af(8, 2, N), af(12, 2, N)]
    vst = af(16, 2, 2, 4, P)
    vall = af(24, B, D)
    x1 = [af(28, TT, D), af(32, TT, D)]
    zb = af(36, TT, D)
    att = zb.rearrange("p a b -> p (a b)").rearrange("p (k n) -> p k n", k=KD)
    sil = [af(40, N), af(42, N)]
    gf = sb("hidden", [P, 2, N])
    stage = [af(0, WCOLS), af(8, WCOLS)]
    xg = af(16, NR, D)
    ye = af(22, NR, D)

    rc = sb("recip_den", [P, N])
    hf = rc
    watt_stage = af(8, 4, 2 * D)
    sh_stage = [af(8, WCOLS), af(28, WCOLS)]
    ctx_f = af(36, KD, B, SK)
    ident = sb("ident", [P, P])
    mones = sb("ones", [P, P])
    lower = sb("earlier_tokens", [P, P])
    lgall = sb("logit_parts", [P, NTT, 2 * E])
    lgs = sb("logits_T", [2 * E, N])
    tbo = sb("gated_bias_o", [P, D])
    bvb = sb("bias_v", [SK, D])
    bq = sb("bias_q", [P, KD])
    bk = sb("bias_k", [P, KD])
    lng = sb("ln_gain", [P, KD])
    lnb = sb("ln_bias", [P, KD])
    wrf = sb("router_raw", [P, KD, E])
    gx = sb("gate_x", [P, 1])
    gy = sb("gate_f", [P, 1])
    tgx = sb("tanh_gate_x", [P, 1])
    tgf = sb("tanh_gate_f", [P, 1])
    passed = sb("all_set", [P, 1])
    nhalf = sb("minus_half", [P, TT])
    stt = sb("bn_parts", [P, TT, 6])
    mv = sb("mean_var", [P, TT, 2])
    vs = sb("var_scaled", [P, TT])
    rstd = sb("rstd", [P, TT])
    mx = sb("row_max", [P, TT, H])
    tabg = sb("gather_table", [P, NSL], I32)
    tabs = sb("scatter_table", [P, NSL], I32)
    tabw = sb("gate_table", [P, NSL])
    gidx = sb("gather_now", [P, NR], I32)
    sidx = [sb("scatter_now0", [P, NR], I32), sb("scatter_now1", [P, NR], I32)]
    gw = [sb("gates_now0", [P, NR]), sb("gates_now1", [P, NR])]

    bank = [ctx.enter_context(nc.psum_tensor(f"bank{j}", [P, 512], F32)) for j in range(8)]

    kscr = nc.dram_tensor("k_scratch", (2, D, B * SK), F32).ap()
    zscr = nc.dram_tensor("z_scratch", (T, D), F32).ap()

    at = {}

    def rt(region_kb, *dims):
        n = 1
        for d in dims:
            n *= d
        off = at.get(region_kb, 0)
        at[region_kb] = off + n
        v = AF[:, region_kb * KB + off:region_kb * KB + off + n]
        names = "abcd"[:len(dims)]
        if len(dims) == 1:
            return v
        return v.rearrange(f"p ({' '.join(names)}) -> p {' '.join(names)}", **dict(zip(names, dims)))

    r_lg, r_tmp, r_em8 = (rt(16, NTT, E) for _ in range(3))
    r_oh = rt(16, 2, NTT, E)
    r_tot, r_inc = (rt(16, 2 * NTT, E) for _ in range(2))
    r_m, r_i, r_g = (rt(24, 2, NTT) for _ in range(3))
    r_d, r_e2, r_tok = (rt(24, NTT) for _ in range(3))
    r_pos, r_hi, r_lo, r_ge, r_ones = (rt(24, 2 * NTT) for _ in range(5))
    r_iota = rt(24, P)
    r_row = rt(36, OHB, RT)
    r_val = rt(36, OHB, 2, NSL)
    assert at[16] <= 8 * KB and at[24] <= 4 * KB and at[36] <= 4 * KB

    names = """passed consts_loaded stage_loaded0 stage_loaded1 x_loaded0 x_loaded1 ident_ready zeros_ready pool_const
    tanh_done wsplit_hi wsplit_lo tbo_ready ctx_hi ctx_lo wr_hi wr_ready kps_ready k_hi k_lo k_stored vps_ready v_ready
    mv_ready rstd_pre rstd_ready xn_ready xb_ready xT_ready xh_ready xl_ready q_ready qh_ready ql_ready
    qst_loaded kst_loaded kbd_loaded vst_ready m_ready m_done mT_ready mtr_ready
    scores_ready exp_done pv_done recip_done attn_done ah_ready al_ready oproj_ready x1_ready mv2_ready rstd2_pre rstd2_ready
    z_ready z_stored zT_ready hh_ready hf_ready hl_ready lg_ready lgs_ready lgT_ready lg_done
    a_ready b_ready sil_done gmul_done gh_ready gl_ready acc_ready acc_done out_stored0 out_stored1
    dve_s1 dve_s2 route_step r_onehots r_counts rexp_done r_const tab_done oh_ready oh_used
    gather_idx gathered scattered ye_free
    xeT_ready xe_hi xe_f xe_lo sidx_ready gw_ready""".split()
    sig = {n: sem(n) for n in names}
    stage_loaded = [sig["stage_loaded0"], sig["stage_loaded1"]]
    x_loaded = [sig["x_loaded0"], sig["x_loaded1"]]
    out_stored = [sig["out_stored0"], sig["out_stored1"]]

    x_rows = a["x"].rearrange("b s d -> (b s) d").rearrange("(n t p) d -> n p t d", t=TT, p=P)
    z_rows = zscr.rearrange("(n t p) d -> n p t d", t=TT, p=P)
    out2 = out.rearrange("b s d -> (b s) d")
    out_rows = out2.rearrange("(n t p) d -> n p t d", t=TT, p=P)
    w1v = a["L0_ffn_W1"].rearrange("e (k p) f -> e p k f", p=P)
    w3v = a["L0_ffn_W3"].rearrange("e (k p) f -> e p k f", p=P)
    w2v = a["L0_ffn_W2"].rearrange("e (k p) d -> e p k d", p=P)
    wv = [w1v, w3v, w2v]
    wsv = [a["L0_ffn_W1s"].rearrange("(k p) f -> p k f", p=P),
           a["L0_ffn_W3s"].rearrange("(k p) f -> p k f", p=P),
           a["L0_ffn_W2s"].rearrange("(k p) d -> p k d", p=P)]

    def matrix(e, m):
        buf = (e.c + m) % 2
        order = [(0, 0), (0, 2), (1, 1)] if buf == 0 else [(0, 1), (1, 0), (1, 2)]
        before = 80 if buf == 0 else 32
        return buf, (e.i * 3 + order.index((e.c, m)) + 1) * 16 + before

    def apart(eng):
        eng.sem_inc(sig["passed"], 1)

    block = ctx.enter_context(nc.Block())

    @block.sync
    def _(sp):
        n_const = 0

        def const(dst, src, small=False):
            nonlocal n_const
            n_const += 1
            sp.dma_start(dst, src, allow_slow_non_contiguous=small).then_inc(sig["consts_loaded"], 16)

        sp.sem_inc(out_stored[1], 16)
        sp.dma_start(xb[0], x_rows[0]).then_inc(x_loaded[0], 16)
        for j, w in enumerate(("WqT", "WkT", "WvT", "WoT")):
            sp.dma_start(watt_stage[:, j], a[w].rearrange("(k p) d -> p k d", p=P)).then_inc(stage_loaded[0], 16)
        for k in range(KD):
            const(ctx_f[:, k], a["ctxT"].rearrange("b (k p) t -> k p b t", p=P)[k])
        const(bq[:, :], a["L0_xattn_b_q"].rearrange("(k p) -> p k", p=P), small=True)
        const(bk[:, :], a["L0_xattn_b_k"].rearrange("(k p) -> p k", p=P), small=True)
        const(lng[:, :], a["L0_ffn_ln_g"].rearrange("(k p) -> p k", p=P), small=True)
        const(lnb[:, :], a["L0_ffn_ln_b"].rearrange("(k p) -> p k", p=P), small=True)
        const(wrf[:, :, :], a["L0_ffn_Wr"].rearrange("(k p) e -> p k e", p=P))
        const(bvb[:, :], a["L0_xattn_b_v"].partition_broadcast(SK))
        const(tbo[:, :], a["L0_xattn_b_o"].partition_broadcast(P))
        const(gx[:, :], a["g_xattn"].partition_broadcast(P))
        const(gy[:, :], a["g_ffn"].partition_broadcast(P))
        assert n_const == NCONST
        for m in range(3):
            if m >= 1:
                sp.wait_ge(sig["wsplit_lo"], NSTEP0 * m)
            sp.dma_start(sh_stage[(m + 1) % 2].rearrange("p (k f) -> p k f", k=wsv[m].shape[1]), wsv[m])\
              .then_inc(stage_loaded[(m + 1) % 2], 16)
        sp.wait_ge(sig["k_lo"], KD)
        for j in range(2):
            sp.dma_start(kscr[j].rearrange("(k p) t -> p k t", p=P), k_s[:, j].bitcast(F32)).then_inc(sig["k_stored"], 16)
        sp.wait_ge(sig["k_stored"], 32)

        def s1(b):
            if b.c == 0:
                bt = b.i
                sp.wait_ge(sig["zeros_ready"], 1)
                sp.wait_ge(sig["m_done"], b.n * TT)
                kd = kscr.rearrange("s (g j d) (b t) -> s j d g b t", g=KD, j=8, b=B)
                for j in range(8):
                    sp.dma_start(kbd[16 * j:16 * j + 16, :, j, :].bitcast(F32), kd[0, j, :, :, bt, :]).then_inc(sig["kbd_loaded"], 16)
                sp.wait_ge(sig["scores_ready"], b.n * NPAIR)
                ks = kscr.rearrange("s (r w d) (b t) -> s w d r b t", w=2, d=DH, b=B)
                for base, part in ((0, 0), (32, 0), (64, 1)):
                    for w in range(2):
                        sp.dma_start(kst[base + 16 * w:base + 16 * w + 16, :, w, :].bitcast(F32), ks[part, w, :, :, bt, :])\
                          .then_inc(sig["kst_loaded"], 16)
            sp.wait_ge(sig["qh_ready"], (b.n + 1) * KD)
            for r in range(4):
                for base in (0, 64):
                    sp.dma_start(qst[base:base + 32, r::4, :].bitcast(F32), qT[32 * r:32 * r + 32, 0].bitcast(F32)).then_inc(sig["qst_loaded"], 16)
            sp.wait_ge(sig["ql_ready"], (b.n + 1) * KD)
            for r in range(4):
                sp.dma_start(qst[32:64, r::4, :].bitcast(F32), qT[32 * r:32 * r + 32, 1].bitcast(F32)).then_inc(sig["qst_loaded"], 16)
            sp.wait_ge(sig["mtr_ready"], b.n + 1)
            for r in range(NPAIR):
                sp.dma_start(qst[96:112, r, :].bitcast(F32), mtr[:, :].bitcast(F32)).then_inc(sig["qst_loaded"], 16)

        def s2(b):
            if not b.at(NB - 1):
                sp.wait_ge(sig["x1_ready"], b.n * TT)
                sp.dma_start(xb[1 - b.c], x_rows[b.n + 1]).then_inc(x_loaded[1 - b.c], 16)
            sp.wait_ge(sig["z_ready"], (b.n + 1) * TT)
            sp.dma_start(z_rows[b.n], zb).then_inc(sig["z_stored"], 16)

        def ffn(b):
            sp.wait_ge(sig["acc_done"], (b.n + 1) * TT)
            sp.dma_start(out_rows[b.n], x1[b.c]).then_inc(out_stored[b.c], 16)

        schedule(sp, s1, s2, ffn, lambda: None)

        def load_weights(e):
            for j in range(3):
                sp.wait_ge(sig["wsplit_lo"], (e.n * 3 + 3 + j) * NSTEP0)
                buf, _ = matrix(e, j)
                sp.dma_start(stage[buf].rearrange("p (k f) -> p k f", k=wv[j].shape[2]), wv[j][e.n])\
                  .then_inc(stage_loaded[buf], 16)

        def expert(e):
            if not e.at(E - 1):
                load_weights(e.next())

        sp.wait_ge(sig["pv_done"], NB * NPAIR)
        sp.wait_ge(sig["x1_ready"], T // P)
        load_weights(Turn(0, 0))
        with_experts(sp, expert)
        for c in range(2):
            sp.wait_ge(out_stored[c], 16 * NB // 2 + 16 * c)
        sp.wait_ge(sig["scattered"], 16 * NR * E)

    @block.gpsimd
    def _(pool):
        st = Steps(pool, sig["pool_const"], 0)

        def do(ins):
            st.did(ins)
            st.wait()

        pool.sem_inc(sig["ye_free"], 1)
        do(pool.memset(ident[:, :], 0.0))
        pool.affine_select(out=ident[:, :], in_=ident[:, :], compare_op=ALU.not_equal, fill=1.0, base=0,
                           pattern=[[-1, P]], channel_multiplier=1).then_inc(sig["ident_ready"], 1)
        do(pool.memset(kbd.bitcast(F32), 0.0))
        do(pool.memset(kst.bitcast(F32), 0.0))
        kneg = kst[96:112].rearrange("p a b t -> p (a b) t")
        do(pool.affine_select(out=kneg, in_=kneg.bitcast(F32), compare_op=ALU.not_equal, fill=-1.0, base=0,
                              pattern=[[-1, H], [0, SK]], channel_multiplier=1))
        do(pool.memset(qst.bitcast(F32), 0.0))
        do(pool.memset(nhalf[:, :], -0.5))
        do(pool.memset(mones[:, :], 1.0))
        do(pool.affine_select(out=lower[:, :], in_=mones[:, :], compare_op=ALU.is_gt, fill=0.0, base=0,
                              pattern=[[1, P]], channel_multiplier=-1))
        do(pool.memset(vst[0:SK], 0.0))
        for par in range(2):
            for j in range(4):
                do(pool.memset(vst[0:SK, :, par, j, den_at(par, j):den_at(par, j) + DH], 1.0))
        pool.memset(passed[:, :], 0.0).then_inc(sig["zeros_ready"], 1)
        pool.wait_ge(sig["v_ready"], B)

        def s1(b):
            if b.c == 0:
                pool.wait_ge(sig["pv_done"], b.n * NPAIR)
                for par in range(2):
                    for j in range(4):
                        src = vall[0:SK, b.i, :].rearrange("t (g w j d) -> t g w j d", g=2, w=2, j=4)[:, :, par, j, :]
                        pool.tensor_copy(vst[0:SK, :, par, j, val_at(par, j):val_at(par, j) + DH], src)\
                            .then_inc(sig["vst_ready"], 1)
                        pool.wait_ge(sig["vst_ready"], b.i * 8 + par * 4 + j + 1)
            pool.wait_ge(sig["rstd2_ready"], b.n)
            pool.wait_ge(sig["mv_ready"], b.n + 1)
            apart(pool)
            pool.tensor_scalar(vs[:, :], mv[:, :, 1], EPS, None, ALU.add).then_inc(sig["rstd_pre"], 1)
            pool.wait_ge(sig["rstd_pre"], b.n + 1)
            pool.tensor_tensor(rstd[:, :], vs[:, :], nhalf[:, :], ALU.pow).then_inc(sig["rstd_ready"], 1)
            pool.wait_ge(sig["xn_ready"], (b.n + 1) * TT)
            pool.wait_ge(sig["tbo_ready"], 1)
            for t in range(TT):
                pool.tensor_tensor(xb[b.c][:, t], xb[b.c][:, t], tbo[:, :], ALU.add).then_inc(sig["xb_ready"], 1)

        def s2(b):
            for k in range(KD):
                pool.wait_ge(sig["ah_ready"], b.n * KD + k + 1)
                pool.tensor_tensor(aT[:, 1, k], att[:, k], aT[:, 0, k].bitcast(F32), ALU.subtract)\
                    .then_inc(sig["al_ready"], 1)
            pool.wait_ge(sig["rstd_ready"], b.n + 1)
            pool.wait_ge(sig["mv2_ready"], b.n + 1)
            apart(pool)
            pool.tensor_scalar(vs[:, :], mv[:, :, 1], 1.0 + EPS, EPS * EPS, ALU.mult, ALU.add)\
                .then_inc(sig["rstd2_pre"], 1)
            pool.wait_ge(sig["rstd2_pre"], b.n + 1)
            pool.tensor_tensor(rstd[:, :], vs[:, :], nhalf[:, :], ALU.pow).then_inc(sig["rstd2_ready"], 1)

        def routing():
            pool.wait_ge(sig["lg_done"], NB)
            pool.wait_ge(sig["z_stored"], 16 * NB)
            pool.iota(r_em8, pattern=[[0, NTT], [1, E]], base=-8, channel_multiplier=0,
                      allow_small_or_imprecise_dtypes=True).then_inc(sig["r_const"], 1)
            pool.iota(r_tok, pattern=[[P, NTT]], base=1, channel_multiplier=1,
                      allow_small_or_imprecise_dtypes=True).then_inc(sig["r_const"], 1)
            pool.iota(r_iota, pattern=[[1, P]], base=0, channel_multiplier=0,
                      allow_small_or_imprecise_dtypes=True).then_inc(sig["r_const"], 1)
            pool.memset(r_ones, 1.0).then_inc(sig["r_const"], 1)

        schedule(pool, s1, s2, lambda b: None, routing)

        def gather(n):
            pool.wait_ge(sig["gather_idx"], n)
            apart(pool)
            for t in range(NR):
                pool.indirect_dma_start(xg[0:RT, t, :], None, zscr,
                                        bass.IndirectOffsetOnAxis(ap=gidx[0:RT, t:t + 1].bitcast(U32), axis=0))\
                    .then_inc(sig["gathered"], 16)

        pool.wait_ge(sig["z_stored"], 16 * NB)
        gather(1)
        for c in range(2):
            pool.wait_ge(out_stored[c], 16 * NB // 2 + 16 * c)

        def expert(e):
            if not e.at(E - 1):
                pool.wait_ge(sig["xeT_ready"], (e.n + 1) * 2 * KD)
                gather(e.n + 2)
            for half in range(2):
                pool.wait_ge(sig["acc_done"], T // P + (e.n * 2 + half + 1) * (NR // 2))
                apart(pool)
                for t in range(half * NR // 2, (half + 1) * NR // 2):
                    pool.indirect_dma_start(out2, bass.IndirectOffsetOnAxis(ap=sidx[e.c][0:RT, t:t + 1].bitcast(U32), axis=0),
                                            ye[0:RT, t, :], None, bounds_check=T - 1, oob_is_err=False,
                                            compute_op=ALU.add).then_inc(sig["scattered"], 16)
            pool.wait_ge(sig["scattered"], (e.n + 1) * NR * 16)
            pool.sem_inc(sig["ye_free"], 1)

        with_experts(pool, expert)

    @block.scalar
    def _(act):
        act.wait_ge(sig["consts_loaded"], 16 * NCONST)
        act.activation(tgx[:, :], gx[:, :], ACT.Tanh).then_inc(sig["tanh_done"], 1)
        act.activation(tgf[:, :], gy[:, :], ACT.Tanh).then_inc(sig["tanh_done"], 1)
        act.copy(ctx_s[:, 0], ctx_f.rearrange("p k b t -> p k (b t)")).then_inc(sig["ctx_hi"], 1)
        act.copy(wrs[:, :, 0:E], wrf[:, :, :]).then_inc(sig["wr_hi"], 1)

        def split_hi(dst_hi, m, piece, src):
            act.copy(dst_hi, src).then_inc(sig["wsplit_hi"], 1)

        act.wait_ge(stage_loaded[0], 64)
        for j in range(NSTEP0):
            split_hi(wat[:, 0, j], 0, j, watt_stage[:, j])
        for m in range(3):
            buf = (m + 1) % 2
            act.wait_ge(stage_loaded[buf], 80 if buf == 0 else 16 * (m // 2 + 1))
            for j in range(NSTEP0):
                split_hi(W0[:, 0, m, j * PIECE:(j + 1) * PIECE], m, j, sh_stage[buf][:, j * PIECE:(j + 1) * PIECE])
            if m == 0:
                for k in range(KD):
                    act.wait_ge(sig["kps_ready"], k + 1)
                    act.activation(k_s[:, 0, k], bank[k][:, 0:B * SK], ACT.Identity, bias=bk[:, k:k + 1])\
                       .then_inc(sig["k_hi"], 1)

        def s1(b):
            for k in range(KD):
                act.wait_ge(sig["xT_ready"], b.n * KD + k + 1)
                act.copy(xT[:, 0, k], bank[4 + k][:, :]).then_inc(sig["xh_ready"], 1)
            for k in range(KD):
                act.wait_ge(sig["q_ready"], b.n * KD + k + 1)
                act.activation(qT[:, 0, k], bank[6 + k][:, :], ACT.Identity, bias=bq[:, k:k + 1])\
                   .then_inc(sig["qh_ready"], 1)
            act.wait_ge(sig["mT_ready"], b.n + 1)
            act.copy(mtr[:, :], bank[4][0:H, :]).then_inc(sig["mtr_ready"], 1)

        def s2(b):
            def attn_hi(k):
                act.wait_ge(sig["attn_done"], b.n * NG + 2 * k + 2)
                act.copy(aT[:, 0, k], att[:, k]).then_inc(sig["ah_ready"], 1)
            for p in range(NPAIR):
                act.wait_ge(sig["scores_ready"], b.n * NPAIR + p + 1)
                if p >= 2:
                    act.wait_ge(sig["pv_done"], b.n * NPAIR + p - 1)
                for w in range(2):
                    last = act.activation(prob[p % 2][0:SK, w], bank[2 * (p % 2) + w][0:SK, :], ACT.Exp,
                                          scale=DH ** -0.5)
                last.then_inc(sig["exp_done"], 1)
                if p == 6:
                    attn_hi(0)
            attn_hi(1)
            for k in range(KD):
                act.wait_ge(sig["zT_ready"], b.n * KD + k + 1)
                act.activation(hT[:, 0, k], bank[4 + k][:, :], ACT.Identity, bias=lnb[:, k:k + 1],
                               scale=lng[:, k:k + 1]).then_inc(sig["hh_ready"], 1)
            act.wait_ge(sig["lg_ready"], b.n + 1)
            act.copy(lgs[:, :], bank[6][0:2 * E, :]).then_inc(sig["lgs_ready"], 1)

        def ffn(b):
            for f in range(NF + 1):
                if f < NF:
                    act.wait_ge(sig["a_ready"], b.n * NF + f + 1)
                    if f >= 2:
                        act.wait_ge(sig["gmul_done"], b.n * NF + f - 1)
                    act.activation(sil[f % 2], bank[2 * (f % 2)][:, :], ACT.Silu).then_inc(sig["sil_done"], 1)
                if f >= 1:
                    act.wait_ge(sig["gmul_done"], b.n * NF + f)
                    act.copy(gT[:, 0, (f - 1) % RING], gf[:, (f - 1) % 2]).then_inc(sig["gh_ready"], 1)

        def routing():
            act.wait_ge(sig["r_onehots"], 1)
            act.activation(r_e2, r_d, ACT.Exp).then_inc(sig["rexp_done"], 1)

        schedule(act, s1, s2, ffn, routing)

        def split_piece(e, n):
            m, j = n // 4, n % 4
            buf, loaded = matrix(e, m)
            if j == 0:
                act.wait_ge(stage_loaded[buf], loaded)
            dst = (W1_ if e.c == 0 else W0)[:, 0, m, j * PIECE:(j + 1) * PIECE]
            act.copy(dst, stage[buf][:, j * PIECE:(j + 1) * PIECE]).then_inc(sig["wsplit_hi"], 1)

        def xe_hi(e, g):
            k, half = g % KD, g // KD
            act.wait_ge(sig["xeT_ready"], e.n * 4 + g + 1)
            act.activation(xe[e.c][:, 0, k, half * HALF:(half + 1) * HALF], bank[7][:, 0:HALF], ACT.Identity,
                           bias=lnb[:, k:k + 1], scale=lng[:, k:k + 1]).then_inc(sig["xe_hi"], 1)

        for n in range(NPIECE):
            split_piece(Turn(0, 0), n)
        for g in range(4):
            xe_hi(Turn(0, 0), g)

        def expert(e):
            base = NB * NF + e.n * 2 * NF
            for n in range(2 * NF + 1):
                if n < 2 * NF:
                    act.wait_ge(sig["a_ready"], base + n + 1)
                    if n >= 2:
                        act.wait_ge(sig["gmul_done"], base + n - 1)
                    act.activation(sil[n % 2][:, 0:HALF], bank[2 * (n % 2)][:, 0:HALF], ACT.Silu)\
                       .then_inc(sig["sil_done"], 1)
                if n >= 1:
                    act.wait_ge(sig["gmul_done"], base + n)
                    act.copy(gT[:, 0, (n - 1) % RING, 0:HALF], gf[:, (n - 1) % 2, 0:HALF]).then_inc(sig["gh_ready"], 1)
                if not e.at(E - 1) and n < NPIECE:
                    split_piece(e.next(), n)
                if not e.at(E - 1) and n in XT_AT:
                    xe_hi(e.next(), XT_AT.index(n))

        with_experts(act, expert)

    @block.vector
    def _(dve):
        dve.wait_ge(sig["tanh_done"], 2)
        dve.tensor_scalar(tbo[:, :], tbo[:, :], tgx[:, 0:1], None, ALU.mult).then_inc(sig["tbo_ready"], 1)
        dve.wait_ge(sig["ctx_hi"], 1)
        dve.tensor_tensor(ctx_s[:, 1], ctx_f.rearrange("p k b t -> p k (b t)"), ctx_s[:, 0].bitcast(F32),
                          ALU.subtract).then_inc(sig["ctx_lo"], 1)
        dve.wait_ge(sig["wr_hi"], 1)
        dve.tensor_tensor(wrs[:, :, E:2 * E], wrf[:, :, :], wrs[:, :, 0:E].bitcast(F32), ALU.subtract)\
           .then_inc(sig["wr_ready"], 1)
        for j in range(NSTEP0):
            dve.wait_ge(sig["wsplit_hi"], j + 1)
            dve.tensor_tensor(wat[:, 1, j], watt_stage[:, j], wat[:, 0, j].bitcast(F32), ALU.subtract)\
               .then_inc(sig["wsplit_lo"], 1)
        for m in range(3):
            buf = (m + 1) % 2
            for j in range(NSTEP0):
                dve.wait_ge(sig["wsplit_hi"], NSTEP0 * (m + 1) + j + 1)
                cols = slice(j * PIECE, (j + 1) * PIECE)
                dve.tensor_tensor(W0[:, 1, m, cols], sh_stage[buf][:, cols], W0[:, 0, m, cols].bitcast(F32),
                                  ALU.subtract).then_inc(sig["wsplit_lo"], 1)
            if m == 0:
                for k in range(KD):
                    dve.wait_ge(sig["k_hi"], k + 1)
                    dve.scalar_tensor_tensor(out=k_s[:, 1, k], in0=bank[k][:, 0:B * SK], scalar=bk[:, k:k + 1],
                                             in1=k_s[:, 0, k].bitcast(F32), op0=ALU.add, op1=ALU.subtract)\
                       .then_inc(sig["k_lo"], 1)
                for b in range(B):
                    dve.wait_ge(sig["vps_ready"], b + 1)
                    dve.tensor_tensor(vall[0:SK, b], bank[2 + b % 2][0:SK, 0:D], bvb[:, :], ALU.add)\
                       .then_inc(sig["v_ready"], 1)

        def norm_stats(st, src, ready):
            for t in range(TT):
                st.did(dve.bn_stats(stt[:, t], src[:, t]))
            st.wait()
            apart(dve)
            for t in range(TT):
                last = dve.bn_aggr(mv[:, t], stt[:, t])
                if t < TT - 1:
                    st.did(last)
            last.then_inc(ready, 1)

        def s1(b):
            st = Steps(dve, sig["dve_s1"], b.n * 7)
            dve.wait_ge(x_loaded[b.c], (b.i + 1) * 16)
            dve.wait_ge(sig["z_ready"], b.n * TT)
            norm_stats(st, xb[b.c], sig["mv_ready"])
            assert st.k == 7
            dve.wait_ge(sig["rstd_ready"], b.n + 1)
            dve.wait_ge(sig["mv_ready"], b.n + 1)
            st.wait()
            dve.wait_ge(sig["z_stored"], b.n * 16)
            for t in range(TT):
                dve.tensor_scalar(zb[:, t], xb[b.c][:, t], mv[:, t, 0:1], rstd[:, t:t + 1], ALU.subtract, ALU.mult)\
                   .then_inc(sig["xn_ready"], 1)
            for k in range(KD):
                dve.wait_ge(sig["xh_ready"], b.n * KD + k + 1)
                dve.tensor_tensor(xT[:, 1, k], bank[4 + k][:, :], xT[:, 0, k].bitcast(F32), ALU.subtract)\
                   .then_inc(sig["xl_ready"], 1)
            for k in range(KD):
                dve.wait_ge(sig["qh_ready"], b.n * KD + k + 1)
                dve.scalar_tensor_tensor(out=qT[:, 1, k], in0=bank[6 + k][:, :], scalar=bq[:, k:k + 1],
                                         in1=qT[:, 0, k].bitcast(F32), op0=ALU.add, op1=ALU.subtract)\
                   .then_inc(sig["ql_ready"], 1)
            for t in range(TT):
                dve.wait_ge(sig["m_ready"], b.n * TT + t + 1)
                for j in range(4):
                    last = dve.tensor_reduce(mx[:, t, 4 * j:4 * j + 4],
                                             bank[j][:, 0:4 * SK].rearrange("p (h t) -> p h t", t=SK), AX.X, ALU.max)
                last.then_inc(sig["m_done"], 1)

        def s2(b):
            st = Steps(dve, sig["dve_s2"], b.n * 7)
            for g in range(NG):
                dve.wait_ge(sig["pv_done"], b.n * NPAIR + 2 * g + 2)
                dve.wait_ge(sig["hl_ready"], b.n * KD)
                dve.wait_ge(sig["attn_done"], b.n * NG + g)
                va, dn = (slice(0, 64), slice(64, 128)) if g % 2 == 0 else (slice(64, 128), slice(0, 64))
                dve.reciprocal(rc[va, :], bank[4 + g % 2][dn, :]).then_inc(sig["recip_done"], 1)
                dve.wait_ge(sig["recip_done"], b.n * NG + g + 1)
                dve.tensor_tensor(att[va, g // 2], bank[4 + g % 2][va, :], rc[va, :], ALU.mult)\
                   .then_inc(sig["attn_done"], 1)
            dve.wait_ge(sig["xb_ready"], (b.n + 1) * TT)
            dve.wait_ge(out_stored[b.c], b.i * 16 + 16 * b.c)
            for t in range(TT):
                dve.wait_ge(sig["oproj_ready"], b.n * TT + t + 1)
                dve.scalar_tensor_tensor(out=x1[b.c][:, t], in0=bank[6 + t % 2][:, 0:D], scalar=tgx[:, 0:1],
                                         in1=xb[b.c][:, t], op0=ALU.mult, op1=ALU.add).then_inc(sig["x1_ready"], 1)
            dve.wait_ge(sig["x1_ready"], (b.n + 1) * TT)
            dve.wait_ge(sig["xn_ready"], (b.n + 1) * TT)
            norm_stats(st, x1[b.c], sig["mv2_ready"])
            dve.wait_ge(sig["rstd2_ready"], b.n + 1)
            dve.wait_ge(sig["mv2_ready"], b.n + 1)
            st.wait()
            for t in range(TT):
                dve.tensor_scalar(zb[:, t], x1[b.c][:, t], mv[:, t, 0:1], rstd[:, t:t + 1], ALU.subtract, ALU.mult)\
                   .then_inc(sig["z_ready"], 1)
            for k in range(KD):
                dve.wait_ge(sig["hl_ready"], b.n * KD + k)
                dve.wait_ge(sig["hh_ready"], b.n * KD + k + 1)
                dve.tensor_scalar(hf[:, :], bank[4 + k][:, :], lng[:, k:k + 1], lnb[:, k:k + 1], ALU.mult, ALU.add)\
                   .then_inc(sig["hf_ready"], 1)
                dve.wait_ge(sig["hf_ready"], b.n * KD + k + 1)
                dve.tensor_tensor(hT[:, 1, k], hf[:, :], hT[:, 0, k].bitcast(F32), ALU.subtract)\
                   .then_inc(sig["hl_ready"], 1)
            dve.wait_ge(sig["lgT_ready"], b.n + 1)
            dve.tensor_copy(lgall[:, bass.ds(b.n * TT, TT), :],
                            bank[7][:, 0:64].rearrange("p (t e) -> p t e", t=TT)[:, :, 0:2 * E]).then_inc(sig["lg_done"], 1)

        def ffn(b):
            for f in range(NF + 1):
                if f < NF:
                    dve.wait_ge(sig["b_ready"], b.n * NF + f + 1)
                    dve.wait_ge(sig["sil_done"], b.n * NF + f + 1)
                    dve.wait_ge(sig["gl_ready"], b.n * NF + max(f - 1, 0))
                    dve.tensor_tensor(gf[:, f % 2], bank[2 * (f % 2) + 1][:, :], sil[f % 2], ALU.mult)\
                       .then_inc(sig["gmul_done"], 1)
                if f >= 1:
                    dve.wait_ge(sig["gh_ready"], b.n * NF + f)
                    dve.tensor_tensor(gT[:, 1, (f - 1) % RING], gf[:, (f - 1) % 2],
                                      gT[:, 0, (f - 1) % RING].bitcast(F32), ALU.subtract).then_inc(sig["gl_ready"], 1)
            for t in range(TT):
                dve.wait_ge(sig["acc_ready"], b.n * TT + t + 1)
                dve.scalar_tensor_tensor(out=x1[b.c][:, t], in0=bank[4 + t][:, 0:D], scalar=tgf[:, 0:1],
                                         in1=x1[b.c][:, t], op0=ALU.mult, op1=ALU.add).then_inc(sig["acc_done"], 1)

        def routing():
            st = Steps(dve, sig["route_step"], 0)

            def do(ins):
                st.did(ins)
                st.wait()

            dve.wait_ge(sig["lg_done"], NB)
            dve.wait_ge(sig["r_const"], 4)
            fl = lambda v: v.rearrange("p t e -> p (t e)")
            bc = lambda v: v.unsqueeze(2).broadcast_to([P, NTT, E])
            do(dve.tensor_tensor(r_lg, lgall[:, :, 0:E], lgall[:, :, E:2 * E], ALU.add))
            for ch in range(2):
                do(dve.tensor_reduce(r_m[:, ch], r_lg, AX.X, ALU.max))
                do(dve.tensor_tensor(r_tmp, r_lg, bc(r_m[:, ch]), ALU.is_equal))
                do(dve.tensor_tensor(r_tmp, r_tmp, r_em8, ALU.mult))
                do(dve.tensor_reduce(r_i[:, ch], r_tmp, AX.X, ALU.min))
                do(dve.tensor_tensor(r_oh[:, ch], r_em8, bc(r_i[:, ch]), ALU.is_equal))
                if ch == 0:
                    do(dve.scalar_tensor_tensor(out=fl(r_lg), in0=fl(r_oh[:, 0]), scalar=-3e38, in1=fl(r_lg),
                                                op0=ALU.mult, op1=ALU.add))
            dve.tensor_tensor(r_d, r_m[:, 1], r_m[:, 0], ALU.subtract).then_inc(sig["r_onehots"], 1)
            dve.wait_ge(sig["rexp_done"], 1)
            do(dve.tensor_scalar(r_d, r_e2, 1.0, None, ALU.add))
            do(dve.reciprocal(r_g[:, 0], r_d))
            do(dve.tensor_scalar(r_g[:, 0], r_g[:, 0], tgf[:, 0:1], None, ALU.mult))
            do(dve.tensor_tensor(r_g[:, 1], r_g[:, 0], r_e2, ALU.mult))
            dve.wait_ge(sig["r_counts"], 2)
            do(dve.tensor_copy(r_tot, bank[7][:, 0:2 * NTT * E].rearrange("p (t e) -> p t e", e=E)))
            for e in range(E):
                st.did(dve.tensor_tensor_scan(r_inc[:, :, e], r_ones, r_tot[:, :, e], 0.0, ALU.mult, ALU.add))
            st.wait()
            do(dve.tensor_tensor(r_inc, r_inc, r_tot, ALU.subtract))
            do(dve.tensor_tensor(r_inc, bank[6][:, 0:2 * NTT * E].rearrange("p (t e) -> p t e", e=E), r_inc, ALU.add))
            do(dve.tensor_tensor(r_inc, r_inc, r_oh.rearrange("p c t e -> p (c t) e"), ALU.mult))
            do(dve.tensor_reduce(r_pos, r_inc, AX.X, ALU.add))
            do(dve.tensor_scalar(r_hi, r_i.rearrange("p c t -> p (c t)"), float(NR), 8.0 * NR, ALU.mult, ALU.add))
            do(dve.tensor_copy(r_lo, r_pos))
            for k in range(1, NR + 1):
                do(dve.tensor_scalar(r_ge, r_pos, float(k * RT), None, ALU.is_ge))
                if k < NR:
                    do(dve.tensor_tensor(r_hi, r_hi, r_ge, ALU.add))
                do(dve.scalar_tensor_tensor(out=r_lo, in0=r_ge, scalar=(-float(RT) if k < NR else 1e6), in1=r_lo,
                                            op0=ALU.mult, op1=ALU.add))
            gall = r_g.rearrange("p c t -> p (c t)")
            for n in range(2 * NTT):
                if n >= OHB:
                    dve.wait_ge(sig["oh_used"], n - OHB + 1)
                dve.tensor_scalar(r_row[:, n % OHB], r_iota[:, 0:RT], r_lo[:, n:n + 1], None, ALU.is_equal)\
                   .then_inc(sig["oh_ready"], 1)
                dve.tensor_scalar(r_val[:, n % OHB, 0], r_iota[:, 0:NSL], r_hi[:, n:n + 1],
                                  r_tok[:, n % NTT:n % NTT + 1], ALU.is_equal, ALU.mult).then_inc(sig["oh_ready"], 1)
                dve.tensor_scalar(r_val[:, n % OHB, 1], r_iota[:, 0:NSL], r_hi[:, n:n + 1],
                                  gall[:, n:n + 1], ALU.is_equal, ALU.mult).then_inc(sig["oh_ready"], 1)
            dve.wait_ge(sig["oh_used"], 2 * NTT)
            tk = r_val[:, 0, 0]
            do(dve.tensor_copy(tabw[0:RT, :], bank[6][0:RT, NSL:2 * NSL]))
            do(dve.tensor_scalar(tk[0:RT], bank[6][0:RT, 0:NSL], -1.0, None, ALU.add))
            do(dve.tensor_scalar(tabg[0:RT, :], tk[0:RT], 0.0, None, ALU.max))
            do(dve.tensor_scalar(r_val[0:RT, 0, 1], tk[0:RT], 0.0, 2.0 * T, ALU.is_lt, ALU.mult))
            dve.tensor_tensor(tabs[0:RT, :], tk[0:RT], r_val[0:RT, 0, 1], ALU.add).then_inc(sig["tab_done"], 1)
            dve.wait_ge(sig["tab_done"], 1)
            dve.tensor_copy(gidx[0:RT, :], tabg[0:RT, 0:NR]).then_inc(sig["gather_idx"], 1)

        schedule(dve, s1, s2, ffn, routing)

        def index_now(e):
            dve.tensor_copy(sidx[e.c][0:RT, :], tabs[0:RT, bass.ds(e.n * NR, NR)]).then_inc(sig["sidx_ready"], 1)
            dve.tensor_copy(gw[e.c][0:RT, :], tabw[0:RT, bass.ds(e.n * NR, NR)]).then_inc(sig["gw_ready"], 1)

        def split_piece(e, n):
            m, j = n // 4, n % 4
            buf, _ = matrix(e, m)
            dve.wait_ge(sig["wsplit_hi"], e.n * NPIECE + 4 * NSTEP0 + n + 1)
            w = W1_ if e.c == 0 else W0
            cols = slice(j * PIECE, (j + 1) * PIECE)
            dve.tensor_tensor(w[:, 1, m, cols], stage[buf][:, cols], w[:, 0, m, cols].bitcast(F32), ALU.subtract)\
               .then_inc(sig["wsplit_lo"], 1)

        def xe_lo(e, g):
            k, half = g % KD, g // KD
            cols = slice(half * HALF, (half + 1) * HALF)
            dve.wait_ge(sig["xe_lo"], e.n * 4 + g)
            dve.wait_ge(sig["xe_hi"], e.n * 4 + g + 1)
            dve.tensor_scalar(hf[:, 0:HALF], bank[7][:, 0:HALF], lng[:, k:k + 1], lnb[:, k:k + 1], ALU.mult, ALU.add)\
               .then_inc(sig["xe_f"], 1)
            dve.wait_ge(sig["xe_f"], e.n * 4 + g + 1)
            dve.tensor_tensor(xe[e.c][:, 1, k, cols], hf[:, 0:HALF], xe[e.c][:, 0, k, cols].bitcast(F32), ALU.subtract)\
               .then_inc(sig["xe_lo"], 1)

        for n in range(NPIECE):
            split_piece(Turn(0, 0), n)
        for g in range(4):
            xe_lo(Turn(0, 0), g)

        def y_out(e, half):
            if half == 0:
                dve.wait_ge(sig["gw_ready"], e.n + 1)
                dve.wait_ge(sig["ye_free"], e.n + 1)
            for t in range(NR // 2):
                dve.wait_ge(sig["acc_ready"], T // P + (e.n * 2 + half) * (NR // 2) + t + 1)
                r = half * (NR // 2) + t
                dve.tensor_scalar(ye[0:RT, r, :], bank[4 + t][0:RT, 0:D], gw[e.c][0:RT, r:r + 1], None, ALU.mult)\
                   .then_inc(sig["acc_done"], 1)

        def expert(e):
            base = NB * NF + e.n * 2 * NF
            dve.wait_ge(sig["acc_done"], T // P + e.n * NR)
            index_now(e)
            if not e.at(E - 1):
                dve.wait_ge(sig["gathered"], (e.n + 1) * NR * 16)
                dve.tensor_copy(gidx[0:RT, :], tabg[0:RT, bass.ds((e.n + 1) * NR, NR)]).then_inc(sig["gather_idx"], 1)
            for n in range(2 * NF + 1):
                if n < 2 * NF:
                    dve.wait_ge(sig["b_ready"], base + n + 1)
                    dve.wait_ge(sig["sil_done"], base + n + 1)
                    dve.wait_ge(sig["gl_ready"], base + max(n - 1, 0))
                    dve.tensor_tensor(gf[:, n % 2, 0:HALF], bank[2 * (n % 2) + 1][:, 0:HALF], sil[n % 2][:, 0:HALF],
                                      ALU.mult).then_inc(sig["gmul_done"], 1)
                if n >= 1:
                    dve.wait_ge(sig["gh_ready"], base + n)
                    dve.tensor_tensor(gT[:, 1, (n - 1) % RING, 0:HALF], gf[:, (n - 1) % 2, 0:HALF],
                                      gT[:, 0, (n - 1) % RING, 0:HALF].bitcast(F32), ALU.subtract)\
                       .then_inc(sig["gl_ready"], 1)
                if not e.at(E - 1) and n < NPIECE:
                    split_piece(e.next(), n)
                if not e.at(E - 1) and n in XT_AT:
                    xe_lo(e.next(), XT_AT.index(n))
                if n == NF + 1:
                    y_out(e, 0)
            y_out(e, 1)

        with_experts(dve, expert)

    @block.tensor
    def _(pe):
        def three(o, lhs, rhs, first, last):
            pe.matmul(o, lhs[0], rhs[0], start=first, stop=False)
            pe.matmul(o, lhs[0], rhs[1], start=False, stop=False)
            return pe.matmul(o, lhs[1], rhs[0], start=False, stop=last)

        pe.wait_ge(sig["ctx_lo"], 1)
        pe.wait_ge(sig["wsplit_lo"], NSTEP0)
        for m in range(KD):
            for k in range(KD):
                last = three(bank[m][:, 0:B * SK], [wat[:, j, 1, k, m * P:(m + 1) * P] for j in range(2)],
                             [ctx_s[:, j, k] for j in range(2)], k == 0, k == KD - 1)
            last.then_inc(sig["kps_ready"], 1)
        for b in range(B):
            if b >= 2:
                pe.wait_ge(sig["v_ready"], b - 1)
            for k in range(KD):
                last = three(bank[2 + b % 2][0:SK, 0:D], [ctx_s[:, j, k, b * SK:(b + 1) * SK] for j in range(2)],
                             [wat[:, j, 2, k] for j in range(2)], k == 0, k == KD - 1)
            last.then_inc(sig["vps_ready"], 1)
        pe.wait_ge(sig["ident_ready"], 1)
        pe.wait_ge(sig["k_lo"], KD)
        pe.wait_ge(sig["v_ready"], B)

        def s1(b):
            for k in range(KD):
                for t in range(TT):
                    if k == 0:
                        pe.wait_ge(sig["xn_ready"], b.n * TT + t + 1)
                    mm = pe.transpose(bank[4 + k][:, t * P:(t + 1) * P], zb[:, t, k * P:(k + 1) * P], ident[:, :])
                mm.then_inc(sig["xT_ready"], 1)
            pe.wait_ge(sig["xl_ready"], (b.n + 1) * KD)
            pe.wait_ge(sig["lg_done"], b.n)
            for m in range(KD):
                for k in range(KD):
                    mm = three(bank[6 + m][:, :], [wat[:, j, 0, k, m * P:(m + 1) * P] for j in range(2)],
                               [xT[:, j, k] for j in range(2)], k == 0, k == KD - 1)
                mm.then_inc(sig["q_ready"], 1)
            pe.wait_ge(sig["qh_ready"], (b.n + 1) * KD)
            if b.c == 0:
                pe.wait_ge(sig["kbd_loaded"], (b.i + 1) * 128)
            for t in range(TT):
                if t >= 1:
                    pe.wait_ge(sig["m_done"], b.n * TT + t)
                for j in range(4):
                    mm = pe.matmul(bank[j][:, 0:4 * SK], qT[:, 0, j // 2, t * P:(t + 1) * P],
                                   kbd[:, j // 2, 4 * (j % 2):4 * (j % 2) + 4, :], start=True, stop=True)
                mm.then_inc(sig["m_ready"], 1)
            pe.wait_ge(sig["m_done"], (b.n + 1) * TT)
            for t in range(TT):
                mm = pe.transpose(bank[4][0:H, t * P:(t + 1) * P], mx[:, t], ident[:, :])
            mm.then_inc(sig["mT_ready"], 1)

        def s2(b):
            def pv(p):
                if p == 0:
                    pe.wait_ge(sig["vst_ready"], (b.i + 1) * 8)
                    pe.wait_ge(sig["acc_done"], b.n * TT)
                    pe.wait_ge(sig["mtr_ready"], b.n + 1)
                if p % 2 == 0 and p >= 4:
                    pe.wait_ge(sig["attn_done"], b.n * NG + p // 2 - 1)
                pe.wait_ge(sig["exp_done"], b.n * NPAIR + p + 1)
                for w in range(2):
                    h = 2 * p + w
                    g, j = h // 4, h % 4
                    mm = pe.matmul(bank[4 + g % 2][:, :], vst[0:SK, g // 2, g % 2, j, :], prob[p % 2][0:SK, w],
                                   start=(j == 0), stop=(j == 3))
                mm.then_inc(sig["pv_done"], 1)

            pe.wait_ge(sig["qst_loaded"], (b.n + 1) * 16 * NQST)
            if b.c == 0:
                pe.wait_ge(sig["kst_loaded"], (b.i + 1) * 96)
            pe.wait_ge(sig["gmul_done"], b.n * NF)
            for p in range(NPAIR):
                if p >= 2:
                    pe.wait_ge(sig["exp_done"], b.n * NPAIR + p - 1)
                for w in range(2):
                    mm = pe.matmul(bank[2 * (p % 2) + w][0:SK, :], kst[:, p, w, :], qst[:, p, :], start=True, stop=True)
                mm.then_inc(sig["scores_ready"], 1)
                if p >= 1:
                    pv(p - 1)
            pv(NPAIR - 1)
            pe.wait_ge(sig["ql_ready"], (b.n + 1) * KD)
            pe.wait_ge(sig["al_ready"], (b.n + 1) * KD)
            for t in range(TT):
                if t >= 2:
                    pe.wait_ge(sig["x1_ready"], b.n * TT + t - 1)
                for k in range(KD):
                    mm = three(bank[6 + t % 2][:, 0:D], [aT[:, j, k, t * P:(t + 1) * P] for j in range(2)],
                               [wat[:, j, 3, k] for j in range(2)], k == 0, k == KD - 1)
                mm.then_inc(sig["oproj_ready"], 1)
            pe.wait_ge(sig["attn_done"], (b.n + 1) * NG)
            for k in range(KD):
                for t in range(TT):
                    if k == 0:
                        pe.wait_ge(sig["z_ready"], b.n * TT + t + 1)
                    mm = pe.transpose(bank[4 + k][:, t * P:(t + 1) * P], zb[:, t, k * P:(k + 1) * P], ident[:, :])
                mm.then_inc(sig["zT_ready"], 1)
            pe.wait_ge(sig["wr_ready"], 1)
            pe.wait_ge(sig["hl_ready"], (b.n + 1) * KD)
            for k in range(KD):
                for j in range(2):
                    mm = pe.matmul(bank[6][0:2 * E, :], wrs[:, k, :], hT[:, j, k], start=(k + j == 0),
                                   stop=(k + j == 2))
            mm.then_inc(sig["lg_ready"], 1)
            pe.wait_ge(sig["lgs_ready"], b.n + 1)
            apart(pe)
            for t in range(TT):
                mm = pe.transpose(bank[7][:, 16 * t:16 * t + 2 * E], lgs[:, t * P:(t + 1) * P], ident[0:2 * E, 0:2 * E])
            mm.then_inc(sig["lgT_ready"], 1)

        def ffn(b):
            def down(f):
                pe.wait_ge(sig["gl_ready"], b.n * NF + f + 1)
                if f == 0:
                    pe.wait_ge(sig["acc_done"], b.n * TT)
                for t in range(TT):
                    mm = three(bank[4 + t][:, 0:D], [gT[:, j, f % RING, t * P:(t + 1) * P] for j in range(2)],
                               [W0[:, j, 2, f * D:(f + 1) * D] for j in range(2)], f == 0, f == NF - 1)
                    if f == NF - 1:
                        mm.then_inc(sig["acc_ready"], 1)

            pe.wait_ge(sig["wsplit_lo"], 4 * NSTEP0)
            pe.wait_ge(sig["gmul_done"], b.n * NF)
            for f in range(NF):
                if f >= 2:
                    pe.wait_ge(sig["gmul_done"], b.n * NF + f - 1)
                for w, ready in ((0, sig["a_ready"]), (1, sig["b_ready"])):
                    for k in range(KD):
                        mm = three(bank[2 * (f % 2) + w][:, :],
                                   [W0[:, j, w, k * FF + f * P:k * FF + (f + 1) * P] for j in range(2)],
                                   [hT[:, j, k] for j in range(2)], k == 0, k == KD - 1)
                    mm.then_inc(ready, 1)
                if f == 1:
                    before_down(pe, b)
                if f >= 2:
                    down(f - 2)
            down(NF - 2)
            down(NF - 1)

        def before_down(pe, b):
            pe.wait_ge(sig["lg_done"], b.n + 1)
            if b.at(NB - 1):
                pe.wait_ge(sig["tab_done"], 1)
            if not b.at(NB - 1):
                pe.wait_ge(sig["ql_ready"], (b.n + 2) * KD)
                pe.wait_ge(sig["mtr_ready"], b.n + 2)

        def routing():
            pe.wait_ge(sig["r_onehots"], 1)
            pe.wait_ge(sig["zeros_ready"], 1)
            pe.wait_ge(sig["acc_done"], (NB - 1) * TT)
            oh = r_oh.rearrange("p c t e -> p (c t e)")
            pe.matmul(bank[6][:, 0:2 * NTT * E], lower[:, :], oh, start=True, stop=True).then_inc(sig["r_counts"], 1)
            pe.matmul(bank[7][:, 0:2 * NTT * E], mones[:, :], oh, start=True, stop=True).then_inc(sig["r_counts"], 1)
            for n in range(2 * NTT):
                pe.wait_ge(sig["oh_ready"], 3 * n + 3)
                mm = pe.matmul(bank[6][0:RT, 0:2 * NSL], r_row[:, n % OHB], r_val[:, n % OHB].rearrange("p a b -> p (a b)"),
                               start=(n == 0), stop=(n == 2 * NTT - 1))
                mm.then_inc(sig["oh_used"], 1)

        schedule(pe, s1, s2, ffn, routing)

        def xpose(e, g):
            k, half = g % KD, g // KD
            pe.wait_ge(sig["gathered"], (e.n + 1) * NR * 16)
            pe.wait_ge(sig["xe_lo"], e.n * 4 + g)
            for t in range(NR // 2):
                mm = pe.transpose(bank[7][:, t * RT:(t + 1) * RT], xg[0:RT, half * (NR // 2) + t, k * P:(k + 1) * P],
                                  ident[0:RT, 0:RT])
            mm.then_inc(sig["xeT_ready"], 1)

        pe.wait_ge(sig["acc_done"], NB * TT)
        for g in range(4):
            xpose(Turn(0, 0), g)

        def expert(e):
            base = NB * NF + e.n * 2 * NF
            w = W1_ if e.c == 0 else W0

            def down(n):
                half, f = n // NF, n % NF
                pe.wait_ge(sig["gl_ready"], base + n + 1)
                if f == 0:
                    pe.wait_ge(sig["acc_done"], T // P + (e.n * 2 + half) * (NR // 2))
                for t in range(NR // 2):
                    mm = three(bank[4 + t][0:RT, 0:D], [gT[:, j, n % RING, t * RT:(t + 1) * RT] for j in range(2)],
                               [w[:, j, 2, f * D:(f + 1) * D] for j in range(2)], f == 0, f == NF - 1)
                    if f == NF - 1:
                        mm.then_inc(sig["acc_ready"], 1)

            pe.wait_ge(sig["wsplit_lo"], e.n * NPIECE + 4 * NSTEP0 + NPIECE)
            pe.wait_ge(sig["xe_lo"], e.n * 4 + 4)
            pe.wait_ge(sig["gmul_done"], base)
            pe.wait_ge(sig["gmul_done"], NB * NF)
            for n in range(2 * NF):
                half, f = n // NF, n % NF
                if n >= 2:
                    pe.wait_ge(sig["gmul_done"], base + n - 1)
                for m, ready in ((0, sig["a_ready"]), (1, sig["b_ready"])):
                    for k in range(KD):
                        mm = three(bank[2 * (n % 2) + m][:, 0:HALF],
                                   [w[:, j, m, k * FF + f * P:k * FF + (f + 1) * P] for j in range(2)],
                                   [xe[e.c][:, j, k, half * HALF:(half + 1) * HALF] for j in range(2)],
                                   k == 0, k == KD - 1)
                    mm.then_inc(ready, 1)
                if not e.at(E - 1) and n in XT_AT:
                    xpose(e.next(), XT_AT.index(n))
                if n >= 2:
                    down(n - 2)
            down(2 * NF - 2)
            down(2 * NF - 1)

        with_experts(pe, expert)

    ctx.close()


INS = {"x": "x", "ctxT": "ctx_1024", "g_xattn": "g_xattn", "g_ffn": "g_ffn",
       "WqT": "L0_xattn_W_q", "WkT": "L0_xattn_W_k", "WvT": "L0_xattn_W_v", "WoT": "L0_xattn_W_o"}
SAME = ["L0_xattn_b_q", "L0_xattn_b_k", "L0_xattn_b_v", "L0_xattn_b_o", "L0_ffn_ln_g", "L0_ffn_ln_b", "L0_ffn_Wr",
        "L0_ffn_W1", "L0_ffn_W3", "L0_ffn_W2", "L0_ffn_W1s", "L0_ffn_W3s", "L0_ffn_W2s"]


def kernel(**inputs):
    import concourse.bacc as bacc
    import numpy as np
    from concourse.bass_utils import run_bass_kernel_spmd

    nc = bacc.Bacc("TRN2", target_bir_lowering=False, num_devices=1)
    arrays, aps = {}, {}
    for name, src in [*INS.items(), *((n, n) for n in SAME)]:
        v = np.asarray(inputs[src])
        if name.endswith("T"):
            v = np.swapaxes(v, -1, -2)
        v = np.ascontiguousarray(v)
        arrays[f"in_{name}"] = v
        aps[name] = nc.dram_tensor(f"in_{name}", v.shape, mybir.dt.from_np(v.dtype), kind="ExternalInput").ap()
    out = nc.dram_tensor("out_0", (B, S, D), F32, kind="ExternalOutput").ap()
    build(nc, aps, out)
    r = run_bass_kernel_spmd(nc, [arrays], core_ids=[0])
    return r.results[0]["out_0"]
```

```python
from contextlib import ExitStack

import concourse.bass as bass
import concourse.mybir as mybir

F32 = mybir.dt.float32
F32R = mybir.dt.float32r
I32 = mybir.dt.int32
U32 = mybir.dt.uint32
ALU = mybir.AluOpType
ACT = mybir.ActivationFunctionType
AX = mybir.AxisListType

P = 128
B, S, D = 4, 1024, 256
SK = 77
H, DH = 16, 16
FF = 1024
E = 7
CAP = 732
EPS = 1e-5
T = B * S
N = 512
TT = N // P
NB = T // N
KD = D // P
NF = FF // P
NPAIR = H // 2
NG = H // 4
RT = 122
NR = CAP // RT
HALF = CAP // 2
NTT = T // P
NSL = E * NR
WCOLS = KD * FF
PIECE = 512
NPIECE = 3 * WCOLS // PIECE
RING = 4


NCONST = 11
NQST = 20
XT_AT = (6, 8, 10, 12)
OHB = 4
NSTEP0 = WCOLS // PIECE
MAX_HEADS = ((0, 6), (6, 12), (12, 16))


class Turn:

    def __init__(self, i, c):
        self.i, self.c = i, c
        self.n = i * 2 + c

    def at(self, n):
        return isinstance(self.n, int) and self.n == n

    def next(self):
        return Turn(self.i, 1) if self.c == 0 else Turn(self.i + 1, 0)

    def prev(self):
        return Turn(self.i, 0) if self.c == 1 else Turn(self.i - 1, 1)


def period(do, b, first=False, last=False):
    n, f = b.next(), b.prev()

    def nxt(step, *args):
        if not last:
            do(step, n, *args)

    def up(k):
        if first:
            do("split_shared", k)
        else:
            do("up", f, k)

    def down(k):
        if not first:
            do("down", f, k)

    nxt("norm")
    do("scores", b)
    up(0)
    nxt("transpose_x")
    up(1)
    do("project", b)
    nxt("queries")
    do("norm2", b)
    up(2)
    down(0)
    do("transpose_z", b)
    up(3)
    down(1)
    do("logits", b)
    up(4)
    do("logits_T", b)
    down(2)
    nxt("maxima", 0)
    up(5)
    nxt("maxima", 1)
    down(3)
    nxt("maxima", 2)
    up(6)
    nxt("maxima", 3)
    down(4)
    nxt("maxima_T")
    up(7)
    if not first:
        down(5)
        do("last_hidden", f)
        down(6)
        down(7)
        do("shared_out", f)


def token_blocks(eng, steps):
    def do(step, *args):
        if step in steps:
            steps[step](*args)

    start, end = Turn(0, 0), Turn(NB // 2 - 1, 1)
    for step in ("norm", "transpose_x", "queries"):
        do(step, start)
    for t in range(TT):
        do("maxima", start, t)
    do("maxima_T", start)
    period(do, start, first=True)
    with eng.Fori(0, NB // 2 - 2) as i:
        period(do, Turn(i, 1))
        period(do, Turn(i + 1, 0))
    period(do, Turn(NB // 2 - 2, 1))
    period(do, Turn(NB // 2 - 1, 0))
    period(do, end, last=True)
    do("choose")
    do("up", end, 0)
    do("up", end, 1)
    do("count")
    for k in range(2, NF):
        do("up", end, k)
        do("down", end, k - 2)
        do("place", k - 2)
    do("last_hidden", end)
    do("down", end, NF - 2)
    do("down", end, NF - 1)
    do("shared_out", end)
    do("place", NF - 2)
    do("table")


def with_experts(eng, expert):
    with eng.Fori(0, E // 2) as i:
        expert(Turn(i, 0))
        expert(Turn(i, 1))
    expert(Turn(E // 2, 0))


def val_at(par, j):
    return DH * j + 64 * par


def den_at(par, j):
    return DH * j + 64 * (1 - par)


def placed(k):
    return {4: (0, 8), 5: (8, 20), 6: (20, 2 * NTT)}.get(k, (0, 0))


class Steps:

    def __init__(self, eng, sem, base):
        self.eng, self.sem, self.base, self.k = eng, sem, base, 0

    def did(self, ins):
        self.k += 1
        ins.then_inc(self.sem, 1)

    def wait(self):
        self.eng.wait_ge(self.sem, self.base + self.k)


def build(nc, a, out):
    ctx = ExitStack()

    def sem(name):
        return ctx.enter_context(nc.semaphore(name))

    def sb(name, shape, dt=F32):
        return ctx.enter_context(nc.sbuf_tensor(name, shape, dt))

    KB = 256
    AR = sb("split_operands", [P, 142 * KB], F32R)

    def ar(off_kb, *dims):
        n = 1
        for d in dims:
            n *= d
        v = AR[:, off_kb * KB:off_kb * KB + n]
        names = "abcd"[:len(dims)]
        if len(dims) == 1:
            return v
        return v.rearrange(f"p ({' '.join(names)}) -> p {' '.join(names)}", **dict(zip(names, dims)))

    W0 = ar(0, 2, 3, WCOLS)
    W1_ = ar(48, 2, 3, WCOLS)
    wat = ar(48, 2, 4, KD, D)
    xT = ar(64, 2, KD, N)
    qT = ar(72, 2, KD, N)
    aT = qT
    qst = ar(80, NPAIR, N)
    kst = ar(96, NPAIR, 2, SK)
    kbd = ar(101, KD, 8, SK)
    hTs = [ar(130, 2, KD, N), ar(106, 2, KD, N)]
    gT = ar(114, 2, RING, N)
    ctx_s = ar(114, 2, KD, B * SK)
    k_s = ar(119, 2, KD, B * SK)
    xe = [ar(130, 2, KD, CAP), ar(96, 2, KD, CAP)]
    wrs = sb("router_split", [P, KD, 2 * E], F32R)
    mtr = sb("row_max_T", [H, N], F32R)

    AF = sb("float_data", [P, 48 * KB], F32)

    def af(off_kb, *dims):
        n = 1
        for d in dims:
            n *= d
        v = AF[:, off_kb * KB:off_kb * KB + n]
        names = "abcd"[:len(dims)]
        if len(dims) == 1:
            return v
        return v.rearrange(f"p ({' '.join(names)}) -> p {' '.join(names)}", **dict(zip(names, dims)))

    xb = [af(0, TT, D), af(4, TT, D)]
    prob = [af(8, 2, N), af(12, 2, N)]
    vst = af(16, 2, 2, 4, P)
    vall = af(24, B, D)
    x1 = [af(28, TT, D), af(32, TT, D)]
    zb = af(36, TT, D)
    att = zb.rearrange("p a b -> p (a b)").rearrange("p (k n) -> p k n", k=KD)
    sil = [af(40, N), af(42, N)]
    xn = af(44, TT, D)
    gf = sb("hidden", [P, 2, N])
    stage = [af(0, WCOLS), af(8, WCOLS)]
    xg = af(16, NR, D)
    ye = af(22, NR, D)

    rc = sb("recip_den", [P, N])
    hf = rc
    watt_stage = af(8, 4, 2 * D)
    sh_stage = [af(32, WCOLS // 2), af(40, WCOLS // 2), gf.rearrange("p a n -> p (a n)")]
    ctx_f = af(36, KD, B, SK)
    ident = sb("ident", [P, P])
    mones = sb("ones", [P, P])
    lower = sb("earlier_tokens", [P, P])
    lgall = sb("logit_parts", [P, NTT, 2 * E])
    lgs = sb("logits_T", [2 * E, N])
    tbo = sb("gated_bias_o", [P, D])
    bvb = sb("bias_v", [SK, D])
    bq = sb("bias_q", [P, KD])
    bk = sb("bias_k", [P, KD])
    lng = sb("ln_gain", [P, KD])
    lnb = sb("ln_bias", [P, KD])
    wrf = sb("router_raw", [P, KD, E])
    gx = sb("gate_x", [P, 1])
    gy = sb("gate_f", [P, 1])
    tgx = sb("tanh_gate_x", [P, 1])
    tgf = sb("tanh_gate_f", [P, 1])
    passed = sb("all_set", [P, 1])
    nhalf = sb("minus_half", [P, TT])
    stt = [sb(f"bn_parts{j}", [P, TT, 6]) for j in range(2)]
    mv = [sb(f"mean_var{j}", [P, TT, 2]) for j in range(2)]
    vs = [sb(f"var_scaled{j}", [P, TT]) for j in range(2)]
    rstd = [sb(f"rstd{j}", [P, TT]) for j in range(2)]
    mx = sb("row_max", [P, TT, H])
    tabg = sb("gather_table", [P, NSL], I32)
    tabs = sb("scatter_table", [P, NSL], I32)
    tabw = sb("gate_table", [P, NSL])
    gidx = sb("gather_now", [P, NR], I32)
    sidx = [sb("scatter_now0", [P, NR], I32), sb("scatter_now1", [P, NR], I32)]
    gw = [sb("gates_now0", [P, NR]), sb("gates_now1", [P, NR])]

    bank = [ctx.enter_context(nc.psum_tensor(f"bank{j}", [P, 512], F32)) for j in range(8)]

    kscr = nc.dram_tensor("k_scratch", (2, D, B * SK), F32).ap()
    zscr = nc.dram_tensor("z_scratch", (T, D), F32).ap()

    at = {}

    def rt(region_kb, *dims):
        n = 1
        for d in dims:
            n *= d
        off = at.get(region_kb, 0)
        at[region_kb] = off + n
        v = AF[:, region_kb * KB + off:region_kb * KB + off + n]
        names = "abcd"[:len(dims)]
        if len(dims) == 1:
            return v
        return v.rearrange(f"p ({' '.join(names)}) -> p {' '.join(names)}", **dict(zip(names, dims)))

    r_lg, r_tmp, r_em8 = (rt(16, NTT, E) for _ in range(3))
    r_oh = rt(16, 2, NTT, E)
    r_tot, r_inc = (rt(16, 2 * NTT, E) for _ in range(2))
    r_m, r_i, r_g = (rt(24, 2, NTT) for _ in range(3))
    r_d, r_e2, r_tok = (rt(24, NTT) for _ in range(3))
    r_pos, r_hi, r_lo, r_ge, r_ones = (rt(24, 2 * NTT) for _ in range(5))
    r_iota = rt(24, P)
    r_row = rt(36, OHB, RT)
    r_val = rt(36, OHB, 2, NSL)
    assert at[16] <= 8 * KB and at[24] <= 4 * KB and at[36] <= 4 * KB

    names = """passed consts_loaded stage_loaded0 stage_loaded1 shared_loaded0 shared_loaded1 shared_loaded2 x_loaded0 x_loaded1 ident_ready zeros_ready pool_const
    tanh_done wsplit_hi wsplit_lo tbo_ready ctx_hi ctx_lo wr_hi wr_ready kps_ready k_hi k_lo k_stored vps_ready v_ready
    mv_ready rstd_pre rstd_ready xn_ready xb_ready xT_ready xh_ready xl_ready q_ready qh_ready ql_ready
    qst_loaded kst_loaded kbd_loaded vst_ready m_ready m_done mT_ready mtr_ready
    scores_ready exp_done pv_done recip_done attn_done ah_ready al_ready oproj_ready x1_ready mv2_ready rstd2_pre rstd2_ready
    z_ready z_stored zT_ready hh_ready hf_ready hl_ready lg_ready lgs_ready lgT_ready lg_done
    a_ready b_ready sil_done gmul_done gh_ready gl_ready acc_ready acc_done out_stored0 out_stored1
    dve_s1 dve_s2 route_step r_onehots r_counts slots_ready rexp_done r_const tab_done oh_row oh_val oh_used
    gather_idx gathered scattered ye_free
    xeT_ready xe_hi xe_f xe_lo sidx_ready gw_ready""".split()
    sig = {n: sem(n) for n in names}
    stage_loaded = [sig["stage_loaded0"], sig["stage_loaded1"]]
    shared_loaded = [sig[f"shared_loaded{j}"] for j in range(3)]
    x_loaded = [sig["x_loaded0"], sig["x_loaded1"]]
    out_stored = [sig["out_stored0"], sig["out_stored1"]]

    x_rows = a["x"].rearrange("b s d -> (b s) d").rearrange("(n t p) d -> n p t d", t=TT, p=P)
    z_rows = zscr.rearrange("(n t p) d -> n p t d", t=TT, p=P)
    out2 = out.rearrange("b s d -> (b s) d")
    out_rows = out2.rearrange("(n t p) d -> n p t d", t=TT, p=P)
    w1v = a["L0_ffn_W1"].rearrange("e (k p) f -> e p k f", p=P)
    w3v = a["L0_ffn_W3"].rearrange("e (k p) f -> e p k f", p=P)
    w2v = a["L0_ffn_W2"].rearrange("e (k p) d -> e p k d", p=P)
    wv = [w1v, w3v, w2v]
    wsv = [a["L0_ffn_W1s"].rearrange("(k p) f -> p k f", p=P),
           a["L0_ffn_W3s"].rearrange("(k p) f -> p k f", p=P),
           a["L0_ffn_W2s"].rearrange("(k p) d -> p k d", p=P)]

    def matrix(e, m):
        buf = (e.c + m) % 2
        order = [(0, 0), (0, 2), (1, 1)] if buf == 0 else [(0, 1), (1, 0), (1, 2)]
        before = 64 if buf == 0 else 0
        return buf, (e.i * 3 + order.index((e.c, m)) + 1) * 16 + before

    def apart(eng):
        eng.sem_inc(sig["passed"], 1)

    block = ctx.enter_context(nc.Block())

    @block.sync
    def _(sp):
        n_const = 0

        def const(dst, src, small=False):
            nonlocal n_const
            n_const += 1
            sp.dma_start(dst, src, allow_slow_non_contiguous=small).then_inc(sig["consts_loaded"], 16)

        sp.sem_inc(out_stored[1], 16)
        for c in range(2):
            sp.dma_start(xb[c], x_rows[c]).then_inc(x_loaded[c], 16)
        for j, w in enumerate(("WqT", "WkT", "WvT", "WoT")):
            sp.dma_start(watt_stage[:, j], a[w].rearrange("(k p) d -> p k d", p=P)).then_inc(stage_loaded[0], 16)
        for k in range(KD):
            const(ctx_f[:, k], a["ctxT"].rearrange("b (k p) t -> k p b t", p=P)[k])
        const(bq[:, :], a["L0_xattn_b_q"].rearrange("(k p) -> p k", p=P), small=True)
        const(bk[:, :], a["L0_xattn_b_k"].rearrange("(k p) -> p k", p=P), small=True)
        const(lng[:, :], a["L0_ffn_ln_g"].rearrange("(k p) -> p k", p=P), small=True)
        const(lnb[:, :], a["L0_ffn_ln_b"].rearrange("(k p) -> p k", p=P), small=True)
        const(wrf[:, :, :], a["L0_ffn_Wr"].rearrange("(k p) e -> p k e", p=P))
        const(bvb[:, :], a["L0_xattn_b_v"].partition_broadcast(SK))
        const(tbo[:, :], a["L0_xattn_b_o"].partition_broadcast(P))
        const(gx[:, :], a["g_xattn"].partition_broadcast(P))
        const(gy[:, :], a["g_ffn"].partition_broadcast(P))
        assert n_const == NCONST
        sp.wait_ge(sig["k_lo"], KD)
        for j in range(2):
            sp.dma_start(kscr[j].rearrange("(k p) t -> p k t", p=P), k_s[:, j].bitcast(F32)).then_inc(sig["k_stored"], 16)
        sp.wait_ge(sig["k_stored"], 32)

        def load_shared(h):
            if h >= 3:
                sp.wait_ge(sig["wsplit_lo"], NSTEP0 + 2 * (h - 2))
            m, part = h // 2, h % 2
            kk = wsv[m].shape[1] // 2
            sp.dma_start(sh_stage[h % 3].rearrange("p (k f) -> p k f", k=kk), wsv[m][:, part * kk:(part + 1) * kk])\
              .then_inc(shared_loaded[h % 3], 16)

        for h in range(3):
            load_shared(h)

        def split_shared(k):
            if 1 <= k <= 3:
                load_shared(k + 2)

        def load_keys(b):
            if b.c == 0:
                bt = b.i
                sp.wait_ge(sig["zeros_ready"], 1)
                sp.wait_ge(sig["m_done"], b.n * TT)
                kd = kscr.rearrange("s (g j d) (b t) -> s j d g b t", g=KD, j=8, b=B)
                for j in range(8):
                    sp.dma_start(kbd[16 * j:16 * j + 16, :, j, :].bitcast(F32), kd[0, j, :, :, bt, :]).then_inc(sig["kbd_loaded"], 16)
                sp.wait_ge(sig["scores_ready"], b.n * NPAIR)
                ks = kscr.rearrange("s (r w d) (b t) -> s w d r b t", w=2, d=DH, b=B)
                for base, part in ((0, 0), (32, 0), (64, 1)):
                    for w in range(2):
                        sp.dma_start(kst[base + 16 * w:base + 16 * w + 16, :, w, :].bitcast(F32), ks[part, w, :, :, bt, :])\
                          .then_inc(sig["kst_loaded"], 16)

        def stack_queries(b):
            sp.wait_ge(sig["qh_ready"], (b.n + 1) * KD)
            for r in range(4):
                for base in (0, 64):
                    sp.dma_start(qst[base:base + 32, r::4, :].bitcast(F32), qT[32 * r:32 * r + 32, 0].bitcast(F32)).then_inc(sig["qst_loaded"], 16)
            sp.wait_ge(sig["ql_ready"], (b.n + 1) * KD)
            for r in range(4):
                sp.dma_start(qst[32:64, r::4, :].bitcast(F32), qT[32 * r:32 * r + 32, 1].bitcast(F32)).then_inc(sig["qst_loaded"], 16)

        def stack_maxima(b):
            sp.wait_ge(sig["mtr_ready"], b.n + 1)
            for r in range(NPAIR):
                sp.dma_start(qst[96:112, r, :].bitcast(F32), mtr[:, :].bitcast(F32)).then_inc(sig["qst_loaded"], 16)

        def store_z(b):
            sp.wait_ge(sig["z_ready"], (b.n + 1) * TT)
            sp.dma_start(z_rows[b.n], zb).then_inc(sig["z_stored"], 16)
            if not (b.at(NB - 2) or b.at(NB - 1)):
                sp.dma_start(xb[b.c], x_rows[b.n + 2]).then_inc(x_loaded[b.c], 16)

        def store_out(b):
            sp.wait_ge(sig["acc_done"], (b.n + 1) * TT)
            sp.dma_start(out_rows[b.n], x1[b.c]).then_inc(out_stored[b.c], 16)

        def load_weights(e):
            for j in range(3):
                sp.wait_ge(sig["wsplit_lo"], (e.n * 3 + 3 + j) * NSTEP0)
                buf, _ = matrix(e, j)
                sp.dma_start(stage[buf].rearrange("p (k f) -> p k f", k=wv[j].shape[2]), wv[j][e.n])\
                  .then_inc(stage_loaded[buf], 16)

        def expert(e):
            if not e.at(E - 1):
                load_weights(e.next())

        def first_weights():
            load_weights(Turn(0, 0))

        token_blocks(sp, {"norm": load_keys, "queries": stack_queries, "maxima_T": stack_maxima, "norm2": store_z,
                          "split_shared": split_shared, "choose": first_weights, "shared_out": store_out})
        with_experts(sp, expert)
        for c in range(2):
            sp.wait_ge(out_stored[c], 16 * NB // 2 + 16 * c)
        sp.wait_ge(sig["scattered"], 16 * NR * E)

    @block.gpsimd
    def _(pool):
        st = Steps(pool, sig["pool_const"], 0)

        def do(ins):
            st.did(ins)
            st.wait()

        pool.sem_inc(sig["ye_free"], 1)
        do(pool.memset(ident[:, :], 0.0))
        pool.affine_select(out=ident[:, :], in_=ident[:, :], compare_op=ALU.not_equal, fill=1.0, base=0,
                           pattern=[[-1, P]], channel_multiplier=1).then_inc(sig["ident_ready"], 1)
        do(pool.memset(kbd.bitcast(F32), 0.0))
        do(pool.memset(kst.bitcast(F32), 0.0))
        kneg = kst[96:112].rearrange("p a b t -> p (a b) t")
        do(pool.affine_select(out=kneg, in_=kneg.bitcast(F32), compare_op=ALU.not_equal, fill=-1.0, base=0,
                              pattern=[[-1, H], [0, SK]], channel_multiplier=1))
        do(pool.memset(qst.bitcast(F32), 0.0))
        do(pool.memset(nhalf[:, :], -0.5))
        do(pool.memset(mones[:, :], 1.0))
        do(pool.affine_select(out=lower[:, :], in_=mones[:, :], compare_op=ALU.is_gt, fill=0.0, base=0,
                              pattern=[[1, P]], channel_multiplier=-1))
        do(pool.memset(vst[0:SK], 0.0))
        for par in range(2):
            for j in range(4):
                do(pool.memset(vst[0:SK, :, par, j, den_at(par, j):den_at(par, j) + DH], 1.0))
        pool.memset(passed[:, :], 0.0).then_inc(sig["zeros_ready"], 1)
        pool.wait_ge(sig["v_ready"], B)

        def norm(b):
            pool.wait_ge(sig["rstd_ready"], b.n)
            pool.wait_ge(sig["mv_ready"], b.n + 1)
            apart(pool)
            pool.tensor_scalar(vs[0][:, :], mv[0][:, :, 1], EPS, None, ALU.add).then_inc(sig["rstd_pre"], 1)
            pool.wait_ge(sig["rstd_pre"], b.n + 1)
            pool.tensor_tensor(rstd[0][:, :], vs[0][:, :], nhalf[:, :], ALU.pow).then_inc(sig["rstd_ready"], 1)
            pool.wait_ge(sig["xn_ready"], (b.n + 1) * TT)
            pool.wait_ge(sig["tbo_ready"], 1)
            for t in range(TT):
                pool.tensor_tensor(xb[b.c][:, t], xb[b.c][:, t], tbo[:, :], ALU.add).then_inc(sig["xb_ready"], 1)

        def attention_lo(b):
            for k in range(KD):
                pool.wait_ge(sig["ah_ready"], b.n * KD + k + 1)
                pool.tensor_tensor(aT[:, 1, k], att[:, k], aT[:, 0, k].bitcast(F32), ALU.subtract)\
                    .then_inc(sig["al_ready"], 1)

        def stationary_values(b):
            if b.c == 0:
                pool.wait_ge(sig["pv_done"], b.n * NPAIR)
                for par in range(2):
                    for j in range(4):
                        src = vall[0:SK, b.i, :].rearrange("t (g w j d) -> t g w j d", g=2, w=2, j=4)[:, :, par, j, :]
                        pool.tensor_copy(vst[0:SK, :, par, j, val_at(par, j):val_at(par, j) + DH], src)\
                            .then_inc(sig["vst_ready"], 1)
                        pool.wait_ge(sig["vst_ready"], b.i * 8 + par * 4 + j + 1)

        def norm2(b):
            pool.wait_ge(sig["rstd2_ready"], b.n)
            pool.wait_ge(sig["mv2_ready"], b.n + 1)
            apart(pool)
            pool.tensor_scalar(vs[1][:, :], mv[1][:, :, 1], 1.0 + EPS, EPS * EPS, ALU.mult, ALU.add)\
                .then_inc(sig["rstd2_pre"], 1)
            pool.wait_ge(sig["rstd2_pre"], b.n + 1)
            pool.tensor_tensor(rstd[1][:, :], vs[1][:, :], nhalf[:, :], ALU.pow).then_inc(sig["rstd2_ready"], 1)

        def route_const():
            pool.wait_ge(sig["lg_done"], NB)
            pool.wait_ge(sig["z_stored"], 16 * NB)
            pool.iota(r_em8, pattern=[[0, NTT], [1, E]], base=-8, channel_multiplier=0,
                      allow_small_or_imprecise_dtypes=True).then_inc(sig["r_const"], 1)
            pool.iota(r_tok, pattern=[[P, NTT]], base=1, channel_multiplier=1,
                      allow_small_or_imprecise_dtypes=True).then_inc(sig["r_const"], 1)
            pool.iota(r_iota, pattern=[[1, P]], base=0, channel_multiplier=0,
                      allow_small_or_imprecise_dtypes=True).then_inc(sig["r_const"], 1)
            pool.memset(r_ones, 1.0).then_inc(sig["r_const"], 1)
            for n in range(NPIECE):
                m, j = n // 4, n % 4
                cols = slice(j * PIECE, (j + 1) * PIECE)
                pool.wait_ge(sig["wsplit_hi"], 4 * NSTEP0 + n + 1)
                pool.tensor_tensor(W1_[:, 1, m, cols], stage[matrix(Turn(0, 0), m)[0]][:, cols],
                                   W1_[:, 0, m, cols].bitcast(F32), ALU.subtract).then_inc(sig["wsplit_lo"], 1)

        def onehot_values():
            pool.wait_ge(sig["slots_ready"], 1)
            gall = r_g.rearrange("p c t -> p (c t)")
            for n in range(2 * NTT):
                if n >= OHB:
                    pool.wait_ge(sig["oh_used"], n - OHB + 1)
                pool.tensor_scalar(r_val[:, n % OHB, 0], r_iota[:, 0:NSL], r_hi[:, n:n + 1],
                                   r_tok[:, n % NTT:n % NTT + 1], ALU.is_equal, ALU.mult).then_inc(sig["oh_val"], 1)
                pool.tensor_scalar(r_val[:, n % OHB, 1], r_iota[:, 0:NSL], r_hi[:, n:n + 1],
                                   gall[:, n:n + 1], ALU.is_equal, ALU.mult).then_inc(sig["oh_val"], 1)

        token_blocks(pool, {"norm": norm, "scores": attention_lo, "transpose_x": stationary_values, "norm2": norm2,
                            "choose": route_const, "table": onehot_values})

        def gather(n):
            pool.wait_ge(sig["gather_idx"], n)
            apart(pool)
            for t in range(NR):
                pool.indirect_dma_start(xg[0:RT, t, :], None, zscr,
                                        bass.IndirectOffsetOnAxis(ap=gidx[0:RT, t:t + 1].bitcast(U32), axis=0))\
                    .then_inc(sig["gathered"], 16)

        pool.wait_ge(sig["z_stored"], 16 * NB)
        gather(1)
        for c in range(2):
            pool.wait_ge(out_stored[c], 16 * NB // 2 + 16 * c)

        def expert(e):
            if not e.at(E - 1):
                pool.wait_ge(sig["xeT_ready"], (e.n + 1) * 2 * KD)
                gather(e.n + 2)
            for half in range(2):
                pool.wait_ge(sig["acc_done"], T // P + (e.n * 2 + half + 1) * (NR // 2))
                apart(pool)
                for t in range(half * NR // 2, (half + 1) * NR // 2):
                    pool.indirect_dma_start(out2, bass.IndirectOffsetOnAxis(ap=sidx[e.c][0:RT, t:t + 1].bitcast(U32), axis=0),
                                            ye[0:RT, t, :], None, bounds_check=T - 1, oob_is_err=False,
                                            compute_op=ALU.add).then_inc(sig["scattered"], 16)
            pool.wait_ge(sig["scattered"], (e.n + 1) * NR * 16)
            pool.sem_inc(sig["ye_free"], 1)

        with_experts(pool, expert)

    @block.scalar
    def _(act):
        act.wait_ge(sig["consts_loaded"], 16 * NCONST)
        act.activation(tgx[:, :], gx[:, :], ACT.Tanh).then_inc(sig["tanh_done"], 1)
        act.activation(tgf[:, :], gy[:, :], ACT.Tanh).then_inc(sig["tanh_done"], 1)
        act.copy(ctx_s[:, 0], ctx_f.rearrange("p k b t -> p k (b t)")).then_inc(sig["ctx_hi"], 1)
        act.copy(wrs[:, :, 0:E], wrf[:, :, :]).then_inc(sig["wr_hi"], 1)

        def split_hi(dst_hi, m, piece, src):
            act.copy(dst_hi, src).then_inc(sig["wsplit_hi"], 1)

        act.wait_ge(stage_loaded[0], 64)
        for j in range(NSTEP0):
            split_hi(wat[:, 0, j], 0, j, watt_stage[:, j])
        for k in range(KD):
            act.wait_ge(sig["kps_ready"], k + 1)
            act.activation(k_s[:, 0, k], bank[k][:, 0:B * SK], ACT.Identity, bias=bk[:, k:k + 1])\
               .then_inc(sig["k_hi"], 1)

        def split_shared(k):
            for n in range(2 * k, min(2 * k + 2, NPIECE)):
                m, j, h = n // 4, n % 4, n // 2
                if n % 2 == 0:
                    act.wait_ge(shared_loaded[h % 3], 16 * (h // 3 + 1))
                split_hi(W0[:, 0, m, j * PIECE:(j + 1) * PIECE], m, j,
                         sh_stage[h % 3][:, n % 2 * PIECE:(n % 2 + 1) * PIECE])

        def transpose_x(b):
            for k in range(KD):
                act.wait_ge(sig["xT_ready"], b.n * KD + k + 1)
                act.copy(xT[:, 0, k], bank[6 + k][:, :]).then_inc(sig["xh_ready"], 1)

        def queries(b):
            for k in range(KD):
                act.wait_ge(sig["q_ready"], b.n * KD + k + 1)
                act.activation(qT[:, 0, k], bank[4 + k][:, :], ACT.Identity, bias=bq[:, k:k + 1])\
                   .then_inc(sig["qh_ready"], 1)

        def maxima_T(b):
            act.wait_ge(sig["mT_ready"], b.n + 1)
            act.copy(mtr[:, :], bank[3][0:H, :]).then_inc(sig["mtr_ready"], 1)

        def scores(b):
            def attn_hi(k):
                act.wait_ge(sig["attn_done"], b.n * NG + 2 * k + 2)
                act.copy(aT[:, 0, k], att[:, k]).then_inc(sig["ah_ready"], 1)
            for p in range(NPAIR):
                act.wait_ge(sig["scores_ready"], b.n * NPAIR + p + 1)
                if p >= 2:
                    act.wait_ge(sig["pv_done"], b.n * NPAIR + p - 1)
                for w in range(2):
                    last = act.activation(prob[p % 2][0:SK, w], bank[2 * (p % 2) + w][0:SK, :], ACT.Exp,
                                          scale=DH ** -0.5)
                last.then_inc(sig["exp_done"], 1)
                if p == NPAIR - 1:
                    attn_hi(0)

        def project(b):
            act.wait_ge(sig["attn_done"], (b.n + 1) * NG)
            act.copy(aT[:, 0, 1], att[:, 1]).then_inc(sig["ah_ready"], 1)

        def transpose_z(b):
            for k in range(KD):
                act.wait_ge(sig["zT_ready"], b.n * KD + k + 1)
                act.activation(hTs[b.c][:, 0, k], bank[3 + k][:, :], ACT.Identity, bias=lnb[:, k:k + 1],
                               scale=lng[:, k:k + 1]).then_inc(sig["hh_ready"], 1)

        def logits(b):
            act.wait_ge(sig["lg_ready"], b.n + 1)
            act.copy(lgs[:, :], bank[5][0:2 * E, :]).then_inc(sig["lgs_ready"], 1)

        def hidden_hi(b, f):
            act.wait_ge(sig["gmul_done"], b.n * NF + f + 1)
            act.copy(gT[:, 0, f % RING], gf[:, f % 2]).then_inc(sig["gh_ready"], 1)

        def up(b, f):
            act.wait_ge(sig["a_ready"], b.n * NF + f + 1)
            if f >= 2:
                act.wait_ge(sig["gmul_done"], b.n * NF + f - 1)
            act.activation(sil[f % 2], bank[2 * f % 3][:, :], ACT.Silu).then_inc(sig["sil_done"], 1)
            if f >= 1:
                hidden_hi(b, f - 1)

        def last_hidden(b):
            hidden_hi(b, NF - 1)

        def gate_exp():
            act.wait_ge(sig["r_onehots"], 1)
            act.activation(r_e2, r_d, ACT.Exp).then_inc(sig["rexp_done"], 1)

        def split_piece(e, n):
            m, j = n // 4, n % 4
            buf, loaded = matrix(e, m)
            if j == 0:
                act.wait_ge(stage_loaded[buf], loaded)
            dst = (W1_ if e.c == 0 else W0)[:, 0, m, j * PIECE:(j + 1) * PIECE]
            act.copy(dst, stage[buf][:, j * PIECE:(j + 1) * PIECE]).then_inc(sig["wsplit_hi"], 1)

        def xe_hi(e, g):
            k, half = g % KD, g // KD
            act.wait_ge(sig["xeT_ready"], e.n * 4 + g + 1)
            act.activation(xe[e.c][:, 0, k, half * HALF:(half + 1) * HALF], bank[7][:, 0:HALF], ACT.Identity,
                           bias=lnb[:, k:k + 1], scale=lng[:, k:k + 1]).then_inc(sig["xe_hi"], 1)

        def first_pieces(k):
            for n in range(3 * k, min(3 * k + 3, NPIECE)):
                split_piece(Turn(0, 0), n)

        token_blocks(act, {"scores": scores, "project": project, "transpose_x": transpose_x, "queries": queries,
                           "maxima_T": maxima_T, "transpose_z": transpose_z, "logits": logits, "up": up,
                           "last_hidden": last_hidden, "split_shared": split_shared, "choose": gate_exp,
                           "place": first_pieces})
        for g in range(4):
            xe_hi(Turn(0, 0), g)

        def expert(e):
            base = NB * NF + e.n * 2 * NF
            for n in range(2 * NF + 1):
                if n < 2 * NF:
                    act.wait_ge(sig["a_ready"], base + n + 1)
                    if n >= 2:
                        act.wait_ge(sig["gmul_done"], base + n - 1)
                    act.activation(sil[n % 2][:, 0:HALF], bank[2 * (n % 2)][:, 0:HALF], ACT.Silu)\
                       .then_inc(sig["sil_done"], 1)
                if n >= 1:
                    act.wait_ge(sig["gmul_done"], base + n)
                    act.copy(gT[:, 0, (n - 1) % RING, 0:HALF], gf[:, (n - 1) % 2, 0:HALF]).then_inc(sig["gh_ready"], 1)
                if not e.at(E - 1) and n < NPIECE:
                    split_piece(e.next(), n)
                if not e.at(E - 1) and n in XT_AT:
                    xe_hi(e.next(), XT_AT.index(n))

        with_experts(act, expert)

    @block.vector
    def _(dve):
        dve.wait_ge(sig["tanh_done"], 2)
        dve.tensor_scalar(tbo[:, :], tbo[:, :], tgx[:, 0:1], None, ALU.mult).then_inc(sig["tbo_ready"], 1)
        dve.wait_ge(sig["ctx_hi"], 1)
        dve.tensor_tensor(ctx_s[:, 1], ctx_f.rearrange("p k b t -> p k (b t)"), ctx_s[:, 0].bitcast(F32),
                          ALU.subtract).then_inc(sig["ctx_lo"], 1)
        dve.wait_ge(sig["wr_hi"], 1)
        dve.tensor_tensor(wrs[:, :, E:2 * E], wrf[:, :, :], wrs[:, :, 0:E].bitcast(F32), ALU.subtract)\
           .then_inc(sig["wr_ready"], 1)
        for j in range(NSTEP0):
            dve.wait_ge(sig["wsplit_hi"], j + 1)
            dve.tensor_tensor(wat[:, 1, j], watt_stage[:, j], wat[:, 0, j].bitcast(F32), ALU.subtract)\
               .then_inc(sig["wsplit_lo"], 1)
        for k in range(KD):
            dve.wait_ge(sig["k_hi"], k + 1)
            dve.scalar_tensor_tensor(out=k_s[:, 1, k], in0=bank[k][:, 0:B * SK], scalar=bk[:, k:k + 1],
                                     in1=k_s[:, 0, k].bitcast(F32), op0=ALU.add, op1=ALU.subtract)\
               .then_inc(sig["k_lo"], 1)
        for b in range(B):
            dve.wait_ge(sig["vps_ready"], b + 1)
            dve.tensor_tensor(vall[0:SK, b], bank[2 + b % 2][0:SK, 0:D], bvb[:, :], ALU.add)\
               .then_inc(sig["v_ready"], 1)

        def split_shared(k):
            for n in range(2 * k, min(2 * k + 2, NPIECE)):
                m, j, h = n // 4, n % 4, n // 2
                cols = slice(j * PIECE, (j + 1) * PIECE)
                dve.wait_ge(sig["wsplit_hi"], NSTEP0 + n + 1)
                dve.tensor_tensor(W0[:, 1, m, cols], sh_stage[h % 3][:, n % 2 * PIECE:(n % 2 + 1) * PIECE],
                                  W0[:, 0, m, cols].bitcast(F32), ALU.subtract).then_inc(sig["wsplit_lo"], 1)

        def norm_stats(st, which, src, ready):
            for t in range(TT):
                st.did(dve.bn_stats(stt[which][:, t], src[:, t]))
            st.wait()
            apart(dve)
            for t in range(TT):
                last = dve.bn_aggr(mv[which][:, t], stt[which][:, t])
                if t < TT - 1:
                    st.did(last)
            last.then_inc(ready, 1)

        def norm(b):
            st = Steps(dve, sig["dve_s1"], b.n * 7)
            dve.wait_ge(x_loaded[b.c], (b.i + 1) * 16)
            dve.wait_ge(sig["xn_ready"], b.n * TT)
            norm_stats(st, 0, xb[b.c], sig["mv_ready"])
            assert st.k == 7
            dve.wait_ge(sig["rstd_ready"], b.n + 1)
            dve.wait_ge(sig["mv_ready"], b.n + 1)
            st.wait()
            for t in range(TT):
                dve.tensor_scalar(xn[:, t], xb[b.c][:, t], mv[0][:, t, 0:1], rstd[0][:, t:t + 1], ALU.subtract, ALU.mult)\
                   .then_inc(sig["xn_ready"], 1)

        def transpose_x(b):
            for k in range(KD):
                dve.wait_ge(sig["xh_ready"], b.n * KD + k + 1)
                dve.tensor_tensor(xT[:, 1, k], bank[6 + k][:, :], xT[:, 0, k].bitcast(F32), ALU.subtract)\
                   .then_inc(sig["xl_ready"], 1)

        def queries(b):
            for k in range(KD):
                dve.wait_ge(sig["qh_ready"], b.n * KD + k + 1)
                dve.scalar_tensor_tensor(out=qT[:, 1, k], in0=bank[4 + k][:, :], scalar=bq[:, k:k + 1],
                                         in1=qT[:, 0, k].bitcast(F32), op0=ALU.add, op1=ALU.subtract)\
                   .then_inc(sig["ql_ready"], 1)

        def maxima(b, t):
            dve.wait_ge(sig["m_ready"], b.n * TT + t + 1)
            for j, (h0, h1) in enumerate(MAX_HEADS):
                last = dve.tensor_reduce(mx[:, t, h0:h1],
                                         bank[3 + j][:, 0:(h1 - h0) * SK].rearrange("p (h t) -> p h t", t=SK), AX.X, ALU.max)
            last.then_inc(sig["m_done"], 1)

        def scores(b):
            dve.wait_ge(sig["z_stored"], b.n * 16)
            for g in range(NG):
                dve.wait_ge(sig["pv_done"], b.n * NPAIR + 2 * g + 2)
                dve.wait_ge(sig["hl_ready"], b.n * KD)
                dve.wait_ge(sig["attn_done"], b.n * NG + g)
                va, dn = (slice(0, 64), slice(64, 128)) if g % 2 == 0 else (slice(64, 128), slice(0, 64))
                dve.reciprocal(rc[va, :], bank[4 + g % 2][dn, :]).then_inc(sig["recip_done"], 1)
                dve.wait_ge(sig["recip_done"], b.n * NG + g + 1)
                dve.tensor_tensor(att[va, g // 2], bank[4 + g % 2][va, :], rc[va, :], ALU.mult)\
                   .then_inc(sig["attn_done"], 1)

        def project(b):
            st = Steps(dve, sig["dve_s2"], b.n * 7)
            dve.wait_ge(sig["xb_ready"], (b.n + 1) * TT)
            dve.wait_ge(out_stored[b.c], b.i * 16 + 16 * b.c)
            for t in range(TT):
                dve.wait_ge(sig["oproj_ready"], b.n * TT + t + 1)
                dve.scalar_tensor_tensor(out=x1[b.c][:, t], in0=bank[3 + t % 3][:, 0:D], scalar=tgx[:, 0:1],
                                         in1=xb[b.c][:, t], op0=ALU.mult, op1=ALU.add).then_inc(sig["x1_ready"], 1)
            dve.wait_ge(sig["x1_ready"], (b.n + 1) * TT)
            dve.wait_ge(sig["z_ready"], b.n * TT)
            norm_stats(st, 1, x1[b.c], sig["mv2_ready"])
            assert st.k == 7

        def norm2(b):
            dve.wait_ge(sig["rstd2_ready"], b.n + 1)
            dve.wait_ge(sig["mv2_ready"], b.n + 1)
            dve.wait_ge(sig["dve_s2"], (b.n + 1) * 7)
            for t in range(TT):
                dve.tensor_scalar(zb[:, t], x1[b.c][:, t], mv[1][:, t, 0:1], rstd[1][:, t:t + 1], ALU.subtract, ALU.mult)\
                   .then_inc(sig["z_ready"], 1)

        def transpose_z(b):
            for k in range(KD):
                dve.wait_ge(sig["hl_ready"], b.n * KD + k)
                dve.wait_ge(sig["hh_ready"], b.n * KD + k + 1)
                dve.tensor_scalar(hf[:, :], bank[3 + k][:, :], lng[:, k:k + 1], lnb[:, k:k + 1], ALU.mult, ALU.add)\
                   .then_inc(sig["hf_ready"], 1)
                dve.wait_ge(sig["hf_ready"], b.n * KD + k + 1)
                dve.tensor_tensor(hTs[b.c][:, 1, k], hf[:, :], hTs[b.c][:, 0, k].bitcast(F32), ALU.subtract)\
                   .then_inc(sig["hl_ready"], 1)

        def logits_T(b):
            dve.wait_ge(sig["lgT_ready"], b.n + 1)
            dve.tensor_copy(lgall[:, bass.ds(b.n * TT, TT), :],
                            bank[3][:, 0:64].rearrange("p (t e) -> p t e", t=TT)[:, :, 0:2 * E]).then_inc(sig["lg_done"], 1)

        def hidden_lo(b, f):
            dve.wait_ge(sig["gh_ready"], b.n * NF + f + 1)
            dve.tensor_tensor(gT[:, 1, f % RING], gf[:, f % 2], gT[:, 0, f % RING].bitcast(F32), ALU.subtract)\
               .then_inc(sig["gl_ready"], 1)

        def up(b, f):
            dve.wait_ge(sig["b_ready"], b.n * NF + f + 1)
            dve.wait_ge(sig["sil_done"], b.n * NF + f + 1)
            if f >= 2:
                dve.wait_ge(sig["gl_ready"], b.n * NF + f - 1)
            dve.tensor_tensor(gf[:, f % 2], bank[(2 * f + 1) % 3][:, :], sil[f % 2], ALU.mult)\
               .then_inc(sig["gmul_done"], 1)
            if f >= 1:
                hidden_lo(b, f - 1)

        def last_hidden(b):
            hidden_lo(b, NF - 1)

        def shared_out(b):
            for t in range(TT):
                dve.wait_ge(sig["acc_ready"], b.n * TT + t // 2 * 2 + 2)
                dve.scalar_tensor_tensor(out=x1[b.c][:, t], in0=bank[6 + t // 2][:, t % 2 * D:t % 2 * D + D],
                                         scalar=tgf[:, 0:1], in1=x1[b.c][:, t], op0=ALU.mult, op1=ALU.add)\
                   .then_inc(sig["acc_done"], 1)

        rst = Steps(dve, sig["route_step"], 0)

        def do(ins):
            rst.did(ins)
            rst.wait()

        def choose():
            dve.wait_ge(sig["lg_done"], NB)
            dve.wait_ge(sig["r_const"], 4)
            fl = lambda v: v.rearrange("p t e -> p (t e)")
            bc = lambda v: v.unsqueeze(2).broadcast_to([P, NTT, E])
            do(dve.tensor_tensor(r_lg, lgall[:, :, 0:E], lgall[:, :, E:2 * E], ALU.add))
            for ch in range(2):
                do(dve.tensor_reduce(r_m[:, ch], r_lg, AX.X, ALU.max))
                do(dve.tensor_tensor(r_tmp, r_lg, bc(r_m[:, ch]), ALU.is_equal))
                do(dve.tensor_tensor(r_tmp, r_tmp, r_em8, ALU.mult))
                do(dve.tensor_reduce(r_i[:, ch], r_tmp, AX.X, ALU.min))
                do(dve.tensor_tensor(r_oh[:, ch], r_em8, bc(r_i[:, ch]), ALU.is_equal))
                if ch == 0:
                    do(dve.scalar_tensor_tensor(out=fl(r_lg), in0=fl(r_oh[:, 0]), scalar=-3e38, in1=fl(r_lg),
                                                op0=ALU.mult, op1=ALU.add))
            dve.tensor_tensor(r_d, r_m[:, 1], r_m[:, 0], ALU.subtract).then_inc(sig["r_onehots"], 1)

        def count():
            dve.wait_ge(sig["rexp_done"], 1)
            do(dve.tensor_scalar(r_d, r_e2, 1.0, None, ALU.add))
            do(dve.reciprocal(r_g[:, 0], r_d))
            do(dve.tensor_scalar(r_g[:, 0], r_g[:, 0], tgf[:, 0:1], None, ALU.mult))
            do(dve.tensor_tensor(r_g[:, 1], r_g[:, 0], r_e2, ALU.mult))
            dve.wait_ge(sig["r_counts"], 2)
            do(dve.tensor_copy(r_tot, bank[4][:, 0:2 * NTT * E].rearrange("p (t e) -> p t e", e=E)))

        def add_counts():
            for e in range(E):
                rst.did(dve.tensor_tensor_scan(r_inc[:, :, e], r_ones, r_tot[:, :, e], 0.0, ALU.mult, ALU.add))
            rst.wait()
            do(dve.tensor_tensor(r_inc, r_inc, r_tot, ALU.subtract))
            do(dve.tensor_tensor(r_inc, bank[3][:, 0:2 * NTT * E].rearrange("p (t e) -> p t e", e=E), r_inc, ALU.add))
            do(dve.tensor_tensor(r_inc, r_inc, r_oh.rearrange("p c t e -> p (c t) e"), ALU.mult))
            do(dve.tensor_reduce(r_pos, r_inc, AX.X, ALU.add))

        def slots():
            do(dve.tensor_scalar(r_hi, r_i.rearrange("p c t -> p (c t)"), float(NR), 8.0 * NR, ALU.mult, ALU.add))
            do(dve.tensor_copy(r_lo, r_pos))
            for k in range(1, NR + 1):
                do(dve.tensor_scalar(r_ge, r_pos, float(k * RT), None, ALU.is_ge))
                if k < NR:
                    do(dve.tensor_tensor(r_hi, r_hi, r_ge, ALU.add))
                last = dve.scalar_tensor_tensor(out=r_lo, in0=r_ge, scalar=(-float(RT) if k < NR else 1e6), in1=r_lo,
                                                op0=ALU.mult, op1=ALU.add)
                if k < NR:
                    do(last)
            last.then_inc(sig["slots_ready"], 1)
            dve.wait_ge(sig["slots_ready"], 1)

        def onehot_rows(first, last):
            for n in range(first, last):
                if n >= OHB:
                    dve.wait_ge(sig["oh_used"], n - OHB + 1)
                dve.tensor_scalar(r_row[:, n % OHB], r_iota[:, 0:RT], r_lo[:, n:n + 1], None, ALU.is_equal)\
                   .then_inc(sig["oh_row"], 1)

        def place(k):
            if k == 0:
                add_counts()
            elif k == 1:
                slots()
            else:
                onehot_rows(*placed(k))

        def table():
            dve.wait_ge(sig["oh_used"], 2 * NTT)
            tk = r_val[:, 0, 0]
            do(dve.tensor_copy(tabw[0:RT, :], bank[5][0:RT, NSL:2 * NSL]))
            do(dve.tensor_scalar(tk[0:RT], bank[5][0:RT, 0:NSL], -1.0, None, ALU.add))
            do(dve.tensor_scalar(tabg[0:RT, :], tk[0:RT], 0.0, None, ALU.max))
            do(dve.tensor_scalar(r_val[0:RT, 0, 1], tk[0:RT], 0.0, 2.0 * T, ALU.is_lt, ALU.mult))
            dve.tensor_tensor(tabs[0:RT, :], tk[0:RT], r_val[0:RT, 0, 1], ALU.add).then_inc(sig["tab_done"], 1)
            dve.wait_ge(sig["tab_done"], 1)
            dve.tensor_copy(gidx[0:RT, :], tabg[0:RT, 0:NR]).then_inc(sig["gather_idx"], 1)

        token_blocks(dve, {"norm": norm, "scores": scores, "transpose_x": transpose_x, "project": project,
                           "queries": queries, "norm2": norm2, "transpose_z": transpose_z, "logits_T": logits_T,
                           "maxima": maxima, "up": up, "last_hidden": last_hidden, "shared_out": shared_out,
                           "split_shared": split_shared, "choose": choose, "count": count, "place": place,
                           "table": table})

        def index_now(e):
            dve.tensor_copy(sidx[e.c][0:RT, :], tabs[0:RT, bass.ds(e.n * NR, NR)]).then_inc(sig["sidx_ready"], 1)
            dve.tensor_copy(gw[e.c][0:RT, :], tabw[0:RT, bass.ds(e.n * NR, NR)]).then_inc(sig["gw_ready"], 1)

        def split_piece(e, n):
            m, j = n // 4, n % 4
            buf, _ = matrix(e, m)
            dve.wait_ge(sig["wsplit_hi"], e.n * NPIECE + 4 * NSTEP0 + n + 1)
            w = W1_ if e.c == 0 else W0
            cols = slice(j * PIECE, (j + 1) * PIECE)
            dve.tensor_tensor(w[:, 1, m, cols], stage[buf][:, cols], w[:, 0, m, cols].bitcast(F32), ALU.subtract)\
               .then_inc(sig["wsplit_lo"], 1)

        def xe_lo(e, g):
            k, half = g % KD, g // KD
            cols = slice(half * HALF, (half + 1) * HALF)
            dve.wait_ge(sig["xe_lo"], e.n * 4 + g)
            dve.wait_ge(sig["xe_hi"], e.n * 4 + g + 1)
            dve.tensor_scalar(hf[:, 0:HALF], bank[7][:, 0:HALF], lng[:, k:k + 1], lnb[:, k:k + 1], ALU.mult, ALU.add)\
               .then_inc(sig["xe_f"], 1)
            dve.wait_ge(sig["xe_f"], e.n * 4 + g + 1)
            dve.tensor_tensor(xe[e.c][:, 1, k, cols], hf[:, 0:HALF], xe[e.c][:, 0, k, cols].bitcast(F32), ALU.subtract)\
               .then_inc(sig["xe_lo"], 1)

        for g in range(4):
            xe_lo(Turn(0, 0), g)

        def y_out(e, half):
            if half == 0:
                dve.wait_ge(sig["gw_ready"], e.n + 1)
                dve.wait_ge(sig["ye_free"], e.n + 1)
            for t in range(NR // 2):
                dve.wait_ge(sig["acc_ready"], T // P + (e.n * 2 + half) * (NR // 2) + t + 1)
                r = half * (NR // 2) + t
                dve.tensor_scalar(ye[0:RT, r, :], bank[4 + t][0:RT, 0:D], gw[e.c][0:RT, r:r + 1], None, ALU.mult)\
                   .then_inc(sig["acc_done"], 1)

        def expert(e):
            base = NB * NF + e.n * 2 * NF
            dve.wait_ge(sig["acc_done"], T // P + e.n * NR)
            index_now(e)
            if not e.at(E - 1):
                dve.wait_ge(sig["gathered"], (e.n + 1) * NR * 16)
                dve.tensor_copy(gidx[0:RT, :], tabg[0:RT, bass.ds((e.n + 1) * NR, NR)]).then_inc(sig["gather_idx"], 1)
            for n in range(2 * NF + 1):
                if n < 2 * NF:
                    dve.wait_ge(sig["b_ready"], base + n + 1)
                    dve.wait_ge(sig["sil_done"], base + n + 1)
                    dve.wait_ge(sig["gl_ready"], base + max(n - 1, 0))
                    dve.tensor_tensor(gf[:, n % 2, 0:HALF], bank[2 * (n % 2) + 1][:, 0:HALF], sil[n % 2][:, 0:HALF],
                                      ALU.mult).then_inc(sig["gmul_done"], 1)
                if n >= 1:
                    dve.wait_ge(sig["gh_ready"], base + n)
                    dve.tensor_tensor(gT[:, 1, (n - 1) % RING, 0:HALF], gf[:, (n - 1) % 2, 0:HALF],
                                      gT[:, 0, (n - 1) % RING, 0:HALF].bitcast(F32), ALU.subtract)\
                       .then_inc(sig["gl_ready"], 1)
                if not e.at(E - 1) and n < NPIECE:
                    split_piece(e.next(), n)
                if not e.at(E - 1) and n in XT_AT:
                    xe_lo(e.next(), XT_AT.index(n))
                if n == NF + 1:
                    y_out(e, 0)
            y_out(e, 1)

        with_experts(dve, expert)

    @block.tensor
    def _(pe):
        def three(o, lhs, rhs, first, last):
            pe.matmul(o, lhs[0], rhs[0], start=first, stop=False)
            pe.matmul(o, lhs[0], rhs[1], start=False, stop=False)
            return pe.matmul(o, lhs[1], rhs[0], start=False, stop=last)

        pe.wait_ge(sig["ctx_lo"], 1)
        pe.wait_ge(sig["wsplit_lo"], NSTEP0)
        for m in range(KD):
            for k in range(KD):
                last = three(bank[m][:, 0:B * SK], [wat[:, j, 1, k, m * P:(m + 1) * P] for j in range(2)],
                             [ctx_s[:, j, k] for j in range(2)], k == 0, k == KD - 1)
            last.then_inc(sig["kps_ready"], 1)
        for b in range(B):
            if b >= 2:
                pe.wait_ge(sig["v_ready"], b - 1)
            for k in range(KD):
                last = three(bank[2 + b % 2][0:SK, 0:D], [ctx_s[:, j, k, b * SK:(b + 1) * SK] for j in range(2)],
                             [wat[:, j, 2, k] for j in range(2)], k == 0, k == KD - 1)
            last.then_inc(sig["vps_ready"], 1)
        pe.wait_ge(sig["ident_ready"], 1)
        pe.wait_ge(sig["k_lo"], KD)
        pe.wait_ge(sig["v_ready"], B)

        def transpose_x(b):
            for k in range(KD):
                for t in range(TT):
                    if k == 0:
                        pe.wait_ge(sig["xn_ready"], b.n * TT + t + 1)
                    mm = pe.transpose(bank[6 + k][:, t * P:(t + 1) * P], xn[:, t, k * P:(k + 1) * P], ident[:, :])
                mm.then_inc(sig["xT_ready"], 1)

        def queries(b):
            pe.wait_ge(sig["xl_ready"], (b.n + 1) * KD)
            if not b.at(0):
                pe.wait_ge(sig["x1_ready"], b.n * TT - 1)
            for m in range(KD):
                for k in range(KD):
                    mm = three(bank[4 + m][:, :], [wat[:, j, 0, k, m * P:(m + 1) * P] for j in range(2)],
                               [xT[:, j, k] for j in range(2)], k == 0, k == KD - 1)
                mm.then_inc(sig["q_ready"], 1)

        def maxima(b, t):
            if t == 0:
                pe.wait_ge(sig["ql_ready"], (b.n + 1) * KD)
                if not b.at(0):
                    pe.wait_ge(sig["lg_done"], b.n)
                if b.c == 0:
                    pe.wait_ge(sig["kbd_loaded"], (b.i + 1) * 128)
            else:
                pe.wait_ge(sig["m_done"], b.n * TT + t)
            for j, (h0, h1) in enumerate(MAX_HEADS):
                for k in range(KD):
                    g0, g1 = max(h0, 8 * k), min(h1, 8 * k + 8)
                    if g0 < g1:
                        mm = pe.matmul(bank[3 + j][:, (g0 - h0) * SK:(g1 - h0) * SK], qT[:, 0, k, t * P:(t + 1) * P],
                                       kbd[:, k, g0 - 8 * k:g1 - 8 * k, :], start=True, stop=True)
            mm.then_inc(sig["m_ready"], 1)

        def maxima_T(b):
            pe.wait_ge(sig["m_done"], (b.n + 1) * TT)
            for t in range(TT):
                mm = pe.transpose(bank[3][0:H, t * P:(t + 1) * P], mx[:, t], ident[:, :])
            mm.then_inc(sig["mT_ready"], 1)

        def scores(b):
            def pv(p):
                if p == 0:
                    pe.wait_ge(sig["vst_ready"], (b.i + 1) * 8)
                if p % 2 == 0 and p >= 4:
                    pe.wait_ge(sig["attn_done"], b.n * NG + p // 2 - 1)
                pe.wait_ge(sig["exp_done"], b.n * NPAIR + p + 1)
                for w in range(2):
                    h = 2 * p + w
                    g, j = h // 4, h % 4
                    mm = pe.matmul(bank[4 + g % 2][:, :], vst[0:SK, g // 2, g % 2, j, :], prob[p % 2][0:SK, w],
                                   start=(j == 0), stop=(j == 3))
                mm.then_inc(sig["pv_done"], 1)

            pe.wait_ge(sig["qst_loaded"], (b.n + 1) * 16 * NQST)
            if b.c == 0:
                pe.wait_ge(sig["kst_loaded"], (b.i + 1) * 96)
            for p in range(NPAIR):
                if p >= 2:
                    pe.wait_ge(sig["exp_done"], b.n * NPAIR + p - 1)
                for w in range(2):
                    mm = pe.matmul(bank[2 * (p % 2) + w][0:SK, :], kst[:, p, w, :], qst[:, p, :], start=True, stop=True)
                mm.then_inc(sig["scores_ready"], 1)
                if p >= 1:
                    pv(p - 1)
            pv(NPAIR - 1)

        def project(b):
            pe.wait_ge(sig["al_ready"], (b.n + 1) * KD)
            for t in range(TT):
                if t >= 3:
                    pe.wait_ge(sig["x1_ready"], b.n * TT + t - 2)
                for k in range(KD):
                    mm = three(bank[3 + t % 3][:, 0:D], [aT[:, j, k, t * P:(t + 1) * P] for j in range(2)],
                               [wat[:, j, 3, k] for j in range(2)], k == 0, k == KD - 1)
                mm.then_inc(sig["oproj_ready"], 1)

        def transpose_z(b):
            for k in range(KD):
                for t in range(TT):
                    if k == 0:
                        pe.wait_ge(sig["z_ready"], b.n * TT + t + 1)
                    mm = pe.transpose(bank[3 + k][:, t * P:(t + 1) * P], zb[:, t, k * P:(k + 1) * P], ident[:, :])
                mm.then_inc(sig["zT_ready"], 1)

        def logits(b):
            if b.at(0):
                pe.wait_ge(sig["wr_ready"], 1)
            pe.wait_ge(sig["hl_ready"], (b.n + 1) * KD)
            for k in range(KD):
                for j in range(2):
                    mm = pe.matmul(bank[5][0:2 * E, :], wrs[:, k, :], hTs[b.c][:, j, k], start=(k + j == 0),
                                   stop=(k + j == 2))
            mm.then_inc(sig["lg_ready"], 1)

        def logits_T(b):
            pe.wait_ge(sig["lgs_ready"], b.n + 1)
            apart(pe)
            for t in range(TT):
                mm = pe.transpose(bank[3][:, 16 * t:16 * t + 2 * E], lgs[:, t * P:(t + 1) * P], ident[0:2 * E, 0:2 * E])
            mm.then_inc(sig["lgT_ready"], 1)

        def up(b, f):
            if b.at(0) and f == 0:
                pe.wait_ge(sig["wsplit_lo"], 4 * NSTEP0)
            for w, ready in ((0, sig["a_ready"]), (1, sig["b_ready"])):
                if w == 0 and f >= 2:
                    pe.wait_ge(sig["gmul_done"], b.n * NF + f - 1)
                if w == 1 and f >= 1:
                    pe.wait_ge(sig["sil_done"], b.n * NF + f)
                for k in range(KD):
                    mm = three(bank[(2 * f + w) % 3][:, :],
                               [W0[:, j, w, k * FF + f * P:k * FF + (f + 1) * P] for j in range(2)],
                               [hTs[b.c][:, j, k] for j in range(2)], k == 0, k == KD - 1)
                mm.then_inc(ready, 1)

        def down(b, f):
            pe.wait_ge(sig["gl_ready"], b.n * NF + f + 1)
            for t in range(TT):
                o = bank[6 + t // 2][:, t % 2 * D:t % 2 * D + D]
                lhs = [gT[:, j, f % RING, t * P:(t + 1) * P] for j in range(2)]
                rhs = [W0[:, j, 2, f * D:(f + 1) * D] for j in range(2)]
                pe.matmul(o, lhs[0], rhs[0], start=(f == 0 and t % 2 == 0), stop=False, skip_group_check=True)
                pe.matmul(o, lhs[0], rhs[1], start=False, stop=False, skip_group_check=True)
                mm = pe.matmul(o, lhs[1], rhs[0], start=False, stop=(f == NF - 1), skip_group_check=True)
                if f == NF - 1:
                    mm.then_inc(sig["acc_ready"], 1)

        def count():
            pe.wait_ge(sig["r_onehots"], 1)
            oh = r_oh.rearrange("p c t e -> p (c t e)")
            pe.matmul(bank[3][:, 0:2 * NTT * E], lower[:, :], oh, start=True, stop=True).then_inc(sig["r_counts"], 1)
            pe.matmul(bank[4][:, 0:2 * NTT * E], mones[:, :], oh, start=True, stop=True).then_inc(sig["r_counts"], 1)

        def place(k):
            for n in range(*placed(k)):
                pe.wait_ge(sig["oh_row"], n + 1)
                pe.wait_ge(sig["oh_val"], 2 * n + 2)
                mm = pe.matmul(bank[5][0:RT, 0:2 * NSL], r_row[:, n % OHB], r_val[:, n % OHB].rearrange("p a b -> p (a b)"),
                               start=(n == 0), stop=(n == 2 * NTT - 1))
                mm.then_inc(sig["oh_used"], 1)

        token_blocks(pe, {"transpose_x": transpose_x, "queries": queries, "maxima": maxima, "maxima_T": maxima_T,
                          "scores": scores, "project": project, "transpose_z": transpose_z, "logits": logits,
                          "logits_T": logits_T, "up": up, "down": down, "count": count, "place": place})

        def xpose(e, g):
            k, half = g % KD, g // KD
            pe.wait_ge(sig["gathered"], (e.n + 1) * NR * 16)
            pe.wait_ge(sig["xe_lo"], e.n * 4 + g)
            for t in range(NR // 2):
                mm = pe.transpose(bank[7][:, t * RT:(t + 1) * RT], xg[0:RT, half * (NR // 2) + t, k * P:(k + 1) * P],
                                  ident[0:RT, 0:RT])
            mm.then_inc(sig["xeT_ready"], 1)

        pe.wait_ge(sig["acc_done"], NB * TT)
        for g in range(4):
            xpose(Turn(0, 0), g)

        def expert(e):
            base = NB * NF + e.n * 2 * NF
            w = W1_ if e.c == 0 else W0

            def down(n):
                half, f = n // NF, n % NF
                pe.wait_ge(sig["gl_ready"], base + n + 1)
                if f == 0:
                    pe.wait_ge(sig["acc_done"], T // P + (e.n * 2 + half) * (NR // 2))
                for t in range(NR // 2):
                    mm = three(bank[4 + t][0:RT, 0:D], [gT[:, j, n % RING, t * RT:(t + 1) * RT] for j in range(2)],
                               [w[:, j, 2, f * D:(f + 1) * D] for j in range(2)], f == 0, f == NF - 1)
                    if f == NF - 1:
                        mm.then_inc(sig["acc_ready"], 1)

            pe.wait_ge(sig["wsplit_lo"], e.n * NPIECE + 4 * NSTEP0 + NPIECE)
            pe.wait_ge(sig["xe_lo"], e.n * 4 + 4)
            pe.wait_ge(sig["gmul_done"], base)
            pe.wait_ge(sig["gmul_done"], NB * NF)
            for n in range(2 * NF):
                half, f = n // NF, n % NF
                if n >= 2:
                    pe.wait_ge(sig["gmul_done"], base + n - 1)
                for m, ready in ((0, sig["a_ready"]), (1, sig["b_ready"])):
                    for k in range(KD):
                        mm = three(bank[2 * (n % 2) + m][:, 0:HALF],
                                   [w[:, j, m, k * FF + f * P:k * FF + (f + 1) * P] for j in range(2)],
                                   [xe[e.c][:, j, k, half * HALF:(half + 1) * HALF] for j in range(2)],
                                   k == 0, k == KD - 1)
                    mm.then_inc(ready, 1)
                if not e.at(E - 1) and n in XT_AT:
                    xpose(e.next(), XT_AT.index(n))
                if n >= 2:
                    down(n - 2)
            down(2 * NF - 2)
            down(2 * NF - 1)

        with_experts(pe, expert)

    ctx.close()


INS = {"x": "x", "ctxT": "ctx_1024", "g_xattn": "g_xattn", "g_ffn": "g_ffn",
       "WqT": "L0_xattn_W_q", "WkT": "L0_xattn_W_k", "WvT": "L0_xattn_W_v", "WoT": "L0_xattn_W_o"}
SAME = ["L0_xattn_b_q", "L0_xattn_b_k", "L0_xattn_b_v", "L0_xattn_b_o", "L0_ffn_ln_g", "L0_ffn_ln_b", "L0_ffn_Wr",
        "L0_ffn_W1", "L0_ffn_W3", "L0_ffn_W2", "L0_ffn_W1s", "L0_ffn_W3s", "L0_ffn_W2s"]


def kernel(**inputs):
    import concourse.bacc as bacc
    import numpy as np
    from concourse.bass_utils import run_bass_kernel_spmd

    nc = bacc.Bacc("TRN2", target_bir_lowering=False, num_devices=1)
    arrays, aps = {}, {}
    for name, src in [*INS.items(), *((n, n) for n in SAME)]:
        v = np.asarray(inputs[src])
        if name.endswith("T"):
            v = np.swapaxes(v, -1, -2)
        v = np.ascontiguousarray(v)
        arrays[f"in_{name}"] = v
        aps[name] = nc.dram_tensor(f"in_{name}", v.shape, mybir.dt.from_np(v.dtype), kind="ExternalInput").ap()
    out = nc.dram_tensor("out_0", (B, S, D), F32, kind="ExternalOutput").ap()
    build(nc, aps, out)
    r = run_bass_kernel_spmd(nc, [arrays], core_ids=[0])
    return r.results[0]["out_0"]
```

```python
from contextlib import ExitStack

import concourse.bass as bass
import concourse.mybir as mybir

F32 = mybir.dt.float32
F32R = mybir.dt.float32r
I32 = mybir.dt.int32
U32 = mybir.dt.uint32
ALU = mybir.AluOpType
ACT = mybir.ActivationFunctionType
AX = mybir.AxisListType

P = 128
B, S, D = 4, 1024, 256
SK = 77
H, DH = 16, 16
FF = 1024
E = 7
CAP = 732
EPS = 1e-5
T = B * S
N = 512
TT = N // P
NB = T // N
KD = D // P
NF = FF // P
NPAIR = H // 2
NG = H // 4
RT = 122
NR = CAP // RT
HALF = CAP // 2
NTT = T // P
NSL = E * NR
WCOLS = KD * FF
PIECE = 512
NPIECE = 3 * WCOLS // PIECE
RING = 4


NCONST = 8
NQST = 13
XE_BANK = (1, 3, 4, 5)
XT_AT = (6, 8, 10, 12)
OHB = 4
OHV = 8
TABLE_AT = 4
NSTEP0 = WCOLS // PIECE
MAX_HEADS = ((0, 6), (6, 12), (12, 16))


class Turn:

    def __init__(self, i, c):
        self.i, self.c = i, c
        self.n = i * 2 + c

    def at(self, n):
        return isinstance(self.n, int) and self.n == n

    def next(self):
        return Turn(self.i, 1) if self.c == 0 else Turn(self.i + 1, 0)

    def prev(self):
        return Turn(self.i, 0) if self.c == 1 else Turn(self.i - 1, 1)


def first_period(do, b):
    n = b.next()
    do("project_keys")
    do("norm", b)
    do("keys_lo")
    do("transpose_x", b)
    do("norm", n)
    do("queries", b)
    do("project_values")
    do("keys", b)
    do("stack", b)
    do("maxima", b, 0)
    do("maxima", b, 1)
    do("transpose_x", n)
    do("maxima", b, 2)
    do("maxima", b, 3)
    do("maxima_T", b)
    do("stack_maxima", b)
    do("queries", n)
    do("first_scores", b)
    for half in range(2):
        do("scores", b, half)
    do("stack", n)
    do("maxima", n, 0)
    do("maxima", n, 1)
    do("attention_hi", b)
    do("project", b)
    do("maxima", n, 2)
    do("maxima", n, 3)
    do("maxima_T", n)
    do("stack_maxima", n)
    do("norm2", b)
    do("transpose_z", b)
    do("first_scores", n)
    do("norm", n.next())


def period(do, b):
    n, f = b.next(), b.prev()

    def nxt(step, *args):
        do(step, n, *args)

    def up(k):
        do("up", f, k)

    def down(k):
        do("down", f, k)

    nxt("keys")
    do("scores", b, 0)
    do("scores", b, 1)
    if b.at(1):
        do("logits", f)
    up(0)
    if b.at(1):
        do("logits_T", f)
    nxt("transpose_x")
    do("attention_hi", b)
    up(1)
    up(2)
    do("project", b)
    nxt("queries")
    nxt("stack")
    do("norm2", b)
    down(0)
    down(1)
    nxt("maxima", 0)
    up(3)
    do("transpose_z", b)
    up(4)
    down(2)
    do("logits", b)
    up(5)
    do("logits_T", b)
    down(3)
    nxt("maxima", 1)
    up(6)
    nxt("maxima", 2)
    down(4)
    down(5)
    nxt("maxima", 3)
    up(7)
    nxt("maxima_T")
    nxt("stack_maxima")
    down(6)
    do("last_hidden", f)
    nxt("first_scores")
    if not b.at(NB - 2):
        do("norm", n.next())
    down(7)
    do("shared_out", f)


def last_period(do, b):
    f = b.prev()

    def up(n, e=f):
        do("up", e, n)

    def down(n, e=f):
        do("down", e, n)

    do("scores", b, 0)
    do("scores", b, 1)
    up(0)
    up(1)
    do("attention_hi", b)
    up(2)
    do("project", b)
    do("norm2", b)
    down(0)
    down(1)
    up(3)
    up(4)
    do("transpose_z", b)
    down(2)
    up(5)
    do("logits", b)
    down(3)
    up(6)
    do("logits_T", b)
    do("choose", 0)
    down(4)
    down(5)
    up(7)
    down(6)
    do("last_hidden", f)
    do("choose", 1)
    down(7)
    do("shared_out", f)
    for k in range(NF):
        up(k, b)
        if k == 0:
            do("count")
        if k == 1:
            do("slots")
        do("place", k, 0)
        if k >= 2:
            down(k - 2, b)
        do("place", k, 1)
        if k == TABLE_AT:
            do("table")
    do("last_hidden", b)
    do("first_tokens")
    down(NF - 2, b)
    down(NF - 1, b)
    do("shared_out", b)


def token_blocks(eng, steps):
    def do(step, *args):
        if step in steps:
            steps[step](*args)

    start, end = Turn(0, 0), Turn(NB // 2 - 1, 1)
    first_period(do, start)
    period(do, start.next())
    with eng.Fori(1, NB // 2 - 1) as i:
        period(do, Turn(i, 0))
        period(do, Turn(i, 1))
    period(do, Turn(NB // 2 - 1, 0))
    last_period(do, end)


def with_experts(eng, expert):
    with eng.Fori(0, E // 2) as i:
        expert(Turn(i, 0))
        expert(Turn(i, 1))
    expert(Turn(E // 2, 0))


def val_at(par, j):
    return DH * j + 64 * par


def den_at(par, j):
    return DH * j + 64 * (1 - par)


def placed(k, part):
    each = -(-2 * NTT // (2 * (TABLE_AT - 2)))
    m = 2 * (k - 3) + part
    return min(max(m, 0) * each, 2 * NTT), min(max(m + 1, 0) * each, 2 * NTT)


def max_banks(b, t):
    if b.at(0):
        return (0, 1, 2) if t % 2 else (3, 4, 5)
    if b.at(1):
        return (3, 6, 7) if t % 2 else (0, 1, 2)
    return 3, 4, 5


def maxT_bank(b):
    return 0 if b.at(1) else 3


def project_bank(b, t):
    return 4 + t % 2 if b.at(0) else 3 + t % 3


def z_bank(b):
    return 6 if b.at(0) else 3


class Steps:

    def __init__(self, eng, sem, base):
        self.eng, self.sem, self.base, self.k = eng, sem, base, 0

    def did(self, ins):
        self.k += 1
        ins.then_inc(self.sem, 1)

    def wait(self):
        self.eng.wait_ge(self.sem, self.base + self.k)


def build(nc, a, out):
    ctx = ExitStack()

    def sem(name):
        return ctx.enter_context(nc.semaphore(name))

    def sb(name, shape, dt=F32):
        return ctx.enter_context(nc.sbuf_tensor(name, shape, dt))

    KB = 256
    AR = sb("split_operands", [P, 142 * KB], F32R)

    def ar(off_kb, *dims):
        n = 1
        for d in dims:
            n *= d
        v = AR[:, off_kb * KB:off_kb * KB + n]
        names = "abcd"[:len(dims)]
        if len(dims) == 1:
            return v
        return v.rearrange(f"p ({' '.join(names)}) -> p {' '.join(names)}", **dict(zip(names, dims)))

    W0 = ar(0, 2, 3, WCOLS)
    W1_ = ar(48, 2, 3, WCOLS)
    wat = ar(48, 2, 4, KD, D)
    xT = ar(64, 2, KD, N)
    qT = ar(72, 2, KD, N)
    qst = ar(80, NPAIR, N)
    kst = ar(96, NPAIR, 2, SK)
    kbd = ar(101, KD, 8, SK)
    hTs = [ar(130, 2, KD, N), ar(106, 2, KD, N)]
    gT = ar(114, 2, RING, N)
    ctx_s = ar(114, 2, KD, B * SK)
    k_s = ar(119, 2, KD, B * SK)
    xe = [ar(130, 2, KD, CAP), ar(96, 2, KD, CAP)]
    wrs = sb("router_split", [P, KD, 2 * E], F32R)
    mtr = sb("row_max_T", [H, N], F32R)

    AF = sb("float_data", [P, 48 * KB], F32)

    def af(off_kb, *dims):
        n = 1
        for d in dims:
            n *= d
        v = AF[:, off_kb * KB:off_kb * KB + n]
        names = "abcd"[:len(dims)]
        if len(dims) == 1:
            return v
        return v.rearrange(f"p ({' '.join(names)}) -> p {' '.join(names)}", **dict(zip(names, dims)))

    xb = [af(0, TT, D), af(4, TT, D)]
    prob = [af(8, 2, N), af(12, 2, N)]
    vst = af(16, 2, 2, 4, P)
    vall = af(24, B, D)
    x1 = [af(28, TT, D), af(32, TT, D)]
    zb = af(36, TT, D)
    att = zb.rearrange("p a b -> p (a b)").rearrange("p (k n) -> p k n", k=KD)
    sil = [af(40, N), af(42, N)]
    xn = af(44, TT, D)
    gf = sb("hidden", [P, 2, N])
    stage = [af(0, WCOLS), af(8, WCOLS)]
    xg = af(16, NR, D)
    ye = af(22, NR, D)

    rc = sb("recip_den", [P, N])
    hf = rc
    watt_stage = af(8, 4, 2 * D)
    sh_stage = [af(32, WCOLS // 2), af(40, WCOLS // 2), gf.rearrange("p a n -> p (a n)")]
    ctx_f = af(36, KD, B, SK)
    ident = sb("ident", [P, P])
    mones = sb("ones", [P, P])
    lower = sb("earlier_tokens", [P, P])
    lgall = sb("logit_parts", [P, NTT, 2 * E])
    lgs = sb("logits_T", [2 * E, N])
    tbo = sb("gated_bias_o", [P, D])
    bvb = sb("bias_v", [SK, D])
    bq = sb("bias_q", [P, KD])
    bk = sb("bias_k", [P, KD])
    lng = sb("ln_gain", [P, KD])
    lnb = sb("ln_bias", [P, KD])
    wrf = sb("router_raw", [P, KD, E])
    gx = sb("gate_x", [P, 1])
    gy = sb("gate_f", [P, 1])
    tgx = sb("tanh_gate_x", [P, 1])
    tgf = sb("tanh_gate_f", [P, 1])
    passed = sb("all_set", [P, 1])
    nhalf = sb("minus_half", [P, TT])
    stt = [sb(f"bn_parts{j}", [P, TT, 6]) for j in range(2)]
    mv = [sb(f"mean_var{j}", [P, TT, 2]) for j in range(2)]
    vs = [sb(f"var_scaled{j}", [P, TT]) for j in range(2)]
    rstd = [sb(f"rstd{j}", [P, TT]) for j in range(2)]
    mx = sb("row_max", [P, TT, H])
    tabg = sb("gather_table", [P, NSL], I32)
    tabs = sb("scatter_table", [P, NSL], I32)
    tabw = sb("gate_table", [P, NSL])
    gidx = sb("gather_now", [P, NR], I32)
    sidx = [sb("scatter_now0", [P, NR], I32), sb("scatter_now1", [P, NR], I32)]
    gw = [sb("gates_now0", [P, NR]), sb("gates_now1", [P, NR])]

    bank = [ctx.enter_context(nc.psum_tensor(f"bank{j}", [P, 512], F32)) for j in range(8)]

    kscr = nc.dram_tensor("k_scratch", (2, D, B * SK), F32).ap()
    zscr = nc.dram_tensor("z_scratch", (T, D), F32).ap()

    at = {}

    def rt(region_kb, *dims):
        n = 1
        for d in dims:
            n *= d
        off = at.get(region_kb, 0)
        at[region_kb] = off + n
        v = AF[:, region_kb * KB + off:region_kb * KB + off + n]
        names = "abcd"[:len(dims)]
        if len(dims) == 1:
            return v
        return v.rearrange(f"p ({' '.join(names)}) -> p {' '.join(names)}", **dict(zip(names, dims)))

    r_lg, r_tmp, r_em8 = (rt(16, NTT, E) for _ in range(3))
    r_oh = rt(16, 2, NTT, E)
    r_tot, r_inc = (rt(16, 2 * NTT, E) for _ in range(2))
    r_m, r_i, r_g = (rt(24, 2, NTT) for _ in range(3))
    r_d, r_e2, r_tok = (rt(24, NTT) for _ in range(3))
    r_pos, r_hi, r_lo, r_ge, r_ones = (rt(24, 2 * NTT) for _ in range(5))
    r_iota = rt(24, P)
    r_steps = rt(24, NR)
    r_row = rc[:, 0:OHB * RT].rearrange("p (a b) -> p a b", a=OHB)
    r_val = [rt(36, OHV, 2, NSL), rt(44, OHV, 2, NSL)]
    assert at[16] <= 8 * KB and at[24] <= 4 * KB and at[36] <= 4 * KB

    names = """passed consts_loaded bk_loaded ctx_loaded wk_loaded wq_loaded stage_loaded0 stage_loaded1 shared_loaded0 shared_loaded1 shared_loaded2 x_loaded0 x_loaded1 ident_ready zeros_ready ones_ready pool_const
    tanh_done wsplit_hi wsplit_lo tbo_ready ctx_hi ctx_lo wr_hi wr_ready kps_ready k_hi k_lo k_stored vps_ready v_ready
    mv_ready rstd_pre rstd_ready xn_ready xb_ready xT_ready xh_ready xl_ready q_ready qh_ready ql_ready
    qst_loaded qst_rest_loaded kst_loaded kbd_loaded vst_ready m_ready m_done mT_ready mtr_ready
    scores_ready exp_done pv_done recip_done attn_done ah_ready al_ready oproj_ready x1_ready mv2_ready rstd2_pre rstd2_ready
    z_ready z_stored zT_ready hh_ready hf_ready hl_ready lg_ready lgs_ready lgT_ready lg_done
    a_ready b_ready sil_done gmul_done gh_ready gl_ready acc_ready acc_done out_stored0 out_stored1
    dve_s1 dve_s2 route_step r_onehots r_counts slots_ready rexp_done r_const tab_done oh_row oh_column oh_val oh_used
    gather_idx gathered scattered ye_free
    xeT_ready xe_hi xe_f xe_lo sidx_ready gw_ready""".split()
    sig = {n: sem(n) for n in names}
    stage_loaded = [sig["stage_loaded0"], sig["stage_loaded1"]]
    shared_loaded = [sig[f"shared_loaded{j}"] for j in range(3)]
    x_loaded = [sig["x_loaded0"], sig["x_loaded1"]]
    out_stored = [sig["out_stored0"], sig["out_stored1"]]

    x_rows = a["x"].rearrange("b s d -> (b s) d").rearrange("(n t p) d -> n p t d", t=TT, p=P)
    z_rows = zscr.rearrange("(n t p) d -> n p t d", t=TT, p=P)
    out2 = out.rearrange("b s d -> (b s) d")
    out_rows = out2.rearrange("(n t p) d -> n p t d", t=TT, p=P)
    w1v = a["L0_ffn_W1"].rearrange("e (k p) f -> e p k f", p=P)
    w3v = a["L0_ffn_W3"].rearrange("e (k p) f -> e p k f", p=P)
    w2v = a["L0_ffn_W2"].rearrange("e (k p) d -> e p k d", p=P)
    wv = [w1v, w3v, w2v]
    wsv = [a["L0_ffn_W1s"].rearrange("(k p) f -> p k f", p=P),
           a["L0_ffn_W3s"].rearrange("(k p) f -> p k f", p=P),
           a["L0_ffn_W2s"].rearrange("(k p) d -> p k d", p=P)]

    def matrix(e, m):
        buf = (e.c + m) % 2
        order = [(0, 0), (0, 2), (1, 1)] if buf == 0 else [(0, 1), (1, 0), (1, 2)]
        before = 32 if buf == 0 else 0
        return buf, (e.i * 3 + order.index((e.c, m)) + 1) * 16 + before

    def q_of(b):
        return hTs[0] if b.at(0) else qT

    def apart(eng):
        eng.sem_inc(sig["passed"], 1)

    block = ctx.enter_context(nc.Block())

    @block.sync
    def _(sp):
        sp.sem_inc(out_stored[1], 16)
        for k in range(KD):
            sp.dma_start(ctx_f[:, k], a["ctxT"].rearrange("b (k p) t -> k p b t", p=P)[k]).then_inc(sig["ctx_loaded"], 16)

        def load_attention(j, loaded):
            sp.dma_start(watt_stage[:, j], a[("WqT", "WkT", "WvT", "WoT")[j]].rearrange("(k p) d -> p k d", p=P))\
              .then_inc(loaded, 16)

        n_const = 0

        def const(dst, src, small=False):
            nonlocal n_const
            n_const += 1
            sp.dma_start(dst, src, allow_slow_non_contiguous=small).then_inc(sig["consts_loaded"], 16)

        load_attention(1, sig["wk_loaded"])
        sp.dma_start(xb[0], x_rows[0]).then_inc(x_loaded[0], 16)
        sp.dma_start(bk[:, :], a["L0_xattn_b_k"].rearrange("(k p) -> p k", p=P), allow_slow_non_contiguous=True)\
          .then_inc(sig["bk_loaded"], 16)
        load_attention(0, sig["wq_loaded"])
        const(bq[:, :], a["L0_xattn_b_q"].rearrange("(k p) -> p k", p=P), small=True)
        const(tbo[:, :], a["L0_xattn_b_o"].partition_broadcast(P))
        const(gx[:, :], a["g_xattn"].partition_broadcast(P))
        const(gy[:, :], a["g_ffn"].partition_broadcast(P))
        sp.dma_start(xb[1], x_rows[1]).then_inc(x_loaded[1], 16)
        const(bvb[:, :], a["L0_xattn_b_v"].partition_broadcast(SK))
        const(wrf[:, :, :], a["L0_ffn_Wr"].rearrange("(k p) e -> p k e", p=P))
        const(lng[:, :], a["L0_ffn_ln_g"].rearrange("(k p) -> p k", p=P), small=True)
        const(lnb[:, :], a["L0_ffn_ln_b"].rearrange("(k p) -> p k", p=P), small=True)
        assert n_const == NCONST
        for j in (2, 3):
            load_attention(j, stage_loaded[0])

        def project_keys():
            sp.wait_ge(sig["k_lo"], KD)
            for j in range(2):
                sp.dma_start(kscr[j].rearrange("(k p) t -> p k t", p=P), k_s[:, j].bitcast(F32)).then_inc(sig["k_stored"], 16)

        def load_shared(h):
            if h >= 3:
                sp.wait_ge(sig["wsplit_lo"], NSTEP0 + 2 * (h - 2))
            m, part = h // 2, h % 2
            kk = wsv[m].shape[1] // 2
            sp.dma_start(sh_stage[h % 3].rearrange("p (k f) -> p k f", k=kk), wsv[m][:, part * kk:(part + 1) * kk])\
              .then_inc(shared_loaded[h % 3], 16)

        for h in range(3):
            load_shared(h)

        def load_more_shared(b, half):
            if b.at(0) and half == 0:
                for h in range(3, 6):
                    load_shared(h)

        def load_keys(b):
            if b.c == 0:
                bt = b.i
                sp.wait_ge(sig["zeros_ready"], 1)
                sp.wait_ge(sig["m_done"], b.n * TT)
                kd = kscr.rearrange("s (g j d) (b t) -> s j d g b t", g=KD, j=8, b=B)
                for j in range(8):
                    src = k_s[16 * j:16 * j + 16, 0, :, 0:SK].bitcast(F32) if b.at(0) else kd[0, j, :, :, bt, :]
                    sp.dma_start(kbd[16 * j:16 * j + 16, :, j, :].bitcast(F32), src).then_inc(sig["kbd_loaded"], 16)
                sp.wait_ge(sig["k_stored"], 32)
                sp.wait_ge(sig["scores_ready"], b.n * NPAIR)
                ks = kscr.rearrange("s (r w d) (b t) -> s w d r b t", w=2, d=DH, b=B)
                for base, part in ((0, 0), (32, 0), (64, 1)):
                    for w in range(2):
                        sp.dma_start(kst[base + 16 * w:base + 16 * w + 16, :, w, :].bitcast(F32), ks[part, w, :, :, bt, :])\
                          .then_inc(sig["kst_loaded"], 16)

        def stack_queries(b):
            sp.wait_ge(sig["qh_ready"], (b.n + 1) * KD)
            if b.at(1):
                sp.wait_ge(sig["scores_ready"], NPAIR)
            for r in range(4):
                for base in (0, 64):
                    sp.dma_start(qst[base:base + 32, r::4, :].bitcast(F32), q_of(b)[32 * r:32 * r + 32, 0].bitcast(F32)).then_inc(sig["qst_loaded"], 16)
            sp.wait_ge(sig["ql_ready"], (b.n + 1) * KD)
            for r in range(4):
                sp.dma_start(qst[32:64, r::4, :].bitcast(F32), q_of(b)[32 * r:32 * r + 32, 1].bitcast(F32)).then_inc(sig["qst_loaded"], 16)

        def stack_maxima(b):
            sp.wait_ge(sig["mtr_ready"], b.n + 1)
            for r0, r1, loaded in ((0, 2, sig["qst_loaded"]), (2, NPAIR, sig["qst_rest_loaded"])):
                sp.dma_start(qst[96:112, r0:r1, :].bitcast(F32),
                             mtr[:, :].bitcast(F32).unsqueeze(1).broadcast_to([H, r1 - r0, N])).then_inc(loaded, 16)

        def store_z(b):
            sp.wait_ge(sig["z_ready"], (b.n + 1) * TT)
            sp.dma_start(z_rows[b.n], zb).then_inc(sig["z_stored"], 16)
            if not (b.at(NB - 2) or b.at(NB - 1)):
                sp.dma_start(xb[b.c], x_rows[b.n + 2]).then_inc(x_loaded[b.c], 16)

        def store_out(b):
            if b.at(NB - 1):
                return
            sp.wait_ge(sig["acc_done"], (b.n + 1) * TT)
            sp.dma_start(out_rows[b.n], x1[b.c]).then_inc(out_stored[b.c], 16)

        def load_weights(e):
            for j in range(3):
                sp.wait_ge(sig["wsplit_lo"], (e.n * 3 + 3 + j) * NSTEP0)
                buf, _ = matrix(e, j)
                sp.dma_start(stage[buf].rearrange("p (k f) -> p k f", k=wv[j].shape[2]), wv[j][e.n])\
                  .then_inc(stage_loaded[buf], 16)

        def expert(e):
            if not e.at(E - 1):
                load_weights(e.next())

        def first_weights(b):
            store_z(b)
            if b.at(NB - 1):
                load_weights(Turn(0, 0))

        token_blocks(sp, {"project_keys": project_keys, "keys": load_keys, "stack": stack_queries,
                          "stack_maxima": stack_maxima, "norm2": first_weights, "scores": load_more_shared,
                          "shared_out": store_out})
        with_experts(sp, expert)
        for c in range(2):
            sp.wait_ge(out_stored[c], 16 * NB // 2 + 16 * c)
        sp.wait_ge(sig["scattered"], 16 * NR * E)

    @block.gpsimd
    def _(pool):
        st = Steps(pool, sig["pool_const"], 0)

        def do(ins):
            st.did(ins)
            st.wait()

        pool.sem_inc(sig["ye_free"], 1)
        do(pool.memset(ident[:, :], 0.0))
        pool.affine_select(out=ident[:, :], in_=ident[:, :], compare_op=ALU.not_equal, fill=1.0, base=0,
                           pattern=[[-1, P]], channel_multiplier=1).then_inc(sig["ident_ready"], 1)
        do(pool.memset(kbd.bitcast(F32), 0.0))
        kneg = kst[96:112].rearrange("p a b t -> p (a b) t")
        do(pool.memset(kst.bitcast(F32), 0.0))
        do(pool.affine_select(out=kneg, in_=kneg.bitcast(F32), compare_op=ALU.not_equal, fill=-1.0, base=0,
                              pattern=[[-1, H], [0, SK]], channel_multiplier=1))
        pool.memset(passed[:, :], 0.0).then_inc(sig["zeros_ready"], 1)
        do(pool.memset(nhalf[:, :], -0.5))
        do(pool.memset(mones[:, :], 1.0))
        do(pool.affine_select(out=lower[:, :], in_=mones[:, :], compare_op=ALU.is_gt, fill=0.0, base=0,
                              pattern=[[1, P]], channel_multiplier=-1))
        do(pool.memset(vst[0:SK], 0.0))
        for par in range(2):
            for j in range(4):
                do(pool.memset(vst[0:SK, :, par, j, den_at(par, j):den_at(par, j) + DH], 1.0))
        pool.memset(passed[:, :], 0.0).then_inc(sig["ones_ready"], 1)

        def norm(b):
            pool.wait_ge(sig["rstd_ready"], b.n)
            pool.wait_ge(sig["mv_ready"], b.n + 1)
            apart(pool)
            pool.tensor_scalar(vs[0][:, :], mv[0][:, :, 1], EPS, None, ALU.add).then_inc(sig["rstd_pre"], 1)
            pool.wait_ge(sig["rstd_pre"], b.n + 1)
            pool.tensor_tensor(rstd[0][:, :], vs[0][:, :], nhalf[:, :], ALU.pow).then_inc(sig["rstd_ready"], 1)
            pool.wait_ge(sig["xn_ready"], (b.n + 1) * TT)
            pool.wait_ge(sig["tbo_ready"], 1)
            for t in range(TT):
                pool.tensor_tensor(xb[b.c][:, t], xb[b.c][:, t], tbo[:, :], ALU.add).then_inc(sig["xb_ready"], 1)

        def split_shared():
            for n in range(NPIECE):
                m, col, h = n // NSTEP0, n % NSTEP0 * PIECE, n // 2
                pool.wait_ge(sig["wsplit_hi"], NSTEP0 + n + 1)
                pool.tensor_tensor(W0[:, 1, m, col:col + PIECE], sh_stage[h % 3][:, n % 2 * PIECE:(n % 2 + 1) * PIECE],
                                   W0[:, 0, m, col:col + PIECE].bitcast(F32), ALU.subtract).then_inc(sig["wsplit_lo"], 1)

        def attention_lo(b, half):
            if half == 0:
                if b.at(0):
                    split_shared()
                return
            for k in range(KD):
                pool.wait_ge(sig["ah_ready"], b.n * KD + k + 1)
                aT = q_of(b)
                pool.tensor_tensor(aT[:, 1, k], att[:, k], aT[:, 0, k].bitcast(F32), ALU.subtract)\
                    .then_inc(sig["al_ready"], 1)

        def stationary_values(b):
            if b.c == 0:
                if b.at(0):
                    pool.wait_ge(sig["v_ready"], B)
                pool.wait_ge(sig["pv_done"], b.n * NPAIR)
                for par in range(2):
                    for j in range(4):
                        src = vall[0:SK, b.i, :].rearrange("t (g w j d) -> t g w j d", g=2, w=2, j=4)[:, :, par, j, :]
                        pool.tensor_copy(vst[0:SK, :, par, j, val_at(par, j):val_at(par, j) + DH], src)\
                            .then_inc(sig["vst_ready"], 1)
                        pool.wait_ge(sig["vst_ready"], b.i * 8 + par * 4 + j + 1)

        def norm2(b):
            pool.wait_ge(sig["rstd2_ready"], b.n)
            pool.wait_ge(sig["mv2_ready"], b.n + 1)
            apart(pool)
            pool.tensor_scalar(vs[1][:, :], mv[1][:, :, 1], 1.0 + EPS, EPS * EPS, ALU.mult, ALU.add)\
                .then_inc(sig["rstd2_pre"], 1)
            pool.wait_ge(sig["rstd2_pre"], b.n + 1)
            pool.tensor_tensor(rstd[1][:, :], vs[1][:, :], nhalf[:, :], ALU.pow).then_inc(sig["rstd2_ready"], 1)

        def route_const(ch):
            if ch > 0:
                return
            pool.wait_ge(sig["lg_done"], NB)
            pool.wait_ge(sig["z_stored"], 16 * NB)
            pool.iota(r_em8, pattern=[[0, NTT], [1, E]], base=-8, channel_multiplier=0,
                      allow_small_or_imprecise_dtypes=True).then_inc(sig["r_const"], 1)
            pool.iota(r_tok, pattern=[[P, NTT]], base=1, channel_multiplier=1,
                      allow_small_or_imprecise_dtypes=True).then_inc(sig["r_const"], 1)
            pool.iota(r_iota, pattern=[[1, P]], base=0, channel_multiplier=0,
                      allow_small_or_imprecise_dtypes=True).then_inc(sig["r_const"], 1)
            pool.iota(r_steps, pattern=[[RT, NR]], base=RT, channel_multiplier=0,
                      allow_small_or_imprecise_dtypes=True).then_inc(sig["r_const"], 1)
            pool.memset(r_ones, 1.0).then_inc(sig["r_const"], 1)
            for n in range(NPIECE):
                m, j = n // 4, n % 4
                cols = slice(j * PIECE, (j + 1) * PIECE)
                pool.wait_ge(sig["wsplit_hi"], 4 * NSTEP0 + n + 1)
                pool.tensor_tensor(W1_[:, 1, m, cols], stage[matrix(Turn(0, 0), m)[0]][:, cols],
                                   W1_[:, 0, m, cols].bitcast(F32), ALU.subtract).then_inc(sig["wsplit_lo"], 1)

        def onehot_values():
            pool.wait_ge(sig["slots_ready"], 1)
            gall = r_g.rearrange("p c t -> p (c t)")
            wide = lambda v: v.unsqueeze(2).broadcast_to([P, OHV, NSL])
            for n in range(0, 2 * NTT, OHV):
                v = r_val[n // OHV % 2]
                pool.wait_ge(sig["oh_column"], n // OHV + 1)
                pool.tensor_tensor(v[:, :, 0], v[:, :, 1], wide(r_tok[:, n % NTT:n % NTT + OHV]), ALU.mult)\
                    .then_inc(sig["oh_val"], 1)
                pool.wait_ge(sig["oh_val"], n // OHV * 2 + 1)
                pool.tensor_tensor(v[:, :, 1], v[:, :, 1], wide(gall[:, n:n + OHV]), ALU.mult).then_inc(sig["oh_val"], 1)

        def gather(n):
            pool.wait_ge(sig["gather_idx"], n)
            apart(pool)
            for t in range(NR):
                pool.indirect_dma_start(xg[0:RT, t, :], None, zscr,
                                        bass.IndirectOffsetOnAxis(ap=gidx[0:RT, t:t + 1].bitcast(U32), axis=0))\
                    .then_inc(sig["gathered"], 16)

        def first_gather():
            gather(1)

        token_blocks(pool, {"norm": norm, "scores": attention_lo, "stack": stationary_values, "norm2": norm2,
                            "choose": route_const, "slots": onehot_values, "table": first_gather})

        for c in range(2):
            pool.wait_ge(out_stored[c], 16 * NB // 2 + 16 * c)

        def expert(e):
            if not e.at(E - 1):
                pool.wait_ge(sig["xeT_ready"], (e.n + 1) * 2 * KD)
                gather(e.n + 2)
            for half in range(2):
                pool.wait_ge(sig["acc_done"], T // P + (e.n * 2 + half + 1) * (NR // 2))
                apart(pool)
                for t in range(half * NR // 2, (half + 1) * NR // 2):
                    pool.indirect_dma_start(out2, bass.IndirectOffsetOnAxis(ap=sidx[e.c][0:RT, t:t + 1].bitcast(U32), axis=0),
                                            ye[0:RT, t, :], None, bounds_check=T - 1, oob_is_err=False,
                                            compute_op=ALU.add).then_inc(sig["scattered"], 16)
            pool.wait_ge(sig["scattered"], (e.n + 1) * NR * 16)
            pool.sem_inc(sig["ye_free"], 1)

        with_experts(pool, expert)

    @block.scalar
    def _(act):
        def split_attention(j):
            act.copy(wat[:, 0, j], watt_stage[:, j]).then_inc(sig["wsplit_hi"], 1)

        def project_keys():
            act.wait_ge(sig["ctx_loaded"], 16 * KD)
            act.copy(ctx_s[:, 0], ctx_f.rearrange("p k b t -> p k (b t)")).then_inc(sig["ctx_hi"], 1)
            act.wait_ge(sig["wk_loaded"], 16)
            split_attention(1)
            act.wait_ge(sig["wq_loaded"], 16)
            split_attention(0)
            act.wait_ge(sig["bk_loaded"], 16)
            for k in range(KD):
                act.wait_ge(sig["kps_ready"], k + 1)
                act.activation(k_s[:, 0, k], bank[k][:, 0:B * SK], ACT.Identity, bias=bk[:, k:k + 1])\
                   .then_inc(sig["k_hi"], 1)
            act.wait_ge(sig["consts_loaded"], 16 * NCONST)
            act.activation(tgx[:, :], gx[:, :], ACT.Tanh).then_inc(sig["tanh_done"], 1)
            act.activation(tgf[:, :], gy[:, :], ACT.Tanh).then_inc(sig["tanh_done"], 1)

        def project_values():
            act.wait_ge(stage_loaded[0], 32)
            for j in (2, 3):
                split_attention(j)
            act.copy(wrs[:, :, 0:E], wrf[:, :, :]).then_inc(sig["wr_hi"], 1)

        def split_shared(h):
            act.wait_ge(shared_loaded[h % 3], 16 * (h // 3 + 1))
            for j in range(2):
                m, col = h // 2, (h % 2 * 2 + j) * PIECE
                act.copy(W0[:, 0, m, col:col + PIECE], sh_stage[h % 3][:, j * PIECE:(j + 1) * PIECE])\
                   .then_inc(sig["wsplit_hi"], 1)

        def transpose_x(b):
            for k in range(KD):
                act.wait_ge(sig["xT_ready"], b.n * KD + k + 1)
                act.copy(xT[:, 0, k], bank[6 + k][:, :]).then_inc(sig["xh_ready"], 1)

        def queries(b):
            for k in range(KD):
                act.wait_ge(sig["q_ready"], b.n * KD + k + 1)
                act.activation(q_of(b)[:, 0, k], bank[4 + k][:, :], ACT.Identity, bias=bq[:, k:k + 1])\
                   .then_inc(sig["qh_ready"], 1)

        def maxima_T(b):
            act.wait_ge(sig["mT_ready"], b.n + 1)
            if b.at(1):
                act.wait_ge(sig["qst_loaded"], 16 * NQST)
                act.wait_ge(sig["qst_rest_loaded"], 16)
            act.copy(mtr[:, :], bank[maxT_bank(b)][0:H, :]).then_inc(sig["mtr_ready"], 1)

        def exps(b, p):
            act.wait_ge(sig["scores_ready"], b.n * NPAIR + p + 1)
            if p >= 2:
                act.wait_ge(sig["pv_done"], b.n * NPAIR + p - 1)
            for w in range(2):
                last = act.activation(prob[p % 2][0:SK, w], bank[2 * (p % 2) + w][0:SK, :], ACT.Exp, scale=DH ** -0.5)
            last.then_inc(sig["exp_done"], 1)

        def first_scores(b):
            for p in range(2):
                exps(b, p)

        def scores(b, half):
            for p in range(2 + 2 * half, 4 + 4 * half):
                exps(b, p)
                if b.at(0):
                    split_shared(p - 2)
            if half == 0:
                return
            act.wait_ge(sig["attn_done"], b.n * NG + 2)
            act.copy(q_of(b)[:, 0, 0], att[:, 0]).then_inc(sig["ah_ready"], 1)

        def attention_hi(b):
            act.wait_ge(sig["attn_done"], (b.n + 1) * NG)
            act.copy(q_of(b)[:, 0, 1], att[:, 1]).then_inc(sig["ah_ready"], 1)

        def transpose_z(b):
            for k in range(KD):
                act.wait_ge(sig["zT_ready"], b.n * KD + k + 1)
                act.activation(hTs[b.c][:, 0, k], bank[z_bank(b) + k][:, :], ACT.Identity, bias=lnb[:, k:k + 1],
                               scale=lng[:, k:k + 1]).then_inc(sig["hh_ready"], 1)

        def logits(b):
            act.wait_ge(sig["lg_ready"], b.n + 1)
            act.copy(lgs[:, :], bank[6 if b.at(0) else 5][0:2 * E, :]).then_inc(sig["lgs_ready"], 1)

        def hidden_hi(b, f):
            act.wait_ge(sig["gmul_done"], b.n * NF + f + 1)
            act.copy(gT[:, 0, f % RING], gf[:, f % 2]).then_inc(sig["gh_ready"], 1)

        def up(b, f):
            if f >= 1:
                hidden_hi(b, f - 1)
            act.wait_ge(sig["a_ready"], b.n * NF + f + 1)
            if f >= 2:
                act.wait_ge(sig["gmul_done"], b.n * NF + f - 1)
            act.activation(sil[f % 2], bank[2 * f % 3][:, :], ACT.Silu).then_inc(sig["sil_done"], 1)

        def last_hidden(b):
            hidden_hi(b, NF - 1)

        def split_piece(e, n):
            m, j = n // 4, n % 4
            buf, loaded = matrix(e, m)
            if j == 0:
                act.wait_ge(stage_loaded[buf], loaded)
            dst = (W1_ if e.c == 0 else W0)[:, 0, m, j * PIECE:(j + 1) * PIECE]
            act.copy(dst, stage[buf][:, j * PIECE:(j + 1) * PIECE]).then_inc(sig["wsplit_hi"], 1)

        def xe_hi(e, g):
            k, half = g % KD, g // KD
            ps = bank[XE_BANK[g] if e.at(0) else 7]
            act.wait_ge(sig["xeT_ready"], e.n * 4 + g + 1)
            act.activation(xe[e.c][:, 0, k, half * HALF:(half + 1) * HALF], ps[:, 0:HALF], ACT.Identity,
                           bias=lnb[:, k:k + 1], scale=lng[:, k:k + 1]).then_inc(sig["xe_hi"], 1)

        def first_pieces(k):
            for n in range(3 * k, 3 * k + 3):
                split_piece(Turn(0, 0), n)

        def choose(ch):
            first_pieces(ch)

        def count():
            act.wait_ge(sig["r_onehots"], 1)
            act.activation(r_e2, r_d, ACT.Exp).then_inc(sig["rexp_done"], 1)
            first_pieces(2)

        def place(k, part):
            if k == 1 and part == 0:
                first_pieces(3)

        def store_last(b):
            if b.at(NB - 1):
                act.wait_ge(sig["acc_done"], NB * TT)
                act.dma_start(out_rows[b.n], x1[b.c]).then_inc(out_stored[b.c], 16)

        def first_tokens():
            for g in range(4):
                xe_hi(Turn(0, 0), g)

        token_blocks(act, {"project_keys": project_keys, "project_values": project_values,
                           "first_scores": first_scores, "scores": scores, "attention_hi": attention_hi,
                           "transpose_x": transpose_x, "queries": queries, "maxima_T": maxima_T,
                           "transpose_z": transpose_z, "logits": logits, "up": up, "last_hidden": last_hidden,
                           "choose": choose, "count": count, "place": place,
                           "first_tokens": first_tokens, "shared_out": store_last})

        def expert(e):
            base = NB * NF + e.n * 2 * NF
            for n in range(2 * NF + 1):
                if n >= 1:
                    act.wait_ge(sig["gmul_done"], base + n)
                    act.copy(gT[:, 0, (n - 1) % RING, 0:HALF], gf[:, (n - 1) % 2, 0:HALF]).then_inc(sig["gh_ready"], 1)
                if n < 2 * NF:
                    act.wait_ge(sig["a_ready"], base + n + 1)
                    act.activation(sil[n % 2][:, 0:HALF], bank[2 * (n % 2)][:, 0:HALF], ACT.Silu)\
                       .then_inc(sig["sil_done"], 1)
                if not e.at(E - 1) and n < NPIECE:
                    split_piece(e.next(), n)
                if not e.at(E - 1) and n in XT_AT:
                    xe_hi(e.next(), XT_AT.index(n))

        with_experts(act, expert)

    @block.vector
    def _(dve):
        def split_attention(n, j):
            dve.wait_ge(sig["wsplit_hi"], n + 1)
            dve.tensor_tensor(wat[:, 1, j], watt_stage[:, j], wat[:, 0, j].bitcast(F32), ALU.subtract)\
               .then_inc(sig["wsplit_lo"], 1)

        def project_keys():
            dve.wait_ge(sig["ctx_hi"], 1)
            dve.tensor_tensor(ctx_s[:, 1], ctx_f.rearrange("p k b t -> p k (b t)"), ctx_s[:, 0].bitcast(F32),
                              ALU.subtract).then_inc(sig["ctx_lo"], 1)
            split_attention(0, 1)
            split_attention(1, 0)

        def keys_lo():
            for k in range(KD):
                dve.wait_ge(sig["k_hi"], k + 1)
                dve.scalar_tensor_tensor(out=k_s[:, 1, k], in0=bank[k][:, 0:B * SK], scalar=bk[:, k:k + 1],
                                         in1=k_s[:, 0, k].bitcast(F32), op0=ALU.add, op1=ALU.subtract)\
                   .then_inc(sig["k_lo"], 1)
            dve.wait_ge(sig["tanh_done"], 2)
            dve.tensor_scalar(tbo[:, :], tbo[:, :], tgx[:, 0:1], None, ALU.mult).then_inc(sig["tbo_ready"], 1)

        def project_values():
            split_attention(2, 2)
            split_attention(3, 3)
            dve.wait_ge(sig["wr_hi"], 1)
            dve.tensor_tensor(wrs[:, :, E:2 * E], wrf[:, :, :], wrs[:, :, 0:E].bitcast(F32), ALU.subtract)\
               .then_inc(sig["wr_ready"], 1)
            for b in range(B):
                dve.wait_ge(sig["vps_ready"], b + 1)
                dve.tensor_tensor(vall[0:SK, b], bank[2 + b % 2][0:SK, 0:D], bvb[:, :], ALU.add)\
                   .then_inc(sig["v_ready"], 1)

        def norm_stats(st, which, src, ready):
            for t in range(TT):
                st.did(dve.bn_stats(stt[which][:, t], src[:, t]))
            st.wait()
            apart(dve)
            for t in range(TT):
                last = dve.bn_aggr(mv[which][:, t], stt[which][:, t])
                if t < TT - 1:
                    st.did(last)
            last.then_inc(ready, 1)

        def norm(b):
            st = Steps(dve, sig["dve_s1"], b.n * 7)
            dve.wait_ge(x_loaded[b.c], (b.i + 1) * 16)
            dve.wait_ge(sig["xn_ready"], b.n * TT)
            norm_stats(st, 0, xb[b.c], sig["mv_ready"])
            assert st.k == 7
            dve.wait_ge(sig["rstd_ready"], b.n + 1)
            dve.wait_ge(sig["mv_ready"], b.n + 1)
            st.wait()
            for t in range(TT):
                dve.tensor_scalar(xn[:, t], xb[b.c][:, t], mv[0][:, t, 0:1], rstd[0][:, t:t + 1], ALU.subtract, ALU.mult)\
                   .then_inc(sig["xn_ready"], 1)

        def transpose_x(b):
            for k in range(KD):
                dve.wait_ge(sig["xh_ready"], b.n * KD + k + 1)
                dve.tensor_tensor(xT[:, 1, k], bank[6 + k][:, :], xT[:, 0, k].bitcast(F32), ALU.subtract)\
                   .then_inc(sig["xl_ready"], 1)

        def queries(b):
            for k in range(KD):
                dve.wait_ge(sig["qh_ready"], b.n * KD + k + 1)
                dve.scalar_tensor_tensor(out=q_of(b)[:, 1, k], in0=bank[4 + k][:, :], scalar=bq[:, k:k + 1],
                                         in1=q_of(b)[:, 0, k].bitcast(F32), op0=ALU.add, op1=ALU.subtract)\
                   .then_inc(sig["ql_ready"], 1)

        def maxima(b, t):
            dve.wait_ge(sig["m_ready"], b.n * TT + t + 1)
            for j, (h0, h1) in enumerate(MAX_HEADS):
                last = dve.tensor_reduce(mx[:, t, h0:h1],
                                         bank[max_banks(b, t)[j]][:, 0:(h1 - h0) * SK].rearrange("p (h t) -> p h t", t=SK), AX.X, ALU.max)
            last.then_inc(sig["m_done"], 1)

        def scores(b, half):
            dve.wait_ge(sig["z_stored"], b.n * 16)
            for g in range(2 * half, 2 * half + 2):
                dve.wait_ge(sig["pv_done"], b.n * NPAIR + 2 * g + 2)
                dve.wait_ge(sig["hl_ready"], b.n * KD)
                dve.wait_ge(sig["attn_done"], b.n * NG + g)
                va, dn = (slice(0, 64), slice(64, 128)) if g % 2 == 0 else (slice(64, 128), slice(0, 64))
                dve.reciprocal(rc[va, :], bank[4 + g % 2][dn, :]).then_inc(sig["recip_done"], 1)
                dve.wait_ge(sig["recip_done"], b.n * NG + g + 1)
                dve.tensor_tensor(att[va, g // 2], bank[4 + g % 2][va, :], rc[va, :], ALU.mult)\
                   .then_inc(sig["attn_done"], 1)

        def project(b):
            st = Steps(dve, sig["dve_s2"], b.n * 7)
            dve.wait_ge(sig["xb_ready"], (b.n + 1) * TT)
            dve.wait_ge(out_stored[b.c], b.i * 16 + 16 * b.c)
            for t in range(TT):
                dve.wait_ge(sig["oproj_ready"], b.n * TT + t + 1)
                dve.scalar_tensor_tensor(out=x1[b.c][:, t], in0=bank[project_bank(b, t)][:, 0:D], scalar=tgx[:, 0:1],
                                         in1=xb[b.c][:, t], op0=ALU.mult, op1=ALU.add).then_inc(sig["x1_ready"], 1)
            dve.wait_ge(sig["x1_ready"], (b.n + 1) * TT)
            dve.wait_ge(sig["z_ready"], b.n * TT)
            norm_stats(st, 1, x1[b.c], sig["mv2_ready"])
            assert st.k == 7

        def norm2(b):
            dve.wait_ge(sig["rstd2_ready"], b.n + 1)
            dve.wait_ge(sig["mv2_ready"], b.n + 1)
            dve.wait_ge(sig["dve_s2"], (b.n + 1) * 7)
            for t in range(TT):
                dve.tensor_scalar(zb[:, t], x1[b.c][:, t], mv[1][:, t, 0:1], rstd[1][:, t:t + 1], ALU.subtract, ALU.mult)\
                   .then_inc(sig["z_ready"], 1)

        def transpose_z(b):
            for k in range(KD):
                dve.wait_ge(sig["hl_ready"], b.n * KD + k)
                dve.wait_ge(sig["hh_ready"], b.n * KD + k + 1)
                dve.tensor_scalar(hf[:, :], bank[z_bank(b) + k][:, :], lng[:, k:k + 1], lnb[:, k:k + 1], ALU.mult, ALU.add)\
                   .then_inc(sig["hf_ready"], 1)
                dve.wait_ge(sig["hf_ready"], b.n * KD + k + 1)
                dve.tensor_tensor(hTs[b.c][:, 1, k], hf[:, :], hTs[b.c][:, 0, k].bitcast(F32), ALU.subtract)\
                   .then_inc(sig["hl_ready"], 1)

        def logits_T(b):
            dve.wait_ge(sig["lgT_ready"], b.n + 1)
            dve.tensor_copy(lgall[:, bass.ds(b.n * TT, TT), :],
                            bank[7 if b.at(0) else 3][:, 0:64].rearrange("p (t e) -> p t e", t=TT)[:, :, 0:2 * E]).then_inc(sig["lg_done"], 1)

        def hidden_lo(b, f):
            dve.wait_ge(sig["gh_ready"], b.n * NF + f + 1)
            dve.tensor_tensor(gT[:, 1, f % RING], gf[:, f % 2], gT[:, 0, f % RING].bitcast(F32), ALU.subtract)\
               .then_inc(sig["gl_ready"], 1)

        def up(b, f):
            if f >= 1:
                hidden_lo(b, f - 1)
            dve.wait_ge(sig["b_ready"], b.n * NF + f + 1)
            dve.wait_ge(sig["sil_done"], b.n * NF + f + 1)
            if f >= 2:
                dve.wait_ge(sig["gl_ready"], b.n * NF + f - 1)
            dve.tensor_tensor(gf[:, f % 2], bank[(2 * f + 1) % 3][:, :], sil[f % 2], ALU.mult)\
               .then_inc(sig["gmul_done"], 1)

        def last_hidden(b):
            hidden_lo(b, NF - 1)

        def shared_out(b):
            for t in range(TT):
                dve.wait_ge(sig["acc_ready"], b.n * TT + t // 2 * 2 + 2)
                dve.scalar_tensor_tensor(out=x1[b.c][:, t], in0=bank[6 + t // 2][:, t % 2 * D:t % 2 * D + D],
                                         scalar=tgf[:, 0:1], in1=x1[b.c][:, t], op0=ALU.mult, op1=ALU.add)\
                   .then_inc(sig["acc_done"], 1)

        rst = Steps(dve, sig["route_step"], 0)

        def do(ins):
            rst.did(ins)
            rst.wait()

        def choose(ch):
            fl = lambda v: v.rearrange("p t e -> p (t e)")
            bc = lambda v: v.unsqueeze(2).broadcast_to([P, NTT, E])
            if ch == 0:
                dve.wait_ge(sig["lg_done"], NB)
                dve.wait_ge(sig["r_const"], 5)
                do(dve.tensor_tensor(r_lg, lgall[:, :, 0:E], lgall[:, :, E:2 * E], ALU.add))
            else:
                do(dve.scalar_tensor_tensor(out=fl(r_lg), in0=fl(r_oh[:, 0]), scalar=-3e38, in1=fl(r_lg),
                                            op0=ALU.mult, op1=ALU.add))
            do(dve.tensor_reduce(r_m[:, ch], r_lg, AX.X, ALU.max))
            do(dve.tensor_tensor(r_tmp, r_lg, bc(r_m[:, ch]), ALU.is_equal))
            do(dve.tensor_tensor(r_tmp, r_tmp, r_em8, ALU.mult))
            do(dve.tensor_reduce(r_i[:, ch], r_tmp, AX.X, ALU.min))
            do(dve.tensor_tensor(r_oh[:, ch], r_em8, bc(r_i[:, ch]), ALU.is_equal))
            if ch == 1:
                dve.tensor_tensor(r_d, r_m[:, 1], r_m[:, 0], ALU.subtract).then_inc(sig["r_onehots"], 1)

        def count():
            dve.wait_ge(sig["rexp_done"], 1)
            do(dve.tensor_scalar(r_d, r_e2, 1.0, None, ALU.add))
            do(dve.reciprocal(r_g[:, 0], r_d))
            do(dve.tensor_scalar(r_g[:, 0], r_g[:, 0], tgf[:, 0:1], None, ALU.mult))
            do(dve.tensor_tensor(r_g[:, 1], r_g[:, 0], r_e2, ALU.mult))
            dve.wait_ge(sig["r_counts"], 2)
            do(dve.tensor_copy(r_tot, bank[4][:, 0:2 * NTT * E].rearrange("p (t e) -> p t e", e=E)))

            for e in range(E):
                rst.did(dve.tensor_tensor_scan(r_inc[:, :, e], r_ones, r_tot[:, :, e], 0.0, ALU.mult, ALU.add))
            rst.wait()
            do(dve.tensor_tensor(r_inc, r_inc, r_tot, ALU.subtract))
            do(dve.tensor_tensor(r_inc, bank[3][:, 0:2 * NTT * E].rearrange("p (t e) -> p t e", e=E), r_inc, ALU.add))
            do(dve.tensor_tensor(r_inc, r_inc, r_oh.rearrange("p c t e -> p (c t) e"), ALU.mult))
            do(dve.tensor_reduce(r_pos, r_inc, AX.X, ALU.add))

        def onehot_columns(m):
            n = m * OHV
            if n >= 2 * OHV:
                dve.wait_ge(sig["oh_used"], n - OHV)
            dve.tensor_tensor(r_val[m % 2][:, :, 1], r_iota[:, 0:NSL].unsqueeze(1).broadcast_to([P, OHV, NSL]),
                              r_hi[:, n:n + OHV].unsqueeze(2).broadcast_to([P, OHV, NSL]), ALU.is_equal)\
               .then_inc(sig["oh_column"], 1)

        def slots():
            reached = r_inc.rearrange("p t e -> p (t e)")[:, 0:2 * NTT * NR].rearrange("p (t k) -> p t k", k=NR)
            do(dve.tensor_tensor(reached, r_pos.unsqueeze(2).broadcast_to([P, 2 * NTT, NR]),
                                 r_steps.unsqueeze(1).broadcast_to([P, 2 * NTT, NR]), ALU.is_ge))
            do(dve.tensor_reduce(r_ge, reached, AX.X, ALU.add))
            do(dve.tensor_scalar(r_hi, r_i.rearrange("p c t -> p (c t)"), float(NR), 8.0 * NR, ALU.mult, ALU.add))
            do(dve.tensor_tensor(r_hi, r_hi, r_ge, ALU.add))
            do(dve.scalar_tensor_tensor(out=r_lo, in0=r_ge, scalar=-float(RT), in1=r_pos, op0=ALU.mult, op1=ALU.add))
            do(dve.tensor_scalar(r_ge, r_pos, float(CAP), None, ALU.is_ge))
            last = dve.scalar_tensor_tensor(out=r_lo, in0=r_ge, scalar=1e6, in1=r_lo, op0=ALU.mult, op1=ALU.add)
            last.then_inc(sig["slots_ready"], 1)
            dve.wait_ge(sig["slots_ready"], 1)
            onehot_columns(0)
            onehot_columns(1)

        def onehot_rows(first, last):
            for n in range(first, last):
                if n >= OHV and n % OHV == OHB and n + OHB < 2 * NTT:
                    onehot_columns(n // OHV + 1)
                if n >= OHB:
                    dve.wait_ge(sig["oh_used"], n - OHB + 1)
                dve.tensor_scalar(r_row[:, n % OHB], r_iota[:, 0:RT], r_lo[:, n:n + 1], None, ALU.is_equal)\
                   .then_inc(sig["oh_row"], 1)

        def place(k, part):
            onehot_rows(*placed(k, part))

        def table():
            dve.wait_ge(sig["oh_used"], 2 * NTT)
            tk = r_val[0][:, 0, 0]
            do(dve.tensor_copy(tabw[0:RT, :], bank[5][0:RT, NSL:2 * NSL]))
            do(dve.tensor_scalar(tk[0:RT], bank[5][0:RT, 0:NSL], -1.0, None, ALU.add))
            do(dve.tensor_scalar(tabg[0:RT, :], tk[0:RT], 0.0, None, ALU.max))
            do(dve.tensor_scalar(r_val[0][0:RT, 0, 1], tk[0:RT], 0.0, 2.0 * T, ALU.is_lt, ALU.mult))
            dve.tensor_tensor(tabs[0:RT, :], tk[0:RT], r_val[0][0:RT, 0, 1], ALU.add).then_inc(sig["tab_done"], 1)
            dve.wait_ge(sig["tab_done"], 1)
            dve.tensor_copy(gidx[0:RT, :], tabg[0:RT, 0:NR]).then_inc(sig["gather_idx"], 1)

        def xe_lo(e, g):
            k, half = g % KD, g // KD
            cols = slice(half * HALF, (half + 1) * HALF)
            ps = bank[XE_BANK[g] if e.at(0) else 7]
            dve.wait_ge(sig["xe_lo"], e.n * 4 + g)
            dve.wait_ge(sig["xe_hi"], e.n * 4 + g + 1)
            dve.tensor_scalar(hf[:, 0:HALF], ps[:, 0:HALF], lng[:, k:k + 1], lnb[:, k:k + 1], ALU.mult, ALU.add)\
               .then_inc(sig["xe_f"], 1)
            dve.wait_ge(sig["xe_f"], e.n * 4 + g + 1)
            dve.tensor_tensor(xe[e.c][:, 1, k, cols], hf[:, 0:HALF], xe[e.c][:, 0, k, cols].bitcast(F32), ALU.subtract)\
               .then_inc(sig["xe_lo"], 1)

        def first_tokens():
            for g in range(4):
                xe_lo(Turn(0, 0), g)

        token_blocks(dve, {"project_keys": project_keys, "keys_lo": keys_lo, "project_values": project_values, "norm": norm, "scores": scores, "transpose_x": transpose_x, "project": project,
                           "queries": queries, "norm2": norm2, "transpose_z": transpose_z, "logits_T": logits_T,
                           "maxima": maxima, "up": up, "last_hidden": last_hidden, "shared_out": shared_out,
                           "choose": choose, "count": count,
                           "slots": slots, "place": place, "table": table, "first_tokens": first_tokens})

        def index_now(e):
            dve.tensor_copy(sidx[e.c][0:RT, :], tabs[0:RT, bass.ds(e.n * NR, NR)]).then_inc(sig["sidx_ready"], 1)
            dve.tensor_copy(gw[e.c][0:RT, :], tabw[0:RT, bass.ds(e.n * NR, NR)]).then_inc(sig["gw_ready"], 1)

        def split_piece(e, n):
            m, j = n // 4, n % 4
            buf, _ = matrix(e, m)
            dve.wait_ge(sig["wsplit_hi"], e.n * NPIECE + 4 * NSTEP0 + n + 1)
            w = W1_ if e.c == 0 else W0
            cols = slice(j * PIECE, (j + 1) * PIECE)
            dve.tensor_tensor(w[:, 1, m, cols], stage[buf][:, cols], w[:, 0, m, cols].bitcast(F32), ALU.subtract)\
               .then_inc(sig["wsplit_lo"], 1)


        def y_out(e, half):
            if half == 0:
                dve.wait_ge(sig["gw_ready"], e.n + 1)
                dve.wait_ge(sig["ye_free"], e.n + 1)
            for t in range(NR // 2):
                dve.wait_ge(sig["acc_ready"], T // P + (e.n * 2 + half) * (NR // 2) + t + 1)
                r = half * (NR // 2) + t
                dve.tensor_scalar(ye[0:RT, r, :], bank[4 + t][0:RT, 0:D], gw[e.c][0:RT, r:r + 1], None, ALU.mult)\
                   .then_inc(sig["acc_done"], 1)

        def expert(e):
            base = NB * NF + e.n * 2 * NF
            dve.wait_ge(sig["acc_done"], T // P + e.n * NR)
            index_now(e)
            if not e.at(E - 1):
                dve.wait_ge(sig["gathered"], (e.n + 1) * NR * 16)
                dve.tensor_copy(gidx[0:RT, :], tabg[0:RT, bass.ds((e.n + 1) * NR, NR)]).then_inc(sig["gather_idx"], 1)
            for n in range(2 * NF + 1):
                if n >= 1:
                    dve.wait_ge(sig["gh_ready"], base + n)
                    dve.tensor_tensor(gT[:, 1, (n - 1) % RING, 0:HALF], gf[:, (n - 1) % 2, 0:HALF],
                                      gT[:, 0, (n - 1) % RING, 0:HALF].bitcast(F32), ALU.subtract)\
                       .then_inc(sig["gl_ready"], 1)
                if n < 2 * NF:
                    dve.wait_ge(sig["b_ready"], base + n + 1)
                    dve.wait_ge(sig["sil_done"], base + n + 1)
                    dve.wait_ge(sig["gl_ready"], base + max(n - 1, 0))
                    dve.tensor_tensor(gf[:, n % 2, 0:HALF], bank[2 * (n % 2) + 1][:, 0:HALF], sil[n % 2][:, 0:HALF],
                                      ALU.mult).then_inc(sig["gmul_done"], 1)
                if not e.at(E - 1) and n < NPIECE:
                    split_piece(e.next(), n)
                if not e.at(E - 1) and n in XT_AT:
                    xe_lo(e.next(), XT_AT.index(n))
                if n == NF + 1:
                    y_out(e, 0)
            y_out(e, 1)

        with_experts(dve, expert)

    @block.tensor
    def _(pe):
        def three(o, lhs, rhs, first, last):
            pe.matmul(o, lhs[0], rhs[0], start=first, stop=False)
            pe.matmul(o, lhs[0], rhs[1], start=False, stop=False)
            return pe.matmul(o, lhs[1], rhs[0], start=False, stop=last)

        def project_keys():
            pe.wait_ge(sig["ctx_lo"], 1)
            pe.wait_ge(sig["wsplit_lo"], 1)
            for m in range(KD):
                for k in range(KD):
                    last = three(bank[m][:, 0:B * SK], [wat[:, j, 1, k, m * P:(m + 1) * P] for j in range(2)],
                                 [ctx_s[:, j, k] for j in range(2)], k == 0, k == KD - 1)
                last.then_inc(sig["kps_ready"], 1)

        def project_values():
            pe.wait_ge(sig["wsplit_lo"], NSTEP0 - 1)
            for b in range(B):
                if b >= 2:
                    pe.wait_ge(sig["v_ready"], b - 1)
                for k in range(KD):
                    last = three(bank[2 + b % 2][0:SK, 0:D], [ctx_s[:, j, k, b * SK:(b + 1) * SK] for j in range(2)],
                                 [wat[:, j, 2, k] for j in range(2)], k == 0, k == KD - 1)
                last.then_inc(sig["vps_ready"], 1)

        def transpose_x(b):
            if b.at(0):
                pe.wait_ge(sig["ident_ready"], 1)
            if b.at(2):
                pe.wait_ge(sig["lg_done"], 1)
            for k in range(KD):
                for t in range(TT):
                    if k == 0:
                        pe.wait_ge(sig["xn_ready"], b.n * TT + t + 1)
                    mm = pe.transpose(bank[6 + k][:, t * P:(t + 1) * P], xn[:, t, k * P:(k + 1) * P], ident[:, :])
                mm.then_inc(sig["xT_ready"], 1)

        def queries(b):
            pe.wait_ge(sig["xl_ready"], (b.n + 1) * KD)
            if b.at(0):
                pe.wait_ge(sig["wsplit_lo"], 2)
            elif b.at(1):
                pe.wait_ge(sig["m_done"], TT)
            else:
                pe.wait_ge(sig["x1_ready"], b.n * TT - 1)
            for m in range(KD):
                for k in range(KD):
                    mm = three(bank[4 + m][:, :], [wat[:, j, 0, k, m * P:(m + 1) * P] for j in range(2)],
                               [xT[:, j, k] for j in range(2)], k == 0, k == KD - 1)
                mm.then_inc(sig["q_ready"], 1)

        def maxima(b, t):
            if b.at(0):
                if t == 0:
                    pe.wait_ge(sig["v_ready"], B)
                    pe.wait_ge(sig["k_lo"], KD)
                    pe.wait_ge(sig["ql_ready"], KD)
                    pe.wait_ge(sig["kbd_loaded"], 128)
                elif t >= 2:
                    pe.wait_ge(sig["m_done"], t - 1)
            elif b.at(1):
                pe.wait_ge(sig["m_done"], TT + max(t - 1, 0))
                if t == 0:
                    pe.wait_ge(sig["ql_ready"], 2 * KD)
            else:
                pe.wait_ge(sig["m_done"], b.n * TT + t)
                if t == 0:
                    pe.wait_ge(sig["x1_ready"], b.n * TT)
                    pe.wait_ge(sig["ql_ready"], (b.n + 1) * KD)
                    if b.c == 0:
                        pe.wait_ge(sig["kbd_loaded"], (b.i + 1) * 128)
                if t == 1:
                    pe.wait_ge(sig["lg_done"], b.n)
            for j, (h0, h1) in enumerate(MAX_HEADS):
                for k in range(KD):
                    g0, g1 = max(h0, 8 * k), min(h1, 8 * k + 8)
                    if g0 < g1:
                        mm = pe.matmul(bank[max_banks(b, t)[j]][:, (g0 - h0) * SK:(g1 - h0) * SK], q_of(b)[:, 0, k, t * P:(t + 1) * P],
                                       kbd[:, k, g0 - 8 * k:g1 - 8 * k, :], start=True, stop=True)
            mm.then_inc(sig["m_ready"], 1)

        def maxima_T(b):
            pe.wait_ge(sig["m_done"], (b.n + 1) * TT)
            for t in range(TT):
                mm = pe.transpose(bank[maxT_bank(b)][0:H, t * P:(t + 1) * P], mx[:, t], ident[:, :])
            mm.then_inc(sig["mT_ready"], 1)

        def pv(b, p):
            if p == 0:
                if b.at(0):
                    pe.wait_ge(sig["ones_ready"], 1)
                    pe.wait_ge(sig["ql_ready"], 2 * KD)
                pe.wait_ge(sig["vst_ready"], (b.i + 1) * 8)
            if p % 2 == 0 and p >= 4:
                pe.wait_ge(sig["attn_done"], b.n * NG + p // 2 - 1)
            pe.wait_ge(sig["exp_done"], b.n * NPAIR + p + 1)
            for w in range(2):
                h = 2 * p + w
                g, j = h // 4, h % 4
                mm = pe.matmul(bank[4 + g % 2][:, :], vst[0:SK, g // 2, g % 2, j, :], prob[p % 2][0:SK, w],
                               start=(j == 0), stop=(j == 3))
            mm.then_inc(sig["pv_done"], 1)

        def pair_scores(b, p):
            for w in range(2):
                mm = pe.matmul(bank[2 * (p % 2) + w][0:SK, :], kst[0:112, p, w, :], qst[0:112, p, :], start=True, stop=True)
            mm.then_inc(sig["scores_ready"], 1)

        def first_scores(b):
            pe.wait_ge(sig["qst_loaded"], (b.n + 1) * 16 * NQST)
            if b.c == 0:
                pe.wait_ge(sig["kst_loaded"], (b.i + 1) * 96)
            if b.at(0) or b.at(1):
                pe.wait_ge(sig["m_done"], (b.n + 1) * TT)
                pe.wait_ge(sig["x1_ready"], b.n * TT)
            else:
                pe.wait_ge(sig["gmul_done"], (b.n - 1) * NF)
            for p in range(2):
                pair_scores(b, p)

        def scores(b, half):
            if half == 0:
                pv(b, 0)
                pe.wait_ge(sig["qst_rest_loaded"], (b.n + 1) * 16)
            for p in range(2 + 2 * half, 4 + 4 * half):
                pe.wait_ge(sig["exp_done"], b.n * NPAIR + p - 1)
                pair_scores(b, p)
                pv(b, p - 1)
            if half == 1:
                pv(b, NPAIR - 1)

        def project(b):
            pe.wait_ge(sig["al_ready"], (b.n + 1) * KD)
            for t in range(TT):
                banks = 2 if b.at(0) else 3
                if t >= banks:
                    pe.wait_ge(sig["x1_ready"], b.n * TT + t - banks + 1)
                for k in range(KD):
                    mm = three(bank[project_bank(b, t)][:, 0:D], [q_of(b)[:, j, k, t * P:(t + 1) * P] for j in range(2)],
                               [wat[:, j, 3, k] for j in range(2)], k == 0, k == KD - 1)
                mm.then_inc(sig["oproj_ready"], 1)

        def transpose_z(b):
            if b.at(0):
                pe.wait_ge(sig["m_done"], 2 * TT)
            elif not b.at(NB - 1):
                pe.wait_ge(sig["m_done"], (b.n + 1) * TT + 1)
            for k in range(KD):
                for t in range(TT):
                    if k == 0:
                        pe.wait_ge(sig["z_ready"], b.n * TT + t + 1)
                    mm = pe.transpose(bank[z_bank(b) + k][:, t * P:(t + 1) * P], zb[:, t, k * P:(k + 1) * P], ident[:, :])
                mm.then_inc(sig["zT_ready"], 1)

        def logits(b):
            if b.at(0):
                pe.wait_ge(sig["wr_ready"], 1)
            pe.wait_ge(sig["hl_ready"], (b.n + 1) * KD)
            for k in range(KD):
                for j in range(2):
                    mm = pe.matmul(bank[6 if b.at(0) else 5][0:2 * E, :], wrs[:, k, :], hTs[b.c][:, j, k], start=(k + j == 0),
                                   stop=(k + j == 2))
            mm.then_inc(sig["lg_ready"], 1)

        def logits_T(b):
            pe.wait_ge(sig["lgs_ready"], b.n + 1)
            apart(pe)
            for t in range(TT):
                mm = pe.transpose(bank[7 if b.at(0) else 3][:, 16 * t:16 * t + 2 * E], lgs[:, t * P:(t + 1) * P], ident[0:2 * E, 0:2 * E])
            mm.then_inc(sig["lgT_ready"], 1)

        def up(b, f):
            if b.at(0) and f == 0:
                pe.wait_ge(sig["wsplit_lo"], 4 * NSTEP0)
            for w, ready in ((0, sig["a_ready"]), (1, sig["b_ready"])):
                if w == 0 and f >= 2:
                    pe.wait_ge(sig["gmul_done"], b.n * NF + f - 1)
                if w == 1 and f >= 1:
                    pe.wait_ge(sig["sil_done"], b.n * NF + f)
                for k in range(KD):
                    mm = three(bank[(2 * f + w) % 3][:, :],
                               [W0[:, j, w, k * FF + f * P:k * FF + (f + 1) * P] for j in range(2)],
                               [hTs[b.c][:, j, k] for j in range(2)], k == 0, k == KD - 1)
                mm.then_inc(ready, 1)

        def down(b, f):
            pe.wait_ge(sig["gl_ready"], b.n * NF + f + 1)
            for t in range(TT):
                o = bank[6 + t // 2][:, t % 2 * D:t % 2 * D + D]
                lhs = [gT[:, j, f % RING, t * P:(t + 1) * P] for j in range(2)]
                rhs = [W0[:, j, 2, f * D:(f + 1) * D] for j in range(2)]
                pe.matmul(o, lhs[0], rhs[0], start=(f == 0 and t % 2 == 0), stop=False, skip_group_check=True)
                pe.matmul(o, lhs[0], rhs[1], start=False, stop=False, skip_group_check=True)
                mm = pe.matmul(o, lhs[1], rhs[0], start=False, stop=(f == NF - 1), skip_group_check=True)
                if f == NF - 1:
                    mm.then_inc(sig["acc_ready"], 1)

        def count():
            pe.wait_ge(sig["r_onehots"], 1)
            oh = r_oh.rearrange("p c t e -> p (c t e)")
            pe.matmul(bank[3][:, 0:2 * NTT * E], lower[:, :], oh, start=True, stop=True).then_inc(sig["r_counts"], 1)
            pe.matmul(bank[4][:, 0:2 * NTT * E], mones[:, :], oh, start=True, stop=True).then_inc(sig["r_counts"], 1)

        def place(k, part):
            for n in range(*placed(k, part)):
                pe.wait_ge(sig["oh_row"], n + 1)
                pe.wait_ge(sig["oh_val"], 2 * (n // OHV + 1))
                mm = pe.matmul(bank[5][0:RT, 0:2 * NSL], r_row[:, n % OHB],
                               r_val[n // OHV % 2][:, n % OHV].rearrange("p a b -> p (a b)"),
                               start=(n == 0), stop=(n == 2 * NTT - 1))
                mm.then_inc(sig["oh_used"], 1)

        def xpose(e, g):
            k, half = g % KD, g // KD
            pe.wait_ge(sig["gathered"], (e.n + 1) * NR * 16)
            if not e.at(0):
                pe.wait_ge(sig["xe_lo"], e.n * 4 + g)
            ps = bank[XE_BANK[g] if e.at(0) else 7]
            for t in range(NR // 2):
                mm = pe.transpose(ps[:, t * RT:(t + 1) * RT], xg[0:RT, half * (NR // 2) + t, k * P:(k + 1) * P],
                                  ident[0:RT, 0:RT])
            mm.then_inc(sig["xeT_ready"], 1)

        def first_tokens():
            pe.wait_ge(sig["gmul_done"], NB * NF - 1)
            for g in range(4):
                xpose(Turn(0, 0), g)

        token_blocks(pe, {"project_keys": project_keys, "project_values": project_values, "transpose_x": transpose_x, "queries": queries, "maxima": maxima, "maxima_T": maxima_T,
                          "first_scores": first_scores, "scores": scores, "project": project, "transpose_z": transpose_z, "logits": logits,
                          "logits_T": logits_T, "up": up, "down": down, "count": count, "place": place,
                          "first_tokens": first_tokens})


        def expert(e):
            base = NB * NF + e.n * 2 * NF
            w = W1_ if e.c == 0 else W0

            def down(n):
                half, f = n // NF, n % NF
                pe.wait_ge(sig["gl_ready"], base + n + 1)
                if f == 0:
                    pe.wait_ge(sig["acc_done"], T // P + (e.n * 2 + half) * (NR // 2))
                for t in range(NR // 2):
                    mm = three(bank[4 + t][0:RT, 0:D], [gT[:, j, n % RING, t * RT:(t + 1) * RT] for j in range(2)],
                               [w[:, j, 2, f * D:(f + 1) * D] for j in range(2)], f == 0, f == NF - 1)
                    if f == NF - 1:
                        mm.then_inc(sig["acc_ready"], 1)

            pe.wait_ge(sig["wsplit_lo"], e.n * NPIECE + 4 * NSTEP0 + NPIECE)
            pe.wait_ge(sig["xe_lo"], e.n * 4 + 2)
            pe.wait_ge(sig["gmul_done"], base)
            pe.wait_ge(sig["gmul_done"], NB * NF)
            for n in range(2 * NF):
                half, f = n // NF, n % NF
                if n == 2:
                    pe.wait_ge(sig["xe_lo"], e.n * 4 + 4)
                if n >= 2:
                    pe.wait_ge(sig["gmul_done"], base + n - 1)
                for m, ready in ((0, sig["a_ready"]), (1, sig["b_ready"])):
                    for k in range(KD):
                        mm = three(bank[2 * (n % 2) + m][:, 0:HALF],
                                   [w[:, j, m, k * FF + f * P:k * FF + (f + 1) * P] for j in range(2)],
                                   [xe[e.c][:, j, k, half * HALF:(half + 1) * HALF] for j in range(2)],
                                   k == 0, k == KD - 1)
                    mm.then_inc(ready, 1)
                if not e.at(E - 1) and n in XT_AT:
                    xpose(e.next(), XT_AT.index(n))
                if n >= 2:
                    down(n - 2)
            down(2 * NF - 2)
            down(2 * NF - 1)

        with_experts(pe, expert)

    ctx.close()


INS = {"x": "x", "ctxT": "ctx_1024", "g_xattn": "g_xattn", "g_ffn": "g_ffn",
       "WqT": "L0_xattn_W_q", "WkT": "L0_xattn_W_k", "WvT": "L0_xattn_W_v", "WoT": "L0_xattn_W_o"}
SAME = ["L0_xattn_b_q", "L0_xattn_b_k", "L0_xattn_b_v", "L0_xattn_b_o", "L0_ffn_ln_g", "L0_ffn_ln_b", "L0_ffn_Wr",
        "L0_ffn_W1", "L0_ffn_W3", "L0_ffn_W2", "L0_ffn_W1s", "L0_ffn_W3s", "L0_ffn_W2s"]


def kernel(**inputs):
    import concourse.bacc as bacc
    import numpy as np
    from concourse.bass_utils import run_bass_kernel_spmd

    nc = bacc.Bacc("TRN2", target_bir_lowering=False, num_devices=1)
    arrays, aps = {}, {}
    for name, src in [*INS.items(), *((n, n) for n in SAME)]:
        v = np.asarray(inputs[src])
        if name.endswith("T"):
            v = np.swapaxes(v, -1, -2)
        v = np.ascontiguousarray(v)
        arrays[f"in_{name}"] = v
        aps[name] = nc.dram_tensor(f"in_{name}", v.shape, mybir.dt.from_np(v.dtype), kind="ExternalInput").ap()
    out = nc.dram_tensor("out_0", (B, S, D), F32, kind="ExternalOutput").ap()
    build(nc, aps, out)
    r = run_bass_kernel_spmd(nc, [arrays], core_ids=[0])
    return r.results[0]["out_0"]
```
